# Optimizing a Trainium2 kernel written in Bass

```python
import numpy as np
import jax
import jax.numpy as jnp

def _softmax(x, axis=-1):
    return jax.nn.softmax(x, axis=axis)

def _gelu(x):
    return jax.nn.gelu(x, approximate=True)

def _silu(x):
    return jax.nn.silu(x)

def _sigmoid(x):
    return jax.nn.sigmoid(x)

def _layernorm(x, axis=-1, eps=1e-05):
    m = jnp.mean(x, axis=axis, keepdims=True)
    v = jnp.var(x, axis=axis, keepdims=True)
    return (x - m) / jnp.sqrt(v + eps)

def _scatter_add(tgt, idx, src, axis=0):
    return tgt.at[idx].add(src)

def _segment_sum(src, seg, n):
    return jax.ops.segment_sum(src, seg, n)
kernel_name = 'mk_xattn_ffn_d2_seqx_r8_bfabb5'

def setup_inputs(seed: int=0):
    np.random.seed(seed)
    _w = jnp.asarray

    def _rec_inputs():
        import jax
        import jax.numpy as jnp
        _rk = jax.random.key(seed)
        x = 7.22e-05 + 1 * jax.random.normal(jax.random.fold_in(_rk, 1), (4, 256, 128), jnp.float32)
        _lenS = 256 - jax.random.randint(jax.random.fold_in(_rk, 7), (4,), 0, max(1, 256 // 4) + 1, jnp.int32)
        _lenS2 = 256 - jax.random.randint(jax.random.fold_in(_rk, 8), (4,), 0, max(1, 256 // 4) + 1, jnp.int32)
        _ctx_1024P = jax.random.normal(jax.random.fold_in(_rk, 11), (4, 16, 128), jnp.float32)
        _ctx_1024c = jax.random.dirichlet(jax.random.fold_in(_rk, 511), 0.3 * jnp.ones((16,), jnp.float32), (4, 256))
        _ctx_1024t = jnp.einsum('bsk,bkd->bsd', _ctx_1024c, _ctx_1024P)
        _ctx_1024t = _ctx_1024t * jax.lax.rsqrt(jnp.mean(jnp.square(_ctx_1024t)) + 1e-12) * 0.953939
        ctx_1024 = 4.13588e-05 + 0.999923 * (_ctx_1024t + 0.3 * jax.random.normal(jax.random.fold_in(_rk, 611), (4, 256, 128), jnp.float32))
        _validS = jnp.arange(256)[None, :] < _lenS[:, None]
        _validS2 = jnp.arange(256)[None, :] < _lenS2[:, None]
        _causal = jnp.tril(jnp.ones((256, 256), dtype=bool))
        mask_1x1xSxS2_ik0 = jnp.where(jnp.broadcast_to(_validS2[0:1, None, None, :], (1, 1, 256, 256)), 0, 1).astype(jnp.int32)
        mask_BxS2_bk0 = jnp.logical_not(jnp.broadcast_to(_validS2[:, :], (4, 256)))
        return (x, ctx_1024, mask_1x1xSxS2_ik0, mask_BxS2_bk0)
    x, ctx_1024, mask_1x1xSxS2_ik0, mask_BxS2_bk0 = _rec_inputs()

    def _L0_xattn_setup():
        import jax, jax.numpy as jnp
        import numpy as np
        import math
        B, S, D, H = (4, 256, 128, 16)
        DK = D // H

        def _rope_tables(seq_len, dim, dtype=jnp.float32):
            inv_freq = 1.0 / 10000.0 ** (jnp.arange(0, dim, 2, dtype=jnp.float32) / dim)
            t = jnp.arange(seq_len, dtype=jnp.float32)
            freqs = jnp.einsum('i,j->ij', t, inv_freq)
            emb = jnp.concatenate([freqs, freqs], axis=-1)
            return (jnp.cos(emb).astype(dtype)[None, None], jnp.sin(emb).astype(dtype)[None, None])

        def _apply_rope(x, cos, sin):
            x_rot = jnp.concatenate([-x[..., 1::2], x[..., ::2]], axis=-1)
            return x * cos + x_rot * sin
        key = jax.random.key(seed)
        ks = jax.random.split(key, 12)
        scale = 1.0 / math.sqrt(D)
        inp = {'query': jax.random.normal(ks[0], (B, S, D), jnp.float32), 'key': jax.random.normal(ks[1], (B, S, D), jnp.float32), 'value': jax.random.normal(ks[2], (B, S, D), jnp.float32), 'mask': jnp.tril(jnp.ones((S, S), jnp.int32))[None, None], 'w_q': jax.random.normal(ks[3], (D, D), jnp.float32) * scale, 'b_q': jnp.zeros((D,), jnp.float32), 'w_k': jax.random.normal(ks[4], (D, D), jnp.float32) * scale, 'b_k': jnp.zeros((D,), jnp.float32), 'w_v': jax.random.normal(ks[5], (D, D), jnp.float32) * scale, 'b_v': jnp.zeros((D,), jnp.float32), 'w_o': jax.random.normal(ks[6], (D, D), jnp.float32) * scale, 'b_o': jnp.zeros((D,), jnp.float32)}
        return inp
    _L0_xattn_all = _L0_xattn_setup()
    _L0_xattn_in = {k: v for k, v in _L0_xattn_all.items() if k in ('w_q', 'b_q', 'w_k', 'b_k', 'w_v', 'b_v', 'w_o', 'b_o')}
    del _L0_xattn_all

    def _L0_ffn_setup():
        import jax, jax.numpy as jnp
        import numpy as np
        B, S, H = (2, 256, 128)
        I = 64
        E_R, E_Z = (32, 8)
        E_T = E_R + E_Z
        K = 6
        SCALE = 2.5
        W_INIT = 0.02
        key = jax.random.key(seed)
        k0, k1, k2, k3 = jax.random.split(key, 4)
        return {'hidden_states': jax.random.normal(k0, (B, S, H), jnp.float32), 'classifier_weight': jax.random.normal(k1, (E_T, H), jnp.float32) * W_INIT, 'e_score_correction_bias': jnp.zeros((E_T,), jnp.float32), 'gate_up_proj': jax.random.normal(k2, (E_T, 2 * I, H), jnp.float32) * W_INIT, 'down_proj': jax.random.normal(k3, (E_R, H, I), jnp.float32) * W_INIT}
    _L0_ffn_all = _L0_ffn_setup()
    _L0_ffn_in = {k: v for k, v in _L0_ffn_all.items() if k in ('classifier_weight', 'e_score_correction_bias', 'gate_up_proj', 'down_proj')}
    del _L0_ffn_all

    def _L1_xattn_setup():
        import jax, jax.numpy as jnp
        import numpy as np
        D_MODEL = 128
        N_HEADS = 1
        HEAD_DIM = D_MODEL // N_HEADS
        N, LEN_Q, LEN_IN = (8, 128, 512)
        key = jax.random.key(seed)
        ks = jax.random.split(key, 7)
        s = 1.0 / np.sqrt(D_MODEL)
        return {'query': jax.random.normal(ks[0], (N, LEN_Q, D_MODEL), dtype=jnp.float32), 'input_flatten': jax.random.normal(ks[1], (N, LEN_IN, D_MODEL), dtype=jnp.float32), 'input_padding_mask': jax.random.randint(ks[2], (N, LEN_IN), 0, 2).astype(bool), 'Wq': jax.random.normal(ks[3], (D_MODEL, D_MODEL), dtype=jnp.float32) * s, 'bq': jnp.zeros((D_MODEL,), dtype=jnp.float32), 'Wk': jax.random.normal(ks[4], (D_MODEL, D_MODEL), dtype=jnp.float32) * s, 'bk': jnp.zeros((D_MODEL,), dtype=jnp.float32), 'Wo': jax.random.normal(ks[5], (D_MODEL, D_MODEL), dtype=jnp.float32) * s, 'bo': jnp.zeros((D_MODEL,), dtype=jnp.float32)}
    _L1_xattn_all = _L1_xattn_setup()
    _L1_xattn_in = {k: v for k, v in _L1_xattn_all.items() if k in ('Wq', 'bq', 'Wk', 'bk', 'Wo', 'bo')}
    del _L1_xattn_all

    def _L1_ffn_setup():
        import jax, jax.numpy as jnp
        import numpy as np
        EPS = 1e-06
        N_EXPERTS = 8

        def _rms_norm(x, scale, eps=EPS):
            mean_sq = jnp.mean(x.astype(jnp.float32) ** 2, axis=-1, keepdims=True)
            s = scale.astype(jnp.float32) * jax.lax.rsqrt(mean_sq + eps)
            return x * s.astype(x.dtype)

        def _dist2(x, y):
            nx = jnp.sum(x ** 2, axis=-1)[..., :, None]
            ny = jnp.sum(y ** 2, axis=-1)[..., None, :]
            return nx + ny - 2.0 * (x @ y.T)
        key = jax.random.key(seed)
        ks = jax.random.split(key, 5)
        dim, hidden, E = (128, 256, N_EXPERTS)
        x = jax.random.normal(ks[0], (4, 256, dim), dtype=jnp.float32)
        scale = jnp.ones((dim,), dtype=jnp.float32)
        centroids = jax.random.normal(ks[1], (E, dim), dtype=jnp.float32)
        up_w = jax.random.normal(ks[2], (E, dim, hidden * 2), dtype=jnp.float32) * dim ** (-0.5)
        down_w = jax.random.normal(ks[3], (E, hidden, dim), dtype=jnp.float32) * hidden ** (-0.5)
        return {'x': x, 'scale': scale, 'centroids': centroids, 'up_w': up_w, 'down_w': down_w}
    _L1_ffn_all = _L1_ffn_setup()
    _L1_ffn_in = {k: v for k, v in _L1_ffn_all.items() if k in ('scale', 'centroids', 'up_w', 'down_w')}
    del _L1_ffn_all
    return {'x': x, 'ctx_1024': ctx_1024, 'mask_1x1xSxS2_ik0': mask_1x1xSxS2_ik0, 'mask_BxS2_bk0': mask_BxS2_bk0, 'L0_xattn_w_q': _L0_xattn_in['w_q'], 'L0_xattn_b_q': _L0_xattn_in['b_q'], 'L0_xattn_w_k': _L0_xattn_in['w_k'], 'L0_xattn_b_k': _L0_xattn_in['b_k'], 'L0_xattn_w_v': _L0_xattn_in['w_v'], 'L0_xattn_b_v': _L0_xattn_in['b_v'], 'L0_xattn_w_o': _L0_xattn_in['w_o'], 'L0_xattn_b_o': _L0_xattn_in['b_o'], 'L0_ffn_classifier_weight': _L0_ffn_in['classifier_weight'], 'L0_ffn_e_score_correction_bias': _L0_ffn_in['e_score_correction_bias'], 'L0_ffn_gate_up_proj': _L0_ffn_in['gate_up_proj'], 'L0_ffn_down_proj': _L0_ffn_in['down_proj'], 'L1_xattn_Wq': _L1_xattn_in['Wq'], 'L1_xattn_bq': _L1_xattn_in['bq'], 'L1_xattn_Wk': _L1_xattn_in['Wk'], 'L1_xattn_bk': _L1_xattn_in['bk'], 'L1_xattn_Wo': _L1_xattn_in['Wo'], 'L1_xattn_bo': _L1_xattn_in['bo'], 'L1_ffn_scale': _L1_ffn_in['scale'], 'L1_ffn_centroids': _L1_ffn_in['centroids'], 'L1_ffn_up_w': _L1_ffn_in['up_w'], 'L1_ffn_down_w': _L1_ffn_in['down_w']}

def reference(x, ctx_1024, mask_1x1xSxS2_ik0, mask_BxS2_bk0, L0_xattn_w_q, L0_xattn_b_q, L0_xattn_w_k, L0_xattn_b_k, L0_xattn_w_v, L0_xattn_b_v, L0_xattn_w_o, L0_xattn_b_o, L0_ffn_classifier_weight, L0_ffn_e_score_correction_bias, L0_ffn_gate_up_proj, L0_ffn_down_proj, L1_xattn_Wq, L1_xattn_bq, L1_xattn_Wk, L1_xattn_bk, L1_xattn_Wo, L1_xattn_bo, L1_ffn_scale, L1_ffn_centroids, L1_ffn_up_w, L1_ffn_down_w):
    import jax
    import jax.numpy as jnp

    def _L0_xattn_ref(query, key, value, mask, w_q, b_q, w_k, b_k, w_v, b_v, w_o, b_o):
        import jax, jax.numpy as jnp
        import numpy as np
        import math
        B, S, D, H = (4, 256, 128, 16)
        DK = D // H

        def _rope_tables(seq_len, dim, dtype=jnp.float32):
            inv_freq = 1.0 / 10000.0 ** (jnp.arange(0, dim, 2, dtype=jnp.float32) / dim)
            t = jnp.arange(seq_len, dtype=jnp.float32)
            freqs = jnp.einsum('i,j->ij', t, inv_freq)
            emb = jnp.concatenate([freqs, freqs], axis=-1)
            return (jnp.cos(emb).astype(dtype)[None, None], jnp.sin(emb).astype(dtype)[None, None])

        def _apply_rope(x, cos, sin):
            x_rot = jnp.concatenate([-x[..., 1::2], x[..., ::2]], axis=-1)
            return x * cos + x_rot * sin
        b, s, _ = query.shape

        def proj(x, w, bias):
            return (x @ w.T + bias).reshape(b, -1, H, DK).transpose(0, 2, 1, 3)
        Q = proj(query, w_q, b_q)
        K = proj(key, w_k, b_k)
        V = proj(value, w_v, b_v)
        cos, sin = _rope_tables(s, DK, Q.dtype)
        Q = _apply_rope(Q, cos, sin)
        K = _apply_rope(K, cos, sin)
        scores = jnp.einsum('bhqd,bhkd->bhqk', Q, K) / math.sqrt(DK)
        scores = jnp.where(mask == 0, jnp.asarray(-1000000000.0, scores.dtype), scores)
        attn = jax.nn.softmax(scores, axis=-1)
        ctx = jnp.einsum('bhqk,bhkd->bhqd', attn, V)
        ctx = ctx.transpose(0, 2, 1, 3).reshape(b, -1, D)
        return ctx @ w_o.T + b_o

    def _L0_ffn_ref(hidden_states, classifier_weight, e_score_correction_bias, gate_up_proj, down_proj):
        import jax, jax.numpy as jnp
        import numpy as np
        B, S, H = (2, 256, 128)
        I = 64
        E_R, E_Z = (32, 8)
        E_T = E_R + E_Z
        K = 6
        SCALE = 2.5
        W_INIT = 0.02
        orig_shape = hidden_states.shape
        x = hidden_states.reshape(-1, H).astype(jnp.float32)
        T = x.shape[0]
        logits = x @ classifier_weight.T
        scores = jax.nn.softmax(logits, axis=-1)
        _, topk_idx = jax.lax.top_k(scores + e_score_correction_bias[None, :], K)
        topk_w = jnp.take_along_axis(scores, topk_idx, axis=1) * SCALE
        w_full = jnp.zeros((T, E_T), jnp.float32).at[jnp.arange(T)[:, None], topk_idx].add(topk_w)
        zero_w = w_full[:, E_R:].sum(axis=-1, keepdims=True)
        out0 = x * zero_w
        routed_w = w_full[:, :E_R].T

        def body(out, xs):
            Wgu, Wd, we = xs
            gate, up = jnp.split(x @ Wgu.T, 2, axis=-1)
            y = jax.nn.silu(gate) * up @ Wd.T
            return (out + we[:, None] * y, None)
        out, _ = jax.lax.scan(body, out0, (gate_up_proj[:E_R], down_proj, routed_w))
        return out.reshape(orig_shape).astype(hidden_states.dtype)

    def _L1_xattn_ref(query, input_flatten, input_padding_mask, Wq, bq, Wk, bk, Wo, bo):
        import jax, jax.numpy as jnp
        import numpy as np
        D_MODEL = 128
        N_HEADS = 1
        HEAD_DIM = D_MODEL // N_HEADS
        N, LEN_Q, LEN_IN = (8, 128, 512)
        n, len_q, _ = query.shape
        len_in = input_flatten.shape[1]
        Q = (query @ Wq.T + bq).reshape(n, len_q, N_HEADS, HEAD_DIM).transpose(0, 2, 1, 3)
        K = (input_flatten @ Wk.T + bk).reshape(n, len_in, N_HEADS, HEAD_DIM).transpose(0, 2, 1, 3)
        scores = jnp.einsum('nhqd,nhkd->nhqk', Q, K)
        scores = jnp.where(input_padding_mask[:, None, None, :], -jnp.inf, scores)
        attn = jax.nn.softmax(scores, axis=-1)
        V = jnp.broadcast_to(input_flatten[:, None], (n, N_HEADS, len_in, D_MODEL))
        out = jnp.einsum('nhql,nhld->nhqd', attn, V)
        out = out.transpose(0, 2, 1, 3).reshape(n, len_q, D_MODEL)
        return out @ Wo.T + bo

    def _L1_ffn_ref(x, scale, centroids, up_w, down_w):
        import jax, jax.numpy as jnp
        import numpy as np
        EPS = 1e-06
        N_EXPERTS = 8

        def _rms_norm(x, scale, eps=EPS):
            mean_sq = jnp.mean(x.astype(jnp.float32) ** 2, axis=-1, keepdims=True)
            s = scale.astype(jnp.float32) * jax.lax.rsqrt(mean_sq + eps)
            return x * s.astype(x.dtype)

        def _dist2(x, y):
            nx = jnp.sum(x ** 2, axis=-1)[..., :, None]
            ny = jnp.sum(y ** 2, axis=-1)[..., None, :]
            return nx + ny - 2.0 * (x @ y.T)
        skip = x
        xn = _rms_norm(x, scale)
        ids = jnp.argmin(_dist2(xn, centroids), axis=-1)
        out = jnp.zeros_like(x)
        for e in range(N_EXPERTS):
            h = jnp.einsum('bsd,dh->bsh', xn, up_w[e])
            a, g = jnp.split(h, 2, axis=-1)
            y = jnp.einsum('bsh,hd->bsd', a * jax.nn.silu(g), down_w[e])
            out = jnp.where((ids == e)[..., None], y, out)
        return out + skip
    x = x + _L0_xattn_ref(_layernorm(x, axis=-1), ctx_1024, ctx_1024, mask_1x1xSxS2_ik0, L0_xattn_w_q, L0_xattn_b_q, L0_xattn_w_k, L0_xattn_b_k, L0_xattn_w_v, L0_xattn_b_v, L0_xattn_w_o, L0_xattn_b_o)
    x = x + _L0_ffn_ref(_layernorm(x, axis=-1), L0_ffn_classifier_weight, L0_ffn_e_score_correction_bias, L0_ffn_gate_up_proj, L0_ffn_down_proj)
    x = x + _L1_xattn_ref(_layernorm(x, axis=-1), ctx_1024, mask_BxS2_bk0, L1_xattn_Wq, L1_xattn_bq, L1_xattn_Wk, L1_xattn_bk, L1_xattn_Wo, L1_xattn_bo)
    x = x + _L1_ffn_ref(_layernorm(x, axis=-1), L1_ffn_scale, L1_ffn_centroids, L1_ffn_up_w, L1_ffn_down_w)
    return x

_drawn_inputs = setup_inputs


def setup_inputs(seed=0):
    import zlib

    import numpy as np

    out = dict(_drawn_inputs(seed))
    spreads = {'L0_xattn_b_q': (0.0, 0.1),
     'L0_xattn_b_k': (0.0, 0.1),
     'L0_xattn_b_v': (0.0, 0.1),
     'L0_xattn_b_o': (0.0, 0.1),
     'L0_ffn_e_score_correction_bias': (0.0, 0.1),
     'L1_xattn_bq': (0.0, 0.1),
     'L1_xattn_bk': (0.0, 0.8),
     'L1_xattn_bo': (0.0, 0.1),
     'L1_ffn_scale': (1.0, 0.2)}
    factors = {'L0_ffn_gate_up_proj': 8.0, 'L0_ffn_down_proj': 8.0}
    for name, (base, spread) in spreads.items():
        noise = np.random.default_rng([zlib.crc32(name.encode()), seed]).standard_normal(out[name].shape)
        drawn = base * np.exp(spread * noise) if base else spread * noise
        out[name] = jnp.asarray(drawn.astype(out[name].dtype))
    for name, factor in factors.items():
        out[name] = (out[name] * factor).astype(out[name].dtype)
    return out
```

```python
import math
from contextlib import ExitStack

import numpy as np

import concourse.bass as bass
from concourse import mybir

F32 = mybir.dt.float32
F32R = mybir.dt.float32r
BF16 = mybir.dt.bfloat16
I32 = mybir.dt.int32
U8 = mybir.dt.uint8
ALU = mybir.AluOpType
ACT = mybir.ActivationFunctionType
AX = mybir.AxisListType

P = 128
B, S, D = 4, 256, 128
T = B * S
TILES = T // P
QT = S // P
H0, DK = 16, 8
PAIRS = H0 // 2
QUADS = H0 // 4
VW = DK + 1
E_ROUTED, E_ZERO, TOP_K, ROUTE_SCALE = 32, 8, 6, 2.5
E_ALL = E_ROUTED + E_ZERO
E1 = 8
UNITS = 16
CHUNK = UNITS * P
GROUPS, GT = 2, 512
MASKED = -float(2 ** 30)
W_PARTS = 3
NEG = -3.0e38
TAKEN = 3.0e38
LN_EPS, RMS_EPS = 1e-5, 1e-6
LAG = 4
A_SLOTS = B * PAIRS
B_START = PAIRS + LAG
SLOTS = A_SLOTS + B_START + 2

SM = {}
_at = 0
for _name, _n in (("wq", D), ("wqr", D), ("wk", D), ("wkr", D), ("wv", D), ("wo", D), ("wq1", D), ("wk1", D),
                  ("wo1", D), ("cls", E_ALL), ("cent", E1), ("bq", 1), ("bqr", 1), ("bk", 1), ("bkr", 1),
                  ("bq1", 1), ("bk1", 1), ("scale", 1)):
    SM[_name] = (_at, _at + _n)
    _at += _n
SMALL = _at
ROW_BV, ROW_BO, ROW_BO1, ROW_EB = 0, D, 2 * D, 3 * D
ROWS = 3 * D + E_ALL


def misc_uses():
    uses = [("notfull", 0)]
    for s in range(SLOTS):
        uses += [t for t in slot_tasks(s) if t[0] in MISC_READER]
    for stage in (0, 1):
        for g in range(GROUPS):
            for u in range(UNITS):
                uses += [t for t in unit_tasks(stage, g, u) if t[0] in MISC_READER]
    uses += [("final", GROUPS - 1)]
    return uses


MISC_READER = {
    "notfull": "dve", "k1proj": "act", "xT": "act", "qproj": "dve", "kproj": "dve", "vproj": "dve",
    "maxT": "dve", "ctx0": "dve", "ctx1": "dve", "ctxT": "act", "oproj": "dve", "xT2": "dve", "logits": "dve",
    "wT": "dve", "yT": "dve", "xT3": "act", "q1": "act", "s1": "dve", "pT": "act", "pv1": "act", "oproj1": "dve",
    "xT4": "dve", "dist": "dve", "ohT": "dve", "final": "dve",
}
PREP = {"xT": 1, "qproj": 2, "kproj": 3, "vproj": 5}
TAIL = ["ctx0", "ctx1", "ctxT", "oproj", "xT2", "logits", "wT"]
SECOND = ["xT3", "k1proj", "q1", "s1", "pT", "pv1", "oproj1", "xT4", "dist", "ohT"]


def slot_tasks(s):
    tasks = []
    if s == 0:
        tasks += [(n, 0) for n in PREP]
        return tasks
    for b in range(B):
        for name, at in PREP.items():
            if b > 0 and s == PAIRS * (b - 1) + at:
                tasks.append((name, b))
        if s == PAIRS * (b + 1) + 1:
            tasks.append(("maxT", b))
        for i, name in enumerate(TAIL):
            if s == PAIRS * b + B_START + PAIRS + 2 + i:
                tasks.append((name, b))
    return tasks


def unit_tasks(stage, g, u):
    tasks = []
    if stage == 0 and g == 0:
        s = SLOTS + u
        for i, name in enumerate(TAIL):
            if s == PAIRS * (B - 1) + B_START + PAIRS + 2 + i:
                tasks.append((name, B - 1))
    if (stage, g) in ((0, 1), (1, 0)):
        done = 0 if stage == 0 else 1
        if u == 1:
            tasks.append(("yT", done))
        for k in range(2):
            i = u - 2 - 4 * k
            if 0 <= i < len(SECOND):
                tasks.append((SECOND[i], 2 * done + k))
    if stage == 1 and g == 1 and u == 1:
        tasks.append(("final", 0))
    return tasks


def misc_index(task):
    return misc_uses().index(task)


def misc_reads(task):
    uses = misc_uses()
    k = uses.index(task)
    return sum(1 for t in uses[:k + 1] if MISC_READER[t[0]] == MISC_READER[task[0]])


def build(nc, x, ctx_t, ctx_tok, mask_q, mask_k, pad, small, rows, experts, ident, rope, sel, out):
    with ExitStack() as ctx:
        def sb(name, shape, dt=F32):
            return ctx.enter_context(nc.sbuf_tensor(name, shape, dt))

        def sem(name):
            return ctx.enter_context(nc.semaphore(name))

        psum = ctx.enter_context(nc.psum_tensor("psum", [P, 8, 512], F32))
        qk_scratch = nc.dram_tensor("qk_scratch", [B, P, 2, 2, S], F32, kind="Internal").ap()

        x_in = sb("x_in", [P, TILES, D])
        acc = x_in
        xn = sb("xn", [P, 2, QT, D])
        xres = sb("xres", [P, 2, QT, D])
        stats = sb("stats", [P, 2, QT, 6])
        mv = sb("mv", [P, 2, QT, 2])
        rstd = sb("rstd", [P, 2, 2 * QT])
        half = sb("half", [P, QT])
        id32 = sb("id32", [P, P])
        id16 = sb("id16", [P, P], BF16)
        sm = sb("sm", [P, SMALL])
        rowb = sb("rowb", [P, ROWS])
        ropet = sb("ropet", [P, 4, S])
        maskb = sb("maskb", [P, 2, QT, S], BF16)
        allmasked = sb("allmasked", [P, QT])
        iddiag = sb("iddiag", [P, QT, P])
        ones = sb("ones", [P, P])
        padneg = sb("padneg", [P, B, S], BF16)
        seln = sb("seln", [P, UNITS, P], BF16)
        ctxT = sb("ctxT", [P, T])
        ctxk = sb("ctxk", [P, TILES, D])
        xnT = sb("xnT", [P, 2, S])
        early = sb("early", [P, 6144])
        probs = early[:, 0:4096].rearrange("p (n r k q) -> p n r k q", n=4, r=2, k=QT)
        rot = early[:, 4096:6144].rearrange("p (n t i q) -> p n t i q", n=2, t=2, i=2)
        qk = sb("qk", [P, 2, S])
        parts = sb("parts", [P, 2048], F32R)
        qks = parts[:, :].rearrange("p (n t l q) -> p n t l q", n=2, t=2, l=2)
        big = sb("big", [P, 6 * CHUNK], F32R)
        stacks = big[:, :].rearrange("p (t b j q) -> p t b j q", t=2, b=3, j=PAIRS)
        vaug = sb("vaug", [P, 3, QT, VW * H0 + 32 - VW])
        vheads = vaug[:, :, :, 0:VW * H0].rearrange("p b k (h c) -> p b k h c", c=VW)
        negmax = sb("negmax", [P, 2, QT, 16])
        maxrow = sb("maxrow", [16, 2, S], F32R)
        pvT = sb("pvT", [P, QUADS, S])
        maskq_i = pvT[:, :, :].bitcast(I32).rearrange("p (m t) k -> p m t k", m=2)
        rden = sb("rden", [P, 2, H0])
        ctxn = sb("ctxn", [P, 2, QT, D])
        pad8 = ctxn[:, 0, :, :].rearrange("p t d -> p (t d)").bitcast(U8)
        ctxnT = sb("ctxnT", [P, 2, S])
        rt_neg = sb("rt_neg", [P, QT])
        rt_sum = sb("rt_sum", [P, QT])
        rt_e = sb("rt_e", [P, QT, E_ALL])
        rt_s = sb("rt_s", [P, QT, E_ALL])
        rt_sel = sb("rt_sel", [P, QT, E_ALL + 8])
        rt_top = sb("rt_top", [P, QT, 8])
        rt_rep = sb("rt_rep", [P, QT, 8])
        rt_mr = sb("rt_mr", [P, QT, E_ALL + 8])
        rt_w = sb("rt_w", [P, QT, E_ALL])
        rt_ws = sb("rt_ws", [P, 2, QT, W_PARTS * E_ROUTED])
        rt_b = sb("rt_b", [P, QT, E_ROUTED], BF16)
        rt_r = sb("rt_r", [P, QT, E_ROUTED])
        rt_zw = sb("rt_zw", [P, QT])
        cls32 = xnT
        wT = sb("wT", [P, T], BF16)
        raw = sb("raw", [P, 2, CHUNK // 2])
        ws0 = sb("ws0", [P, 3, 2, CHUNK], F32R)
        ws1 = big[:, :].rearrange("p (c h n) -> p c h n", c=3, h=2)
        xs = sb("xs", [P, 2, T], F32R)
        sg = early[:, 0:1024].rearrange("p (n t) -> p n t", n=2)
        h32 = early[:, 1024:2048].rearrange("p (n t) -> p n t", n=2)
        hs = parts[:, :].rearrange("p (n l t) -> p n l t", n=2, l=2)
        yT = early[:, 2048:2560]
        k1T = sb("k1T", [P, 2, S])
        xT3 = early[:, 2560:3072].rearrange("p (n q) -> p n q", n=2)
        q1T = early[:, 3072:3584].rearrange("p (n q) -> p n q", n=2)
        sm1 = early[:, 3584:4608].rearrange("p (n t k) -> p n t k", n=2, t=QT)
        pT1 = early[:, 4608:5632].rearrange("p (n k q) -> p n k q", n=2, k=QT)
        nm1 = sb("nm1", [P, 2, QT])
        sum1 = sb("sum1", [P, 2, QT])
        ms4 = sb("ms4", [P, 2, QT])
        xsq = qk
        c2 = sb("c2", [P, 3, E1])
        d_nd = sb("d_nd", [P, QT, 16])
        d_top = sb("d_top", [P, QT, 8])
        d_rep = sb("d_rep", [P, QT, 8])
        d_mr = sb("d_mr", [P, QT, 16])
        d_oh = rt_ws

        in_x, in_xrest, in_ctx, in_small, in_const, in_mask, in_rows, in_pad, in_late = (
            sem(n) for n in ("in_x", "in_xrest", "in_ctx", "in_small", "in_const", "in_mask", "in_rows", "in_pad", "in_late"))
        in_raw = [sem(f"in_raw{i}") for i in range(12)]
        scratch_out = [sem(f"scratch_out{b}") for b in range(B)]
        stack_in = [sem(f"stack_in{b}") for b in range(B)]
        maxrow_in = [sem(f"maxrow_in{b}") for b in range(B)]
        out_done = sem("out_done")
        dve_self, pool_self, act_self = sem("dve_self"), sem("pool_self"), sem("act_self")
        misc_full, misc_dve, misc_act = sem("misc_full"), sem("misc_dve"), sem("misc_act")
        consts_ready, masks_ready, norm_stats, normed = (sem(n) for n in ("consts_ready", "masks_ready", "norm_stats", "normed"))
        rot_ready, v_ready, maxes_read, maxrow_ready, ctxn_ready, neg_ready = (
            sem(n) for n in ("rot_ready", "v_ready", "maxes_read", "maxrow_ready", "ctxn_ready", "neg_ready"))
        x2_ready, xs_ready, ws_ready, wT_ready = (sem(n) for n in ("x2_ready", "xs_ready", "ws_ready", "wT_ready"))
        hidden_ready, up_read, nm1_ready, p1_ready, oh_ready, xf_ready, xr_ready, fin_ready, x4_ready = (
            sem(n) for n in ("hidden_ready", "up_read", "nm1_ready", "p1_ready", "oh_ready", "xf_ready", "xr_ready",
                             "fin_ready", "x4_ready"))
        rstd_ready, qks_ready, pool_consts, wsplit, lo_ready, acc4_ready, rms_ready = (
            sem(n) for n in ("rstd_ready", "qks_ready", "pool_consts", "wsplit", "lo_ready", "acc4_ready", "rms_ready"))
        exps_done, pv_evicted, act_exp_rt, silu_ready, hi_ready, y_evicted, exp1_done, sq_done, xsq_done = (
            sem(n) for n in ("exps_done", "pv_evicted", "act_exp_rt", "silu_ready", "hi_ready", "y_evicted",
                             "exp1_done", "sq_done", "xsq_done"))
        scores_max, scores_exp, pv_done, gates_done, wb_done, y_done = (
            sem(n) for n in ("scores_max", "scores_exp", "pv_done", "gates_done", "wb_done", "y_done"))

        def small_w(name):
            return sm[:, SM[name][0]:SM[name][1]]

        def misc_bank(task):
            return psum[:, 6 + misc_index(task) % 2, :]

        BANK_PV = 4

        def ln_index(kind, b):
            return LN_ORDER.index((kind, b))

        block = ctx.enter_context(nc.Block())

        LN_ORDER = [(0, 0)]
        for s in range(SLOTS):
            for name, b in slot_tasks(s):
                if name == "vproj" and b + 1 < B:
                    LN_ORDER.append((0, b + 1))
                if name == "oproj":
                    LN_ORDER.append((1, b))
        for stage in (0, 1):
            for g in range(GROUPS):
                for u in range(UNITS):
                    for name, b in unit_tasks(stage, g, u):
                        if name == "oproj":
                            LN_ORDER.append((1, b))
                        if name == "yT":
                            LN_ORDER.append((2, 2 * b))
                        if name == "xT3" and b % 2 == 0:
                            LN_ORDER.append((2, b + 1))
                        if name == "oproj1":
                            LN_ORDER.append((3, b))

        @block.sync
        def _(sp):
            sp.dma_start(x_in[:, 0:QT, :], x[0:S, :].rearrange("(t p) d -> p t d", p=P)).then_inc(in_x, 16)
            sp.dma_start(sm[:, :], small).then_inc(in_small, 16)
            sp.dma_start(ctxT[:, :], ctx_t).then_inc(in_ctx, 16)
            sp.dma_start(id32[:, :], ident).then_inc(in_const, 16)
            sp.dma_start(ropet[:, :, :], rope).then_inc(in_const, 16)
            sp.dma_start(maskq_i[:, 0, :, :], mask_q).then_inc(in_mask, 16)
            sp.dma_start(maskq_i[:, 1, :, :], mask_k).then_inc(in_mask, 16)
            sp.dma_start(rowb[:, :], rows.to_broadcast([P, ROWS])).then_inc(in_rows, 16)
            sp.dma_start(x_in[:, QT:TILES, :], x[S:T, :].rearrange("(t p) d -> p t d", p=P)).then_inc(in_xrest, 16)
            sp.dma_start(pad8, pad.to_broadcast([P, T])).then_inc(in_pad, 16)
            sp.dma_start(ctxk[:, :, :], ctx_tok.rearrange("(t p) d -> p t d", p=P)).then_inc(in_late, 16)
            sp.dma_start(sg[:, :, :], sel[:, 0:1024]).then_inc(in_late, 16)
            sp.dma_start(h32[:, :, :], sel[:, 1024:2048]).then_inc(in_late, 16)

            def stack_batch(b):
                sp.wait_ge(qks_ready, b + 1)
                sp.dma_start(qk_scratch[b], qks[:, b % 2, :, :, :].bitcast(F32)).then_inc(scratch_out[b], 16)
                sp.wait_ge(scratch_out[b], 16)
                if b >= 3:
                    sp.wait_ge(scores_exp, PAIRS * (b - 2))
                src = qk_scratch[b].rearrange("(j r d) t l q -> r t l d j q", r=2, d=DK)
                for r in range(2):
                    for i in range(4):
                        for t, part in ((0, i % 2), (1, i // 2)):
                            row = 64 * r + DK * i
                            sp.dma_start(stacks[row:row + DK, t, b % 3, :, :].bitcast(F32), src[r, t, part]).then_inc(stack_in[b], 16)

            def maxrow_batch(b):
                sp.wait_ge(maxrow_ready, b + 1)
                for r in range(2):
                    sp.dma_start(stacks[64 * r + 32:64 * r + 33, 0, b % 3, :, :].bitcast(F32),
                                 maxrow[PAIRS * r:PAIRS * (r + 1), b % 2, :].bitcast(F32)).then_inc(maxrow_in[b], 16)

            for s in range(SLOTS):
                for name, b in slot_tasks(s):
                    if name == "kproj":
                        stack_batch(b)
                    if name == "maxT":
                        maxrow_batch(b)
            for g in range(GROUPS):
                sp.wait_ge(fin_ready, g + 1)
                sp.dma_start(out[GT * g:GT * (g + 1), :].rearrange("(t p) d -> p t d", p=P),
                             acc[:, 4 * g:4 * g + 4, :]).then_inc(out_done, 16)
            sp.wait_ge(out_done, 16 * GROUPS)

        @block.gpsimd
        def _(pool):
            own = [0]

            def then(ins):
                own[0] += 1
                ins.then_inc(pool_self, 1)
                pool.wait_ge(pool_self, own[0])

            nc.gpsimd.memset(vaug[:, :, :, :], 1.0)
            nc.gpsimd.memset(wT[:, :], 0.0)
            nc.gpsimd.memset(negmax[:, :, :, :], 0.0)
            nc.gpsimd.memset(ones[:, :], 1.0)
            then(nc.gpsimd.memset(half[:, :], -0.5))
            then(nc.gpsimd.memset(stacks[32:33, 1, :, :, :].bitcast(F32), 1.0))
            nc.gpsimd.memset(stacks[96:97, 1, :, :, :].bitcast(F32), 1.0).then_inc(pool_consts, 1)
            pool.wait_ge(pool_consts, 1)

            def inv_sqrt(n):
                pool.wait_ge(norm_stats, n + 1)
                then(nc.gpsimd.tensor_scalar_add(rstd[:, n % 2, 0:QT], mv[:, n % 2, :, 1], LN_EPS))
                nc.gpsimd.tensor_tensor(rstd[:, n % 2, QT:2 * QT], rstd[:, n % 2, 0:QT], half[:, :],
                                        ALU.pow).then_inc(rstd_ready, 1)

            def split_qk(b):
                pool.wait_ge(rot_ready, 2 * (b + 1))
                if b >= 2:
                    pool.wait_ge(scratch_out[b - 2], 16)
                then(nc.gpsimd.tensor_tensor(qk[:, :, :], rot[:, b % 2, :, 0, :], rot[:, b % 2, :, 1, :], ALU.add))
                then(nc.gpsimd.tensor_copy(qks[:, b % 2, :, 0, :], qk[:, :, :]))
                nc.gpsimd.tensor_tensor(qks[:, b % 2, :, 1, :], qk[:, :, :], qks[:, b % 2, :, 0, :].bitcast(F32),
                                        ALU.subtract).then_inc(qks_ready, 1)
                pool.wait_ge(qks_ready, b + 1)

            def load_raw(k):
                pool.dma_start(raw[:, k % 2, :], experts[:, k // 2, 1024 * (k % 2):1024 * (k % 2 + 1)]).then_inc(in_raw[k], 16)

            def split_weights(i):
                c, q = i // 4, i % 4
                if q % 2 == 0:
                    pool.wait_ge(in_raw[i // 2], 16)
                if i == 12:
                    pool.wait_ge(scores_exp, A_SLOTS)
                ws = (ws0 if c < 3 else ws1)[:, c % 3, :, 512 * q:512 * (q + 1)]
                src = raw[:, (i // 2) % 2, 512 * (q % 2):512 * (q % 2 + 1)]
                then(nc.gpsimd.tensor_copy(ws[:, 0, :], src))
                nc.gpsimd.tensor_tensor(ws[:, 1, :], src, ws[:, 0, :].bitcast(F32), ALU.subtract).then_inc(wsplit, 1)
                if q % 2 == 1 and i // 2 + 2 < 12:
                    pool.wait_ge(wsplit, i + 1)
                    load_raw(i // 2 + 2)

            inv_sqrt(ln_index(0, 0))
            load_raw(0)
            load_raw(1)
            wi = 0
            for s in range(SLOTS):
                for name, b in slot_tasks(s):
                    if name == "kproj":
                        split_qk(b)
                    if name == "vproj":
                        if b + 1 < B:
                            inv_sqrt(ln_index(0, b + 1))
                    if name == "oproj":
                        inv_sqrt(ln_index(1, b))
                if s >= 2 and s % 3 == 2 and wi < 12:
                    split_weights(wi)
                    wi += 1

            n_unit = 0
            for stage in (0, 1):
                for g in range(GROUPS):
                    for u in range(UNITS):
                        n = n_unit
                        for name, b in unit_tasks(stage, g, u):
                            if name == "oproj":
                                inv_sqrt(ln_index(1, b))
                            if name == "yT":
                                inv_sqrt(ln_index(2, 2 * b))
                            if name == "xT3" and b % 2 == 0:
                                inv_sqrt(ln_index(2, b + 1))
                            if name == "oproj1":
                                inv_sqrt(ln_index(3, b))
                                k = ln_index(3, b)
                                pool.wait_ge(xr_ready, b + 1)
                                nc.gpsimd.tensor_tensor(acc[:, 2 * b:2 * b + 2, :], xres[:, b % 2, :, :],
                                                        xn[:, k % 2, :, :], ALU.add).then_inc(acc4_ready, 1)
                                pool.wait_ge(sq_done, b + 1)
                                then(nc.gpsimd.tensor_scalar(ms4[:, b % 2, :], ms4[:, b % 2, :], 1.0 / D, RMS_EPS,
                                                             ALU.mult, ALU.add))
                                nc.gpsimd.tensor_tensor(ms4[:, b % 2, :], ms4[:, b % 2, :], half[:, :],
                                                        ALU.pow).then_inc(rms_ready, 1)
                        pool.wait_ge(hi_ready, n + 1)
                        nc.gpsimd.tensor_tensor(hs[:, n % 2, 1, :], h32[:, n % 2, :], hs[:, n % 2, 0, :].bitcast(F32),
                                                ALU.subtract).then_inc(lo_ready, 1)
                        if wi < 24 and stage == 0:
                            split_weights(wi)
                            wi += 1
                        n_unit += 1

        @block.scalar
        def _(act):
            act.wait_ge(in_late, 48)
            nc.scalar.copy(seln[:, 0:8, :], sg[:, :, :].rearrange("p a (b n) -> p (a b) n", n=P))
            nc.scalar.copy(seln[:, 8:16, :], h32[:, :, :].rearrange("p a (b n) -> p (a b) n", n=P)).then_inc(act_self, 1)
            self_n = [1]

            def evict(task, dst, src, bias=None):
                act.wait_ge(misc_full, misc_index(task) + 1)
                if bias is None:
                    nc.scalar.copy(dst, src).then_inc(misc_act, 1)
                else:
                    nc.scalar.activation(dst, src, ACT.Identity, bias=bias).then_inc(misc_act, 1)

            def misc_task(name, b):
                task = (name, b)
                if name not in ("logits", "s1", "xT4", "oproj1") and MISC_READER[name] != "act":
                    return
                m = misc_bank(task)
                if name == "k1proj":
                    evict(task, k1T[:, b % 2, :], m[:, 0:S], small_w("bk1"))
                elif name == "xT":
                    evict(task, xnT[:, b % 2, :], m[:, 0:S])
                elif name == "ctxT":
                    evict(task, ctxnT[:, b % 2, :], m[:, 0:S])
                elif name == "logits":
                    act.wait_ge(neg_ready, b + 1)
                    for t in range(QT):
                        last = nc.scalar.activation(rt_e[:, t, :], m[:, 64 * t:64 * t + E_ALL], ACT.Exp,
                                                    bias=rt_neg[:, t:t + 1], accum_out=rt_sum[:, t:t + 1])
                    last.then_inc(act_exp_rt, 1)
                elif name == "xT3":
                    evict(task, xT3[:, b % 2, :], m[:, 0:S])
                elif name == "q1":
                    evict(task, q1T[:, b % 2, :], m[:, 0:S], small_w("bq1"))
                elif name == "s1":
                    act.wait_ge(nm1_ready, b + 1)
                    for t in range(QT):
                        last = nc.scalar.activation(sm1[:, b % 2, t, :], sm1[:, b % 2, t, :], ACT.Exp,
                                                    bias=nm1[:, b % 2, t:t + 1], accum_out=sum1[:, b % 2, t:t + 1])
                    last.then_inc(exp1_done, 1)
                elif name == "pT":
                    evict(task, pT1[:, b % 2, :, :], m.rearrange("p (k q) -> p k q", k=QT))
                elif name == "pv1":
                    evict(task, q1T[:, b % 2, :], m[:, 0:S])
                elif name == "oproj1":
                    k = ln_index(3, b)
                    act.wait_ge(xr_ready, b + 1)
                    for t in range(QT):
                        last = nc.scalar.activation(xsq[:, b % 2, D * t:D * (t + 1)], xn[:, k % 2, t, :], ACT.Square,
                                                    accum_out=ms4[:, b % 2, t:t + 1])
                    last.then_inc(sq_done, 1)
                elif name == "xT4":
                    act.wait_ge(xf_ready, b + 1)
                    nc.scalar.activation(xsq[:, b % 2, :], cls32[:, b % 2, :], ACT.Square).then_inc(xsq_done, 1)

            for s in range(SLOTS):
                t = s - B_START
                if 0 <= t < A_SLOTS:
                    act.wait_ge(scores_exp, t + 1)
                    if t >= 4:
                        act.wait_ge(pv_done, (t - 4) // 2 + 1)
                    nc.scalar.activation(probs[:, t % 4, :, :, :],
                                         psum[:, 2:4, :].rearrange("p r (k q) -> p r k q", k=QT),
                                         ACT.Exp).then_inc(exps_done, 1)
                if t >= 5 and t % 4 == 1:
                    c = (t - 5) // 4
                    act.wait_ge(pv_done, 2 * (c + 1))
                    if c == 0:
                        act.wait_ge(masks_ready, 1)
                    elif c % 2 == 0:
                        act.wait_ge(misc_full, misc_index(("ctx1", c // 2 - 1)) + 1)
                    nc.scalar.copy(pvT[:, 2 * (c % 2):2 * (c % 2) + 2, :],
                                   psum[:, BANK_PV + c % 2, :].rearrange("p (a q) -> p a q", a=2)).then_inc(pv_evicted, 1)
                for name, b in slot_tasks(s):
                    misc_task(name, b)

            n_unit = 0
            for stage in (0, 1):
                for g in range(GROUPS):
                    for u in range(UNITS):
                        n = n_unit
                        act.wait_ge(gates_done, n + 1)
                        if n == 0:
                            act.wait_ge(act_self, 1)
                        if n >= 2:
                            act.wait_ge(up_read, n - 1)
                        nc.scalar.activation(sg[:, n % 2, :], psum[:, n % 2, :], ACT.Silu).then_inc(silu_ready, 1)
                        act.wait_ge(hidden_ready, n + 1)
                        if n >= 2:
                            act.wait_ge(y_done, n - 1)
                        nc.scalar.copy(hs[:, n % 2, 0, :], h32[:, n % 2, :]).then_inc(hi_ready, 1)
                        if n % UNITS == 0 and n > 0:
                            k = n // UNITS - 1
                            act.wait_ge(y_done, n)
                            if k >= 1:
                                act.wait_ge(misc_full, misc_index(("yT", k - 1) if k < 3 else ("final", 0)) + 1)
                            nc.scalar.copy(yT[:, :], psum[:, 5, :]).then_inc(y_evicted, 1)
                        for name, b in unit_tasks(stage, g, u):
                            misc_task(name, b)
                        n_unit += 1
            act.wait_ge(y_done, 4 * UNITS)
            act.wait_ge(misc_full, misc_index(("final", 0)) + 1)
            nc.scalar.copy(yT[:, :], psum[:, 5, :]).then_inc(y_evicted, 1)

        @block.vector
        def _(dve):
            own = [0]

            def then(ins):
                own[0] += 1
                ins.then_inc(dve_self, 1)
                dve.wait_ge(dve_self, own[0])

            def norm_begin(kind, b, src):
                n = ln_index(kind, b)
                for t in range(QT):
                    nc.vector.bn_stats(stats[:, n % 2, t, :], src[:, t, :])
                then(nc.vector.memset(rt_zw[:, 0:1], 0.0))
                for t in range(QT):
                    last = nc.vector.bn_aggr(mv[:, n % 2, t, :], stats[:, n % 2, t, :])
                last.then_inc(norm_stats, 1)

            def norm_end(kind, b, src):
                n = ln_index(kind, b)
                dve.wait_ge(rstd_ready, n + 1)
                for t in range(QT):
                    last = nc.vector.tensor_scalar(xn[:, n % 2, t, :], src[:, t, :], mv[:, n % 2, t, 0:1],
                                                   rstd[:, n % 2, QT + t:QT + t + 1], ALU.subtract, ALU.mult)
                last.then_inc(normed, 1)
                dve.wait_ge(normed, n + 1)

            dve.wait_ge(in_x, 16)
            norm_begin(0, 0, x_in[:, 0:QT, :])
            dve.wait_ge(in_const, 32)
            nc.vector.tensor_copy(id16[:, :], id32[:, :])
            dve.wait_ge(in_mask, 32)
            then(nc.vector.tensor_scalar(maskb[:, :, :, :], maskq_i[:, :, :, :], 0.0, MASKED, ALU.is_equal, ALU.mult))
            then(nc.vector.tensor_reduce(allmasked[:, :], maskb[:, 0, :, :], AX.X, ALU.max))
            then(nc.vector.tensor_scalar(allmasked[:, :], allmasked[:, :], -1.0, None, ALU.is_gt))
            for t in range(QT):
                last = nc.vector.tensor_scalar(iddiag[:, t, :], id32[:, :], allmasked[:, t:t + 1], None, ALU.mult)
            last.then_inc(masks_ready, 1)
            norm_end(0, 0, x_in[:, 0:QT, :])
            dve.wait_ge(misc_full, misc_index(("notfull", 0)) + 1)
            for t in range(2):
                last = nc.vector.tensor_tensor(ropet[:, t, :], ropet[:, t, :], misc_bank(("notfull", 0))[:, 0:S], ALU.mult)
            last.then_inc(misc_dve, 1)
            dve.wait_ge(misc_dve, 1)
            dve.wait_ge(in_small, 16)
            nc.vector.tensor_scalar(c2[:, 0, :], small_w("cent"), 2.0, None, ALU.mult)
            nc.vector.scalar_tensor_tensor(c2[:, 1, :], small_w("cent"), -1.0, small_w("cent"), ALU.mult, ALU.mult)
            nc.vector.memset(c2[:, 2, :], -1.0)
            nc.vector.memset(rt_sel[:, :, :], NEG)
            nc.vector.memset(rt_rep[:, :, :], NEG)
            nc.vector.memset(d_nd[:, :, :], NEG)
            nc.vector.memset(d_rep[:, :, :], NEG).then_inc(consts_ready, 1)
            dve.wait_ge(consts_ready, 1)
            dve.wait_ge(in_rows, 16)

            def misc_task(name, b):
                task = (name, b)
                if MISC_READER.get(name) != "dve":
                    return
                m = misc_bank(task)
                if name not in ("xT3",):
                    dve.wait_ge(misc_full, misc_index(task) + 1)
                if name in ("qproj", "kproj"):
                    t, names = (0, ("bq", "bqr")) if name == "qproj" else (1, ("bk", "bkr"))
                    if b >= 2 and t == 0:
                        dve.wait_ge(qks_ready, b - 1)
                    nc.vector.scalar_tensor_tensor(rot[:, b % 2, t, 0, :], m[:, 0:S], small_w(names[0]),
                                                   ropet[:, 2 * t, :] if t else ropet[:, 0, :], ALU.add, ALU.mult)
                    nc.vector.scalar_tensor_tensor(rot[:, b % 2, t, 1, :], m[:, S:2 * S], small_w(names[1]),
                                                   ropet[:, 2 * t + 1, :] if t else ropet[:, 1, :], ALU.add,
                                                   ALU.mult).then_inc(misc_dve, 1)
                    dve.wait_ge(misc_dve, misc_reads(task))
                    nc.vector.memset(rt_zw[:, 1:2], 0.0).then_inc(rot_ready, 1)
                elif name == "vproj":
                    dve.wait_ge(pool_consts, 1)
                    if b >= 3:
                        dve.wait_ge(pv_done, QUADS * (b - 2))
                    for k in range(QT):
                        last = nc.vector.tensor_tensor(
                            vheads[:, b % 3, k, :, 0:DK], m[:, D * k:D * (k + 1)].rearrange("p (h d) -> p h d", d=DK),
                            rowb[:, ROW_BV:ROW_BV + D].rearrange("p (h d) -> p h d", d=DK), ALU.add)
                    last.then_inc(misc_dve, 1)
                    if b + 1 < B:
                        if b == 0:
                            dve.wait_ge(in_xrest, 16)
                        src = x_in[:, QT * (b + 1):QT * (b + 2), :]
                        norm_begin(0, b + 1, src)
                        norm_end(0, b + 1, src)
                elif name == "maxT":
                    nc.vector.tensor_copy(maxrow[:, b % 2, :], m[0:16, 0:S]).then_inc(misc_dve, 1)
                    dve.wait_ge(misc_dve, misc_reads(task))
                    nc.vector.memset(rt_zw[:, 1:2], 0.0).then_inc(maxrow_ready, 1)
                elif name in ("ctx0", "ctx1"):
                    t = 0 if name == "ctx0" else 1
                    v = m.rearrange("p (h c) -> p h c", c=32)
                    then(nc.vector.reciprocal(rden[:, t, :], v[:, :, DK]))
                    nc.vector.tensor_tensor(ctxn[:, b % 2, t, :].rearrange("p (h d) -> p h d", d=DK), v[:, :, 0:DK],
                                            rden[:, t, :].unsqueeze(2).to_broadcast([P, H0, DK]),
                                            ALU.mult).then_inc(misc_dve, 1)
                elif name == "oproj":
                    then(nc.vector.tensor_tensor(x_in[:, 2 * b:2 * b + 2, :], x_in[:, 2 * b:2 * b + 2, :],
                                                 rowb[:, ROW_BO:ROW_BO + D].unsqueeze(1).to_broadcast([P, QT, D]), ALU.add))
                    nc.vector.tensor_tensor(xres[:, b % 2, :, :], x_in[:, 2 * b:2 * b + 2, :],
                                            m[:, 0:QT * D].rearrange("p (t d) -> p t d", t=QT), ALU.add).then_inc(misc_dve, 1)
                    dve.wait_ge(misc_dve, misc_reads(task))
                    norm_begin(1, b, xres[:, b % 2, :, :])
                    norm_end(1, b, xres[:, b % 2, :, :])
                elif name == "xT2":
                    cols = slice(S * b, S * (b + 1))
                    then(nc.vector.tensor_copy(cls32[:, b % 2, :], m[:, 0:S]))
                    then(nc.vector.tensor_copy(xs[:, 0, cols], m[:, 0:S]))
                    nc.vector.tensor_tensor(xs[:, 1, cols], m[:, 0:S], xs[:, 0, cols].bitcast(F32),
                                            ALU.subtract).then_inc(misc_dve, 1)
                elif name == "logits":
                    n = ln_index(1, b)
                    lg = m[:, 0:64 * QT].rearrange("p (t e) -> p t e", t=QT)[:, :, 0:E_ALL]
                    nc.vector.tensor_reduce(rt_neg[:, :], lg, AX.X, ALU.max, negate=True).then_inc(neg_ready, 1)
                    dve.wait_ge(act_exp_rt, b + 1)
                    then(nc.vector.reciprocal(rt_sum[:, :], rt_sum[:, :]))
                    then(nc.vector.tensor_tensor(rt_s[:, :, :], rt_e[:, :, :],
                                                 rt_sum[:, :].unsqueeze(2).to_broadcast([P, QT, E_ALL]), ALU.mult))
                    then(nc.vector.tensor_tensor(rt_sel[:, :, 0:E_ALL], rt_s[:, :, :],
                                                 rowb[:, ROW_EB:ROW_EB + E_ALL].unsqueeze(1).to_broadcast([P, QT, E_ALL]),
                                                 ALU.add))
                    for t in range(QT):
                        last = nc.vector.max(rt_top[:, t, :], rt_sel[:, t, :])
                    then(last)
                    then(nc.vector.tensor_copy(rt_rep[:, :, 0:TOP_K], rt_top[:, :, 0:TOP_K]))
                    for t in range(QT):
                        last = nc.vector.match_replace(rt_mr[:, t, :], rt_rep[:, t, :], rt_sel[:, t, :], TAKEN)
                    then(last)
                    then(nc.vector.scalar_tensor_tensor(rt_w[:, :, :], rt_mr[:, :, 0:E_ALL], TAKEN, rt_s[:, :, :],
                                                        ALU.is_equal, ALU.mult))
                    then(nc.vector.tensor_scalar(rt_w[:, :, :], rt_w[:, :, :], ROUTE_SCALE, None, ALU.mult))
                    then(nc.vector.tensor_reduce(rt_zw[:, :], rt_w[:, :, E_ROUTED:E_ALL], AX.X, ALU.add))
                    for t in range(QT):
                        nc.vector.scalar_tensor_tensor(acc[:, 2 * b + t, :], xn[:, n % 2, t, :], rt_zw[:, t:t + 1],
                                                       xres[:, b % 2, t, :], ALU.mult, ALU.add)
                    left = rt_w[:, :, 0:E_ROUTED]
                    for i in range(W_PARTS):
                        part = rt_ws[:, b % 2, :, E_ROUTED * i:E_ROUTED * (i + 1)]
                        then(nc.vector.tensor_copy(rt_b[:, :, :], left))
                        if i < W_PARTS - 1:
                            nc.vector.tensor_copy(part, rt_b[:, :, :])
                            then(nc.vector.tensor_tensor(rt_r[:, :, :], left, rt_b[:, :, :], ALU.subtract))
                            left = rt_r[:, :, :]
                        else:
                            nc.vector.tensor_copy(part, rt_b[:, :, :]).then_inc(misc_dve, 1)
                    dve.wait_ge(misc_dve, misc_reads(task))
                elif name in ("wT", "ohT"):
                    if name == "wT" and b == 0:
                        dve.wait_ge(pool_consts, 1)
                    nc.vector.tensor_copy(wT[0:W_PARTS * E_ROUTED, S * b:S * (b + 1)], m[0:W_PARTS * E_ROUTED, 0:S]).then_inc(misc_dve, 1)
                elif name == "yT":
                    nc.vector.tensor_tensor(acc[:, 4 * b:4 * b + 4, :], acc[:, 4 * b:4 * b + 4, :],
                                            m.rearrange("p (t d) -> p t d", t=4), ALU.add).then_inc(misc_dve, 1)
                    dve.wait_ge(misc_dve, misc_reads(task))
                elif name == "s1":
                    then(nc.vector.tensor_tensor(sm1[:, b % 2, :, :], m.rearrange("p (t k) -> p t k", t=QT),
                                                 padneg[:, b, :].unsqueeze(1).to_broadcast([P, QT, S]), ALU.add))
                    nc.vector.tensor_reduce(nm1[:, b % 2, :], sm1[:, b % 2, :, :], AX.X, ALU.max,
                                            negate=True).then_inc(nm1_ready, 1)
                    dve.wait_ge(exp1_done, b + 1)
                    then(nc.vector.reciprocal(sum1[:, b % 2, :], sum1[:, b % 2, :]))
                    for t in range(QT):
                        last = nc.vector.tensor_scalar(sm1[:, b % 2, t, :], sm1[:, b % 2, t, :],
                                                       sum1[:, b % 2, t:t + 1], None, ALU.mult)
                    last.then_inc(misc_dve, 1)
                elif name == "oproj1":
                    then(nc.vector.tensor_tensor(acc[:, 2 * b:2 * b + 2, :], acc[:, 2 * b:2 * b + 2, :],
                                                 rowb[:, ROW_BO1:ROW_BO1 + D].unsqueeze(1).to_broadcast([P, QT, D]),
                                                 ALU.add))
                    nc.vector.tensor_tensor(xres[:, b % 2, :, :], acc[:, 2 * b:2 * b + 2, :],
                                            m[:, 0:QT * D].rearrange("p (t d) -> p t d", t=QT), ALU.add).then_inc(misc_dve, 1)
                    dve.wait_ge(misc_dve, misc_reads(task))
                    norm_begin(3, b, xres[:, b % 2, :, :])
                    norm_end(3, b, xres[:, b % 2, :, :])
                    nc.vector.memset(rt_zw[:, 1:2], 0.0).then_inc(xr_ready, 1)
                    dve.wait_ge(rms_ready, b + 1)
                    dve.wait_ge(acc4_ready, b + 1)
                    k = ln_index(3, b)
                    for t in range(QT):
                        last = nc.vector.tensor_scalar(xn[:, k % 2, t, :], xn[:, k % 2, t, :], ms4[:, b % 2, t:t + 1],
                                                       None, ALU.mult)
                    last.then_inc(x4_ready, 1)
                elif name == "xT4":
                    cols = slice(S * b, S * (b + 1))
                    then(nc.vector.tensor_scalar(cls32[:, b % 2, :], m[:, 0:S], small_w("scale"), None, ALU.mult))
                    nc.vector.memset(rt_zw[:, 1:2], 0.0).then_inc(xf_ready, 1)
                    then(nc.vector.tensor_copy(xs[:, 0, cols], cls32[:, b % 2, :]))
                    nc.vector.tensor_tensor(xs[:, 1, cols], cls32[:, b % 2, :], xs[:, 0, cols].bitcast(F32),
                                            ALU.subtract).then_inc(misc_dve, 1)
                elif name == "dist":
                    nc.vector.memset(d_oh[:, b % 2, :, E_ROUTED:], 0.0)
                    then(nc.vector.tensor_copy(d_nd[:, :, 0:E1], m[:, 0:E1 * QT].rearrange("p (t e) -> p t e", t=QT)))
                    for t in range(QT):
                        last = nc.vector.max(d_top[:, t, :], d_nd[:, t, :])
                    then(last)
                    then(nc.vector.tensor_copy(d_rep[:, :, 0:1], d_top[:, :, 0:1]))
                    for t in range(QT):
                        last = nc.vector.match_replace(d_mr[:, t, :], d_rep[:, t, :], d_nd[:, t, :], TAKEN)
                    then(last)
                    for t in range(QT):
                        last = nc.vector.tensor_scalar(
                            d_oh[:, b % 2, t, 0:E_ROUTED].rearrange("p (e r) -> p e r", r=4),
                            d_mr[:, t, 0:E1].unsqueeze(2).to_broadcast([P, E1, 4]), TAKEN, None, ALU.is_equal)
                    last.then_inc(misc_dve, 1)
                elif name == "final":
                    nc.vector.tensor_tensor(acc[:, 4 * b:4 * b + 4, :], acc[:, 4 * b:4 * b + 4, :],
                                            m.rearrange("p (t d) -> p t d", t=4), ALU.add).then_inc(misc_dve, 1)
                    dve.wait_ge(misc_dve, misc_reads(task))
                    nc.vector.memset(rt_zw[:, 1:2], 0.0).then_inc(fin_ready, 1)

            for s in range(SLOTS):
                if s < A_SLOTS:
                    b, j = s // PAIRS, s % PAIRS
                    if s == 0:
                        dve.wait_ge(pool_consts, 1)
                        for task in slot_tasks(0):
                            misc_task(*task)
                    dve.wait_ge(scores_max, s + 1)
                    nc.vector.tensor_reduce(negmax[:, b % 2, :, :].rearrange("p t (r j) -> p r t j", r=2)[:, :, :, j],
                                            psum[:, 0:2, :].rearrange("p r (t k) -> p r t k", t=QT), AX.X, ALU.max,
                                            negate=True).then_inc(maxes_read, 1)
                if s > 0:
                    for task in slot_tasks(s):
                        misc_task(*task)
                if s == 7:
                    dve.wait_ge(in_pad, 16)
                    then(nc.vector.tensor_scalar(padneg[:, :, :], pad8.rearrange("p (b k) -> p b k", b=B), NEG, None,
                                                 ALU.mult))

            n_unit = 0
            for stage in (0, 1):
                for g in range(GROUPS):
                    for u in range(UNITS):
                        n = n_unit
                        dve.wait_ge(silu_ready, n + 1)
                        nc.vector.tensor_tensor(sg[:, n % 2, :], sg[:, n % 2, :], psum[:, 2 + n % 2, :],
                                                ALU.mult).then_inc(up_read, 1)
                        dve.wait_ge(up_read, n + 1)
                        dve.wait_ge(wb_done, n + 1)
                        if n >= 2:
                            dve.wait_ge(lo_ready, n - 1)
                        nc.vector.tensor_tensor(h32[:, n % 2, :], sg[:, n % 2, :], psum[:, 4, :],
                                                ALU.mult).then_inc(hidden_ready, 1)
                        for name, b in unit_tasks(stage, g, u):
                            misc_task(name, b)
                            if name == "yT":
                                norm_begin(2, 2 * b, acc[:, 4 * b:4 * b + 2, :])
                                norm_end(2, 2 * b, acc[:, 4 * b:4 * b + 2, :])
                            if name == "xT3" and b % 2 == 0:
                                norm_begin(2, b + 1, acc[:, 2 * b + 2:2 * b + 4, :])
                                norm_end(2, b + 1, acc[:, 2 * b + 2:2 * b + 4, :])
                        n_unit += 1
            misc_task("final", GROUPS - 1)

        @block.tensor
        def _(pe):
            uses = misc_uses()

            def claim(task):
                k = uses.index(task)
                if k >= 2:
                    prev = uses[k - 2]
                    pe.wait_ge(misc_dve if MISC_READER[prev[0]] == "dve" else misc_act, misc_reads(prev))
                return misc_bank(task)

            def mm(o, w, r, start=True, stop=True):
                return nc.tensor.matmul(o, w, r, start=start, stop=stop, skip_group_check=True)

            def split3(o, wh, wl, xh, xl, start, stop):
                mm(o, wh, xh, start, False)
                mm(o, wh, xl, False, False)
                return mm(o, wl, xh, False, stop)

            def misc_task(name, b):
                task = (name, b)
                m = claim(task)
                if name == "notfull":
                    pe.wait_ge(masks_ready, 1)
                    pe.wait_ge(pool_consts, 1)
                    for t in range(QT):
                        last = mm(m[:, P * t:P * (t + 1)], ones[:, :], iddiag[:, t, :])
                elif name == "k1proj":
                    last = mm(m[:, 0:S], small_w("wk1"), ctxT[:, S * b:S * (b + 1)])
                elif name == "xT":
                    k = ln_index(0, b)
                    pe.wait_ge(normed, k + 1)
                    for t in range(QT):
                        last = nc.tensor.transpose(m[:, P * t:P * (t + 1)], xn[:, k % 2, t, :], id32[:, :])
                elif name == "qproj":
                    pe.wait_ge(misc_act, misc_reads(("xT", b)))
                    pe.wait_ge(in_small, 16)
                    mm(m[:, 0:S], small_w("wq"), xnT[:, b % 2, :])
                    last = mm(m[:, S:2 * S], small_w("wqr"), xnT[:, b % 2, :])
                elif name == "kproj":
                    pe.wait_ge(in_ctx, 16)
                    mm(m[:, 0:S], small_w("wk"), ctxT[:, S * b:S * (b + 1)])
                    last = mm(m[:, S:2 * S], small_w("wkr"), ctxT[:, S * b:S * (b + 1)])
                elif name == "vproj":
                    for k in range(QT):
                        last = mm(m[:, D * k:D * (k + 1)], ctxT[:, S * b + P * k:S * b + P * (k + 1)], small_w("wv"))
                elif name == "maxT":
                    pe.wait_ge(maxes_read, PAIRS * (b + 1))
                    for t in range(QT):
                        last = nc.tensor.transpose(m[0:16, P * t:P * (t + 1)], negmax[:, b % 2, t, :], id32[:, :])
                elif name in ("ctx0", "ctx1"):
                    t = 0 if name == "ctx0" else 1
                    pe.wait_ge(pv_evicted, 2 * (b + 1))
                    for q in range(QUADS):
                        last = nc.tensor.transpose(m[:, P * q:P * (q + 1)], pvT[:, q, P * t:P * (t + 1)], id32[:, :])
                elif name == "ctxT":
                    pe.wait_ge(misc_dve, misc_reads(("ctx1", b)))
                    for t in range(QT):
                        last = nc.tensor.transpose(m[:, P * t:P * (t + 1)], ctxn[:, b % 2, t, :], id32[:, :])
                elif name == "oproj":
                    pe.wait_ge(misc_act, misc_reads(("ctxT", b)))
                    for t in range(QT):
                        last = mm(m[:, D * t:D * (t + 1)], ctxnT[:, b % 2, P * t:P * (t + 1)], small_w("wo"))
                elif name in ("xT2", "xT3"):
                    k = ln_index(1 if name == "xT2" else 2, b)
                    pe.wait_ge(normed, k + 1)
                    for t in range(QT):
                        last = nc.tensor.transpose(m[:, P * t:P * (t + 1)], xn[:, k % 2, t, :], id32[:, :])
                elif name == "logits":
                    pe.wait_ge(misc_dve, misc_reads(("xT2", b)))
                    for t in range(QT):
                        last = mm(m[:, 64 * t:64 * t + E_ALL], cls32[:, b % 2, P * t:P * (t + 1)], small_w("cls"))
                elif name == "wT":
                    pe.wait_ge(misc_dve, misc_reads(("logits", b)))
                    for t in range(QT):
                        last = nc.tensor.transpose(m[0:W_PARTS * E_ROUTED, P * t:P * (t + 1)], rt_ws[:, b % 2, t, :], id32[:, :])
                elif name in ("yT", "final"):
                    pe.wait_ge(y_evicted, (b + 1) if name == "yT" else GROUPS + b + 1)
                    for t in range(4):
                        last = nc.tensor.transpose(m[:, P * t:P * (t + 1)], yT[:, P * t:P * (t + 1)], id32[:, :])
                elif name == "q1":
                    pe.wait_ge(misc_act, misc_reads(("xT3", b)))
                    last = mm(m[:, 0:S], small_w("wq1"), xT3[:, b % 2, :])
                elif name == "s1":
                    pe.wait_ge(misc_act, misc_reads(("q1", b)))
                    for t in range(QT):
                        last = mm(m[:, S * t:S * (t + 1)], q1T[:, b % 2, P * t:P * (t + 1)], k1T[:, b % 2, :])
                elif name == "pT":
                    pe.wait_ge(misc_dve, misc_reads(("s1", b)))
                    for k in range(QT):
                        for t in range(QT):
                            last = nc.tensor.transpose(m[:, S * k + P * t:S * k + P * (t + 1)],
                                                       sm1[:, b % 2, t, P * k:P * (k + 1)], id32[:, :])
                elif name == "pv1":
                    pe.wait_ge(misc_act, misc_reads(("pT", b)))
                    pe.wait_ge(in_late, 48)
                    for k in range(QT):
                        last = mm(m[:, 0:S], ctxk[:, QT * b + k, :], pT1[:, b % 2, k, :], k == 0, k == QT - 1)
                elif name == "oproj1":
                    pe.wait_ge(misc_act, misc_reads(("pv1", b)))
                    for t in range(QT):
                        last = mm(m[:, D * t:D * (t + 1)], q1T[:, b % 2, P * t:P * (t + 1)], small_w("wo1"))
                elif name == "xT4":
                    k = ln_index(3, b)
                    pe.wait_ge(x4_ready, b + 1)
                    for t in range(QT):
                        last = nc.tensor.transpose(m[:, P * t:P * (t + 1)], xn[:, k % 2, t, :], id32[:, :])
                elif name == "dist":
                    pe.wait_ge(misc_dve, misc_reads(("xT4", b)))
                    pe.wait_ge(xsq_done, b + 1)
                    pe.wait_ge(consts_ready, 1)
                    for t in range(QT):
                        o = m[:, E1 * t:E1 * (t + 1)]
                        mm(o, ones[:, :], c2[:, 1, :], t == 0, False)
                        mm(o, xsq[:, b % 2, P * t:P * (t + 1)], c2[:, 2, :], False, False)
                        last = mm(o, cls32[:, b % 2, P * t:P * (t + 1)], c2[:, 0, :], False, True)
                elif name == "ohT":
                    pe.wait_ge(misc_dve, misc_reads(("dist", b)))
                    for t in range(QT):
                        last = nc.tensor.transpose(m[0:W_PARTS * E_ROUTED, P * t:P * (t + 1)], d_oh[:, b % 2, t, :], id32[:, :])
                last.then_inc(misc_full, 1)

            misc_task("notfull", 0)
            for task in slot_tasks(0):
                misc_task(*task)
            for s in range(SLOTS):
                t = s - B_START
                has_a, has_b = s < A_SLOTS, 0 <= t < A_SLOTS
                a_b, a_j, b_b, b_j = s // PAIRS, s % PAIRS, t // PAIRS, t % PAIRS
                if has_a:
                    if s >= 1:
                        pe.wait_ge(maxes_read, s)
                    for r in range(2):
                        mm(psum[:, r, :], id16[:, :], maskb[:, 0, :, :].rearrange("p t k -> p (t k)"), True, False)
                if has_b:
                    if t >= 1:
                        pe.wait_ge(exps_done, t)
                    for r in range(2):
                        mm(psum[:, 2 + r, :], id16[:, :], maskb[:, 1, :, :].rearrange("p k q -> p (k q)"), True, False)
                if has_a:
                    if a_j == 0:
                        pe.wait_ge(stack_in[a_b], 256)
                    for q in range(QT):
                        for r in range(2):
                            rows_r = slice(64 * r, 64 * r + 32)
                            last = mm(psum[:, r, S * q:S * (q + 1)], stacks[rows_r, 0, a_b % 3, a_j, P * q:P * (q + 1)],
                                      stacks[rows_r, 1, a_b % 3, a_j, :], False, q == QT - 1)
                    last.then_inc(scores_max, 1)
                if has_b:
                    if b_j == 0:
                        pe.wait_ge(maxrow_in[b_b], 32)
                    for k in range(QT):
                        for r in range(2):
                            rows_r = slice(64 * r, 64 * r + 33)
                            last = mm(psum[:, 2 + r, S * k:S * (k + 1)], stacks[rows_r, 1, b_b % 3, b_j, P * k:P * (k + 1)],
                                      stacks[rows_r, 0, b_b % 3, b_j, :], False, k == QT - 1)
                    last.then_inc(scores_exp, 1)
                if 3 <= t <= A_SLOTS + 1 and t % 2 == 1:
                    qd = (t - 3) // 2
                    pb, pq = qd // QUADS, qd % QUADS
                    pe.wait_ge(exps_done, 2 * (qd + 1))
                    if pq == 0:
                        pe.wait_ge(misc_dve, misc_reads(("vproj", pb)))
                    if qd % 2 == 0 and qd >= 4:
                        pe.wait_ge(pv_evicted, qd // 2 - 1)
                    for k in range(QT):
                        for g in range(4):
                            last = mm(psum[32 * g:32 * (g + 1), BANK_PV + (qd // 2) % 2, S * (qd % 2):S * (qd % 2 + 1)],
                                      vaug[:, pb % 3, k, VW * (4 * pq + g):VW * (4 * pq + g) + 32], probs[:, (2 * qd + g // 2) % 4, g % 2, k, :],
                                      k == 0, k == QT - 1)
                    last.then_inc(pv_done, 1)
                if s > 0:
                    for task in slot_tasks(s):
                        misc_task(*task)

            def down(n):
                stage, g, u = n // (2 * UNITS), (n // UNITS) % 2, n % UNITS
                w = ws0 if stage == 0 else ws1
                pe.wait_ge(hi_ready, n + 1)
                pe.wait_ge(lo_ready, n + 1)
                if u == 0 and n > 0:
                    pe.wait_ge(y_evicted, n // UNITS)
                if n == 0:
                    pe.wait_ge(pv_evicted, 2 * B)
                cols = slice(P * u, P * (u + 1))
                split3(psum[:, 5, :], w[:, 2, 0, cols], w[:, 2, 1, cols], hs[:, n % 2, 0, :], hs[:, n % 2, 1, :],
                       u == 0, u == UNITS - 1).then_inc(y_done, 1)

            n_unit = 0
            for stage in (0, 1):
                w = ws0 if stage == 0 else ws1
                for g in range(GROUPS):
                    toks = slice(GT * g, GT * (g + 1))
                    if stage == 0:
                        pe.wait_ge(misc_dve, misc_reads(("wT", 2 * g + 1)))
                        pe.wait_ge(wsplit, 12)
                        pe.wait_ge(act_self, 1)
                        if g == 0:
                            pe.wait_ge(maxes_read, A_SLOTS)
                            pe.wait_ge(exps_done, A_SLOTS)
                            pe.wait_ge(pv_evicted, 2 * B - 1)
                    else:
                        pe.wait_ge(misc_dve, misc_reads(("ohT", 2 * g + 1)))
                        pe.wait_ge(wsplit, 24)
                    for u in range(UNITS):
                        n = n_unit
                        cols = slice(P * u, P * (u + 1))
                        if n >= 2:
                            pe.wait_ge(up_read, n - 1)
                        split3(psum[:, n % 2, :], w[:, 0, 0, cols], w[:, 0, 1, cols], xs[:, 0, toks], xs[:, 1, toks], True, True)
                        split3(psum[:, 2 + n % 2, :], w[:, 1, 0, cols], w[:, 1, 1, cols], xs[:, 0, toks], xs[:, 1, toks],
                               True, True).then_inc(gates_done, 1)
                        if n >= 1:
                            pe.wait_ge(hidden_ready, n)
                        mm(psum[:, 4, :], seln[:, u, :], wT[:, toks]).then_inc(wb_done, 1)
                        if n >= 1:
                            down(n - 1)
                        for task in unit_tasks(stage, g, u):
                            misc_task(*task)
                        n_unit += 1
            down(4 * UNITS - 1)
            misc_task("final", GROUPS - 1)


def rope_tables():
    inv = (1.0 / 10000.0 ** (np.arange(0, DK, 2, dtype=np.float32) / DK)).astype(np.float32)
    f = np.arange(S, dtype=np.float32)[None, :] * np.concatenate([inv, inv])[:, None]
    cos, sin = np.cos(f), np.sin(f)
    sign = np.array([-1.0] * (DK // 2) + [1.0] * (DK // 2), np.float32)[:, None]
    one = np.stack([cos / math.sqrt(DK), sign * sin / math.sqrt(DK), cos, sign * sin], axis=1)
    return np.tile(one, (H0, 1, 1)).astype(np.float32)


def selectors():
    m = np.zeros((P, UNITS, P), np.float32)
    for u in range(UNITS):
        for e in range(2):
            for i in range(W_PARTS):
                m[E_ROUTED * i + 2 * u + e, u, 64 * e:64 * (e + 1)] = 1.0
    return m.reshape(P, UNITS * P)


def kernel(x, ctx_1024, mask_1x1xSxS2_ik0, mask_BxS2_bk0, L0_xattn_w_q, L0_xattn_b_q, L0_xattn_w_k, L0_xattn_b_k,
           L0_xattn_w_v, L0_xattn_b_v, L0_xattn_w_o, L0_xattn_b_o, L0_ffn_classifier_weight,
           L0_ffn_e_score_correction_bias, L0_ffn_gate_up_proj, L0_ffn_down_proj, L1_xattn_Wq, L1_xattn_bq,
           L1_xattn_Wk, L1_xattn_bk, L1_xattn_Wo, L1_xattn_bo, L1_ffn_scale, L1_ffn_centroids, L1_ffn_up_w,
           L1_ffn_down_w):
    import concourse.bacc as bacc
    from concourse.bass_utils import run_bass_kernel_spmd as run

    a = np.asarray
    swap = np.concatenate([np.arange(1, DK, 2), np.arange(0, DK, 2)])
    turned = (DK * np.arange(H0)[:, None] + swap[None, :]).reshape(-1)
    wq, wk, bq, bk = a(L0_xattn_w_q), a(L0_xattn_w_k), a(L0_xattn_b_q), a(L0_xattn_b_k)
    small = np.concatenate([
        wq.T, wq[turned].T, wk.T, wk[turned].T, a(L0_xattn_w_v).T, a(L0_xattn_w_o).T, a(L1_xattn_Wq).T,
        a(L1_xattn_Wk).T, a(L1_xattn_Wo).T, a(L0_ffn_classifier_weight).T, a(L1_ffn_centroids).T, bq[:, None],
        bq[turned][:, None], bk[:, None], bk[turned][:, None], a(L1_xattn_bq)[:, None], a(L1_xattn_bk)[:, None],
        a(L1_ffn_scale)[:, None]], axis=1)
    rows = np.concatenate([a(L0_xattn_b_v), a(L0_xattn_b_o), a(L1_xattn_bo), a(L0_ffn_e_score_correction_bias)])[None]
    gu = a(L0_ffn_gate_up_proj)[:E_ROUTED].reshape(E_ROUTED, 2, 64, D)
    up1 = a(L1_ffn_up_w).reshape(E1, D, 2, CHUNK // E1)
    experts = np.stack([
        gu[:, 0].transpose(2, 0, 1).reshape(D, CHUNK),
        gu[:, 1].transpose(2, 0, 1).reshape(D, CHUNK),
        a(L0_ffn_down_proj).transpose(0, 2, 1).reshape(UNITS, P, D).transpose(1, 0, 2).reshape(P, CHUNK),
        up1[:, :, 1].transpose(1, 0, 2).reshape(D, CHUNK),
        up1[:, :, 0].transpose(1, 0, 2).reshape(D, CHUNK),
        a(L1_ffn_down_w).reshape(UNITS, P, D).transpose(1, 0, 2).reshape(P, CHUNK)], axis=1)
    mask = a(mask_1x1xSxS2_ik0)[0, 0]
    arrays = {
        "x": a(x).reshape(T, D), "ctx_t": a(ctx_1024).reshape(T, D).T, "ctx_tok": a(ctx_1024).reshape(T, D),
        "mask_q": mask.reshape(QT, P, S).transpose(1, 0, 2), "mask_k": mask.T.reshape(QT, P, S).transpose(1, 0, 2),
        "pad": a(mask_BxS2_bk0).reshape(1, T), "small": small, "rows": rows, "experts": experts,
        "ident": np.eye(P, dtype=np.float32), "rope": rope_tables(), "sel": selectors()}
    arrays = {k: np.ascontiguousarray(v) for k, v in arrays.items()}
    nc = bacc.Bacc("TRN2", target_bir_lowering=False, num_devices=1)
    aps = [nc.dram_tensor(k, v.shape, mybir.dt.from_np(v.dtype), kind="ExternalInput").ap() for k, v in arrays.items()]
    out = nc.dram_tensor("out", (T, D), F32, kind="ExternalOutput").ap()
    build(nc, *aps, out)
    result = run(nc, [arrays], core_ids=[0])
    return result.results[0]["out"].reshape(B, S, D)
```

```python
import math
from contextlib import ExitStack

import numpy as np

import concourse.bass as bass
from concourse import mybir

F32 = mybir.dt.float32
F32R = mybir.dt.float32r
BF16 = mybir.dt.bfloat16
I32 = mybir.dt.int32
U8 = mybir.dt.uint8
ALU = mybir.AluOpType
ACT = mybir.ActivationFunctionType
AX = mybir.AxisListType

P = 128
B, S, D = 4, 256, 128
T = B * S
TILES = T // P
QT = S // P
H0, DK = 16, 8
PAIRS = H0 // 2
QUADS = H0 // 4
VW = DK + 1
E_ROUTED, E_ZERO, TOP_K, ROUTE_SCALE = 32, 8, 6, 2.5
E_ALL = E_ROUTED + E_ZERO
E1 = 8
UNITS = 16
CHUNK = UNITS * P
GROUPS, GT = 2, 512
MASKED = -float(2 ** 30)
W_PARTS = 3
NEG = -3.0e38
TAKEN = 3.0e38
LN_EPS, RMS_EPS = 1e-5, 1e-6
LAG = 3
A_SLOTS = B * PAIRS
B_START = PAIRS + LAG
SLOTS = A_SLOTS + B_START + 1
DOWN_LAG = 3

SM = {}
_at = 0
for _name, _n in (("bq", 1), ("bqr", 1), ("bk", 1), ("bkr", 1), ("wq", D), ("wqr", D), ("wk", D), ("wkr", D),
                  ("wv", D), ("wo", D), ("wq1", D), ("wk1", D), ("wo1", D), ("cls", E_ALL), ("cent", E1),
                  ("bq1", 1), ("bk1", 1), ("scale", 1)):
    SM[_name] = (_at, _at + _n)
    _at += _n
SMALL = _at
SMALL_QK = SM["wv"][0]
ROW_BV, ROW_BO, ROW_BO1, ROW_EB = 0, D, 2 * D, 3 * D
ROWS = 3 * D + E_ALL


def misc_uses():
    uses = [("notfull", 0)]
    for s in range(SLOTS):
        uses += [t for t in slot_tasks(s) if t[0] in MISC_READER]
    for stage in (0, 1):
        for g in range(GROUPS):
            for u in range(UNITS):
                uses += [t for t in unit_tasks(stage, g, u) if t[0] in MISC_READER]
    uses += [("final", GROUPS - 1)]
    return uses


MISC_READER = {
    "notfull": "dve", "xT": "act", "qproj": "dve", "kproj": "dve", "vproj": "dve", "maxT": "dve", "ctx0": "dve",
    "ctx1": "dve", "ctxT": "act", "oproj": "dve", "xT2": "dve", "logits": "dve", "wT": "dve", "yT": "dve",
    "k1proj": "act", "xT3": "act", "q1": "act", "s1": "act", "s1_": "act", "pT": "act", "pT_": "act", "pv1": "act",
    "oproj1": "dve", "xT4": "dve", "dist": "dve", "ohT": "dve", "final": "dve",
}
PREP = {"xT": 3, "qproj": 4, "kproj": 5, "vproj": 6}
TAIL = {"ctx0": 0, "ctx1": 0, "ctxT": 1, "oproj": 2, "norm": 3, "xT2": 4, "logits": 5, "route": 6, "wT": 7}
SECOND = {"yT": 3, "norm2": 4, "k1proj": 4, "xT3": 5, "q1": 6, "s1": 7, "s1_": 7, "pT": 8, "pT_": 8, "pv1": 9,
          "oproj1": 10, "norm3": 11, "xT4": 12, "dist": 13, "ohT": 14}


def slot_tasks(s):
    tasks = []
    if s == 0:
        return [("xT", 0), ("qproj", 0), ("kproj", 0), ("xT", 1), ("qproj", 1), ("kproj", 1), ("vproj", 0)]
    if s == 3:
        tasks.append(("vproj", 1))
    for b in range(B):
        for name, at in PREP.items():
            first = 8 if b == B - 1 else 0
            if b > 1 and s == PAIRS * (b - 2) + at + first // 2 + (2 if b == B - 1 else 0):
                tasks.append((name, b))
        if s == PAIRS * (b + 1):
            tasks.append(("maxT", b))
        tasks += tail_tasks(s, b)
    return tasks


def tail_tasks(s, b):
    return [(name, b) for name, at in TAIL.items() if s == PAIRS * b + B_START + PAIRS + 1 + at]


def unit_tasks(stage, g, u):
    tasks = []
    if stage == 0 and g == 0:
        tasks += tail_tasks(SLOTS + u, B - 1)
    if (stage, g) in ((0, 1), (1, 0)):
        tasks += [(name, g ^ 1) for name, at in SECOND.items() if u == at]
    if stage == 1 and g == 1 and u == SECOND["yT"]:
        tasks.append(("final", 0))
    return tasks


def misc_index(task):
    return misc_uses().index(task)


def misc_reads(task):
    uses = misc_uses()
    k = uses.index(task)
    return sum(1 for t in uses[:k + 1] if MISC_READER[t[0]] == MISC_READER[task[0]])


def build(nc, x, ctx_t, ctx_tok, mask_q, mask_k, pad, small, rows, experts, ident, rope, sel, out):
    with ExitStack() as ctx:
        def sb(name, shape, dt=F32):
            return ctx.enter_context(nc.sbuf_tensor(name, shape, dt))

        def sem(name):
            return ctx.enter_context(nc.semaphore(name))

        psum = ctx.enter_context(nc.psum_tensor("psum", [P, 8, 512], F32))
        qk_scratch = nc.dram_tensor("qk_scratch", [B, 2, 2, 2, DK * PAIRS, S], F32, kind="Internal").ap()

        x_in = sb("x_in", [P, TILES, D])
        acc = x_in
        xn = sb("xn", [P, 2, QT, D])
        xres = sb("xres", [P, 2, QT, D])
        stats = sb("stats", [P, 2, QT, 6])
        mv = sb("mv", [P, 2, QT, 2])
        rstd = sb("rstd", [P, 2, QT])
        veps = sb("veps", [P, 2, QT])
        rms = sb("rms", [P, 3, 2, QT])
        half = sb("half", [P, 2, QT])
        id32 = sb("id32", [P, P])
        id16 = sb("id16", [P, P], BF16)
        sm = sb("sm", [P, SMALL])
        rowb = sb("rowb", [P, ROWS])
        ropet = sb("ropet", [P, 4, S])
        maskb = sb("maskb", [P, 2, QT, S], BF16)
        allmasked = sb("allmasked", [P, QT])
        iddiag = sb("iddiag", [P, QT, P])
        ones16 = iddiag[0:1, 0, 0:P // 2].bitcast(BF16)
        ones = sb("ones", [P, P])
        padneg = sb("padneg", [P, B, S], BF16)
        seln = sb("seln", [P, UNITS, P], BF16)
        ctxT = sb("ctxT", [P, T])
        ctxk = sb("ctxk", [P, TILES, D])
        xnT = sb("xnT", [P, 2, S])
        early = sb("early", [P, 6144])
        probs = early[:, 0:4096].rearrange("p (n r k q) -> p n r k q", n=4, r=2, k=QT)
        rot = early[:, 4096:6144].rearrange("p (n t i q) -> p n t i q", n=2, t=2, i=2)
        qk = sb("qk", [P, 2, S])
        parts = sb("parts", [P, 2048], F32R)
        qks = parts[:, :].rearrange("p (n t l q) -> p n t l q", n=2, t=2, l=2)
        big = sb("big", [P, 6 * CHUNK], F32R)
        stacks = big[:, :].rearrange("p (t b j q) -> p t b j q", t=2, b=3, j=PAIRS)
        vaug = sb("vaug", [P, 3, QT, VW * H0 + 32 - VW])
        vheads = vaug[:, :, :, 0:VW * H0].rearrange("p b k (h c) -> p b k h c", c=VW)
        negmax = sb("negmax", [P, 2, QT, 16])
        maxrow = sb("maxrow", [16, 2, S], F32R)
        pvT = sb("pvT", [P, QUADS, S])
        maskq_i = pvT[:, :, :].bitcast(I32).rearrange("p (m t) k -> p m t k", m=2)
        rden = sb("rden", [P, 2, H0])
        ctxn = sb("ctxn", [P, 2, QT, D])
        pad8 = ctxn[:, 0, :, :].rearrange("p t d -> p (t d)").bitcast(U8)
        ctxnT = sb("ctxnT", [P, 2, S])
        rt_neg = sb("rt_neg", [P, QT])
        rt_sum = sb("rt_sum", [P, QT])
        rt_e = sb("rt_e", [P, QT, E_ALL])
        rt_s = sb("rt_s", [P, QT, E_ALL])
        rt_sel = sb("rt_sel", [P, QT, E_ALL + 8])
        rt_top = sb("rt_top", [P, QT, 8])
        rt_rep = sb("rt_rep", [P, QT, 8])
        rt_mr = sb("rt_mr", [P, QT, E_ALL + 8])
        rt_w = sb("rt_w", [P, QT, E_ALL])
        rt_ws = sb("rt_ws", [P, 2, QT, W_PARTS * E_ROUTED])
        rt_b = sb("rt_b", [P, QT, E_ROUTED], BF16)
        rt_r = sb("rt_r", [P, QT, E_ROUTED])
        rt_zw = sb("rt_zw", [P, QT])
        cls32 = xnT
        wT = sb("wT", [P, T], BF16)
        raw = sb("raw", [P, 2, CHUNK // 2])
        ws0 = sb("ws0", [P, 3, 2, CHUNK], F32R)
        ws1 = big[:, :].rearrange("p (c h n) -> p c h n", c=3, h=2)
        xs = sb("xs", [P, 2, T], F32R)
        sg = early[:, 0:1024].rearrange("p (n t) -> p n t", n=2)
        h32 = early[:, 1024:2048].rearrange("p (n t) -> p n t", n=2)
        yT = early[:, 2048:2560]
        k1T = sb("k1T", [P, 2, S])
        xT3 = early[:, 2560:3072].rearrange("p (n q) -> p n q", n=2)
        q1T = early[:, 3072:3584].rearrange("p (n q) -> p n q", n=2)
        sm1 = early[:, 3584:4608].rearrange("p (n t k) -> p n t k", n=2, t=QT)
        pT1 = early[:, 4608:5632].rearrange("p (n k q) -> p n k q", n=2, k=QT)
        nm1 = sb("nm1", [P, 2, QT])
        sum1 = sb("sum1", [P, 2, QT])
        x4n = ctxn
        xsq = qk
        c2 = sb("c2", [P, 3, E1])
        d_nd = sb("d_nd", [P, GT // P, 16])
        d_top = sb("d_top", [P, GT // P, 8])
        d_rep = sb("d_rep", [P, GT // P, 8])
        d_mr = rt_mr[:, :, :].rearrange("p t e -> p (t e)")[:, 0:GT // P * 16].rearrange("p (t c) -> p t c", c=16)
        d_oh = rt_ws

        in_x, in_x1, in_xrest, in_ctx0, in_ctx, in_qkw, in_small, in_ident, in_rope, in_mask, in_rows, in_pad, in_late = (
            sem(n) for n in ("in_x", "in_x1", "in_xrest", "in_ctx0", "in_ctx", "in_qkw", "in_small", "in_ident", "in_rope",
                             "in_mask", "in_rows", "in_pad", "in_late"))
        ones_rows = sem("ones_rows")
        in_raw = [sem(f"in_raw{i}") for i in range(12)]
        scratch_out = [sem(f"scratch_out{b}") for b in range(B)]
        stack_in = [sem(f"stack_in{b}") for b in range(B)]
        maxrow_in = [sem(f"maxrow_in{b}") for b in range(B)]
        out_done = sem("out_done")
        dve_self, pool_self, act_self = sem("dve_self"), sem("pool_self"), sem("act_self")
        misc_full, misc_dve, misc_act = sem("misc_full"), sem("misc_dve"), sem("misc_act")
        consts_ready, masks_ready, norm_stats, normed = (sem(n) for n in ("consts_ready", "masks_ready", "norm_stats", "normed"))
        rot_ready, v_ready, maxes_read, maxrow_ready, ctxn_ready, neg_ready = (
            sem(n) for n in ("rot_ready", "v_ready", "maxes_read", "maxrow_ready", "ctxn_ready", "neg_ready"))
        x2_ready, xs_ready, ws_ready, wT_ready = (sem(n) for n in ("x2_ready", "xs_ready", "ws_ready", "wT_ready"))
        hidden_ready, up_read, nm1_ready, dve_consts, qk_ready, xf_ready, xlo_ready, routed, fin_ready, x4_ready = (
            sem(n) for n in ("hidden_ready", "up_read", "nm1_ready", "dve_consts", "qk_ready", "xf_ready", "xlo_ready",
                             "routed", "fin_ready", "x4_ready"))
        rstd_ready, qks_ready, pool_consts, wsplit, lo_ready, acc4_ready = (
            sem(n) for n in ("rstd_ready", "qks_ready", "pool_consts", "wsplit", "lo_ready", "acc4_ready"))
        exps_done, pv_evicted, act_exp_rt, silu_ready, hi_ready, y_evicted, exp1_done, whi_ready, xsq_done, qhi_ready = (
            sem(n) for n in ("exps_done", "pv_evicted", "act_exp_rt", "silu_ready", "hi_ready", "y_evicted",
                             "exp1_done", "whi_ready", "xsq_done", "qhi_ready"))
        scores_max, scores_exp, pv_done, gates_done, wb_done, y_done = (
            sem(n) for n in ("scores_max", "scores_exp", "pv_done", "gates_done", "wb_done", "y_done"))

        def hs(n):
            if n % 4 < 2:
                room = parts[:, 1024 * (n % 4):1024 * (n % 4 + 1)]
            elif n < 2 * UNITS:
                room = ws1[:, 2, n % 4 - 2, CHUNK // 2:CHUNK]
            else:
                room = ws0[:, 0, n % 4 - 2, 0:CHUNK // 2]
            return room.rearrange("p (l t) -> p l t", l=2)

        def small_w(name):
            return sm[:, SM[name][0]:SM[name][1]]

        def misc_bank(task):
            return psum[:, 6 + misc_index(task) % 2, :]

        BANK_PV = 4

        def a_bank(s):
            return 2 if s < B_START and s % 2 == 1 else 0

        def ln_index(kind, b):
            return LN_ORDER.index((kind, b))

        block = ctx.enter_context(nc.Block())

        LN_ORDER = [(0, 0), (0, 1)]
        for s in range(SLOTS):
            for name, b in slot_tasks(s):
                if name == "vproj" and 2 <= b + 1 < B:
                    LN_ORDER.append((0, b + 1))
                if name == "oproj":
                    LN_ORDER.append((1, b))
        for u in range(UNITS):
            for name, b in unit_tasks(0, 0, u):
                if name == "oproj":
                    LN_ORDER.append((1, b))
        for g in range(GROUPS):
            LN_ORDER += [(2, g), (3, g)]

        @block.sync
        def _(sp):
            def x_batches(lo, hi, signal):
                sp.dma_start(x_in[:, QT * lo:QT * hi, :],
                             x[S * lo:S * hi, :].rearrange("(t p) d -> p t d", p=P)).then_inc(signal, 16)

            x_batches(0, 1, in_x)
            sp.dma_start(id32[:, :], ident).then_inc(in_ident, 16)
            sp.dma_start(maskq_i[:, 0, :, :], mask_q).then_inc(in_mask, 16)
            sp.dma_start(maskq_i[:, 1, :, :], mask_k).then_inc(in_mask, 16)
            sp.dma_start(sm[:, 0:SMALL_QK], small[:, 0:SMALL_QK]).then_inc(in_qkw, 16)
            sp.dma_start(ctxT[:, 0:S], ctx_t[:, 0:S]).then_inc(in_ctx0, 16)
            sp.dma_start(ropet[:, :, :], rope).then_inc(in_rope, 16)
            x_batches(1, 2, in_x1)
            sp.dma_start(ctxT[:, S:T], ctx_t[:, S:T]).then_inc(in_ctx, 16)
            sp.dma_start(sm[:, SMALL_QK:SMALL], small[:, SMALL_QK:SMALL]).then_inc(in_small, 16)
            sp.dma_start(rowb[:, :], rows.to_broadcast([P, ROWS])).then_inc(in_rows, 16)

            def late_loads():
                x_batches(2, B, in_xrest)
                sp.dma_start(sg[:, :, :], sel[:, 0:1024]).then_inc(in_late, 16)
                sp.dma_start(h32[:, :, :], sel[:, 1024:2048]).then_inc(in_late, 16)
                sp.dma_start(pad8, pad.to_broadcast([P, T])).then_inc(in_pad, 16)
                sp.dma_start(ctxk[:, :, :], ctx_tok.rearrange("(t p) d -> p t d", p=P)).then_inc(in_late, 16)

            def stack_batch(b):
                sp.wait_ge(qks_ready, b + 1)
                for r in range(2):
                    sp.dma_start(qk_scratch[b, r].rearrange("t l c q -> c t l q"),
                                 qks[64 * r:64 * (r + 1), b % 2, :, :, :].bitcast(F32)).then_inc(scratch_out[b], 16)
                sp.wait_ge(scratch_out[b], 32)
                if b >= 3:
                    sp.wait_ge(scores_exp, PAIRS * (b - 2))
                for r in range(2):
                    src = qk_scratch[b, r].rearrange("t l (d j) q -> t l d (j q)", j=PAIRS)
                    dst = stacks[64 * r:64 * r + 32, :, b % 3, :, :].bitcast(F32).rearrange("c t j q -> c t (j q)")
                    sp.dma_start(dst[:, 0, :], src[0].unsqueeze(0).to_broadcast([2, 2, DK, PAIRS * S])).then_inc(stack_in[b], 16)
                    for k in range(2):
                        sp.dma_start(dst[16 * k:16 * (k + 1), 1, :],
                                     src[1, k].unsqueeze(0).to_broadcast([2, DK, PAIRS * S])).then_inc(stack_in[b], 16)

            def maxrow_batch(b):
                sp.wait_ge(maxrow_ready, b + 1)
                for r in range(2):
                    sp.dma_start(stacks[64 * r + 32:64 * r + 33, 0, b % 3, :, :].bitcast(F32),
                                 maxrow[PAIRS * r:PAIRS * (r + 1), b % 2, :].bitcast(F32)).then_inc(maxrow_in[b], 16)

            for s in range(SLOTS):
                for name, b in slot_tasks(s):
                    if name == "kproj":
                        stack_batch(b)
                    if name == "maxT":
                        maxrow_batch(b)
                if s == 0:
                    late_loads()
            for g in range(GROUPS):
                sp.wait_ge(fin_ready, g + 1)
                sp.dma_start(out[GT * g:GT * (g + 1), :].rearrange("(t p) d -> p t d", p=P),
                             acc[:, 4 * g:4 * g + 4, :]).then_inc(out_done, 16)
            sp.wait_ge(out_done, 16 * GROUPS)

        @block.gpsimd
        def _(pool):
            own = [0]

            def then(ins):
                own[0] += 1
                ins.then_inc(pool_self, 1)
                pool.wait_ge(pool_self, own[0])

            nc.gpsimd.memset(half[:, :, :], -0.5)
            nc.gpsimd.memset(ones[:, :], 1.0)
            nc.gpsimd.memset(wT[:, :], 0.0).then_inc(pool_consts, 1)
            pool.wait_ge(pool_consts, 1)

            def ones_beside_keys(buffer):
                for r in range(2):
                    nc.gpsimd.memset(stacks[64 * r + 32:64 * r + 33, 1, buffer, :, :].bitcast(F32), 1.0).then_inc(ones_rows, 1)
                pool.wait_ge(ones_rows, 2 * (buffer + 1))

            ones_beside_keys(0)

            def inv_sqrt(n, at):
                pool.wait_ge(norm_stats, n + 1)
                then(nc.gpsimd.tensor_scalar_add(veps[:, at, :], mv[:, at, :, 1], LN_EPS))
                nc.gpsimd.tensor_tensor(rstd[:, at, :], veps[:, at, :], half[:, 0, :], ALU.pow).then_inc(rstd_ready, 1)

            def inv_sqrt_group(n, with_rms):
                pool.wait_ge(norm_stats, n + 1)
                then(nc.gpsimd.tensor_scalar_add(veps[:, :, :], mv[:, :, :, 1], LN_EPS))
                last = nc.gpsimd.tensor_tensor(rstd[:, :, :], veps[:, :, :], half[:, :, :], ALU.pow)
                if with_rms:
                    then(last)
                    then(nc.gpsimd.tensor_tensor(rms[:, 0, :, :], mv[:, :, :, 1], rstd[:, :, :], ALU.mult))
                    then(nc.gpsimd.tensor_tensor(rms[:, 0, :, :], rms[:, 0, :, :], rstd[:, :, :], ALU.mult))
                    then(nc.gpsimd.tensor_scalar_add(rms[:, 0, :, :], rms[:, 0, :, :], RMS_EPS))
                    then(nc.gpsimd.tensor_tensor(rms[:, 1, :, :], rms[:, 0, :, :], half[:, :, :], ALU.pow))
                    last = nc.gpsimd.tensor_tensor(rms[:, 2, :, :], rms[:, 1, :, :], rstd[:, :, :], ALU.mult)
                last.then_inc(rstd_ready, 1)

            def split_qk(b):
                pool.wait_ge(qhi_ready, b + 1)
                nc.gpsimd.tensor_tensor(qks[:, b % 2, :, 1, :], qk[:, :, :], qks[:, b % 2, :, 0, :].bitcast(F32),
                                        ALU.subtract).then_inc(qks_ready, 1)

            def split_weights(i):
                c, q = i // 4, i % 4
                pool.wait_ge(whi_ready, i + 1)
                ws = (ws0 if c < 3 else ws1)[:, c % 3, :, 512 * q:512 * (q + 1)]
                src = raw[:, (i // 2) % 2, 512 * (q % 2):512 * (q % 2 + 1)]
                nc.gpsimd.tensor_tensor(ws[:, 1, :], src, ws[:, 0, :].bitcast(F32), ALU.subtract).then_inc(wsplit, 1)

            inv_sqrt(0, 0)
            inv_sqrt(1, 1)
            wi = 0
            for s in range(SLOTS):
                if s in (1, 2):
                    pool.wait_ge(qks_ready, 2)
                    ones_beside_keys(s)
                for name, b in slot_tasks(s):
                    if name == "kproj":
                        split_qk(b)
                    if name == "vproj" and 2 <= b + 1 < B:
                        inv_sqrt(ln_index(0, b + 1), ln_index(0, b + 1) % 2)
                    if name == "oproj":
                        inv_sqrt(ln_index(1, b), ln_index(1, b) % 2)
                if s % 3 == 2 and wi < 12:
                    split_weights(wi)
                    wi += 1

            n_unit = 0
            for stage in (0, 1):
                for g in range(GROUPS):
                    for u in range(UNITS):
                        n = n_unit
                        for name, b in unit_tasks(stage, g, u):
                            if name == "oproj":
                                inv_sqrt(ln_index(1, b), ln_index(1, b) % 2)
                            if name == "yT":
                                inv_sqrt_group(ln_index(2, b), False)
                            if name == "oproj1":
                                inv_sqrt_group(ln_index(3, b), True)
                            if name == "dist":
                                for t in range(4):
                                    last = nc.gpsimd.tensor_scalar(xn[:, t // 2, t % 2, :], xres[:, t // 2, t % 2, :],
                                                                   mv[:, t // 2, t % 2, 0:1],
                                                                   rstd[:, t // 2, t % 2:t % 2 + 1], ALU.subtract, ALU.mult)
                                then(last)
                                nc.gpsimd.tensor_tensor(acc[:, 4 * b:4 * b + 4, :],
                                                        xres[:, :, :, :].rearrange("p a t d -> p (a t) d"),
                                                        xn[:, :, :, :].rearrange("p a t d -> p (a t) d"),
                                                        ALU.add).then_inc(acc4_ready, 1)
                        pool.wait_ge(hi_ready, n + 1)
                        nc.gpsimd.tensor_tensor(hs(n)[:, 1, :], h32[:, n % 2, :], hs(n)[:, 0, :].bitcast(F32),
                                                ALU.subtract).then_inc(lo_ready, 1)
                        if wi < 24 and n % 2 == 1 and (wi < 22 or n > 2 * UNITS + DOWN_LAG):
                            split_weights(wi)
                            wi += 1
                        n_unit += 1

        @block.scalar
        def _(act):
            for k in range(2):
                nc.scalar.dma_start(raw[:, k, :], experts[:, 0, 1024 * k:1024 * (k + 1)]).then_inc(in_raw[k], 16)

            def unpack_selectors():
                act.wait_ge(in_late, 48)
                nc.scalar.copy(seln[:, 0:8, :], sg[:, :, :].rearrange("p a (b n) -> p (a b) n", n=P))
                nc.scalar.copy(seln[:, 8:16, :], h32[:, :, :].rearrange("p a (b n) -> p (a b) n", n=P)).then_inc(act_self, 1)
                act.wait_ge(act_self, 1)

            def split_weights(i):
                c, q = i // 4, i % 4
                if q % 2 == 0:
                    act.wait_ge(in_raw[i // 2], 16)
                if q % 2 == 0 and 4 <= i + 2 and i >= 2 and i // 2 + 1 < 12:
                    act.wait_ge(wsplit, i)
                    k = i // 2 + 1
                    nc.scalar.dma_start(raw[:, k % 2, :],
                                        experts[:, k // 2, 1024 * (k % 2):1024 * (k % 2 + 1)]).then_inc(in_raw[k], 16)
                if i == 12:
                    act.wait_ge(scores_exp, A_SLOTS)
                if i == 22:
                    act.wait_ge(y_done, 2 * UNITS)
                ws = (ws0 if c < 3 else ws1)[:, c % 3, :, 512 * q:512 * (q + 1)]
                src = raw[:, (i // 2) % 2, 512 * (q % 2):512 * (q % 2 + 1)]
                nc.scalar.copy(ws[:, 0, :], src).then_inc(whi_ready, 1)

            def evict(task, dst, src, bias=None):
                act.wait_ge(misc_full, misc_index(task) + 1)
                if bias is None:
                    nc.scalar.copy(dst, src).then_inc(misc_act, 1)
                else:
                    nc.scalar.activation(dst, src, ACT.Identity, bias=bias).then_inc(misc_act, 1)

            def misc_task(name, b):
                task = (name, b)
                m = misc_bank(task) if name in MISC_READER else None
                if name == "xT":
                    evict(task, xnT[:, b % 2, :], m[:, 0:S])
                elif name == "kproj":
                    act.wait_ge(qk_ready, b + 1)
                    if b >= 2:
                        act.wait_ge(scratch_out[b - 2], 32)
                    nc.scalar.copy(qks[:, b % 2, :, 0, :], qk[:, :, :]).then_inc(qhi_ready, 1)
                elif name == "ctxT":
                    evict(task, ctxnT[:, b % 2, :], m[:, 0:S])
                elif name == "logits":
                    act.wait_ge(neg_ready, b + 1)
                    for t in range(QT):
                        last = nc.scalar.activation(rt_e[:, t, :], rt_s[:, t, :], ACT.Exp,
                                                    bias=rt_neg[:, t:t + 1], accum_out=rt_sum[:, t:t + 1])
                    last.then_inc(act_exp_rt, 1)
                elif name == "k1proj":
                    evict(task, k1T[:, :, :].rearrange("p b k -> p (b k)"), m, small_w("bk1"))
                elif name == "xT3":
                    evict(task, xT3[:, :, :].rearrange("p b q -> p (b q)"), m)
                elif name == "q1":
                    evict(task, q1T[:, :, :].rearrange("p b q -> p (b q)"), m, small_w("bq1"))
                elif name in ("s1", "s1_"):
                    k = int(name == "s1_")
                    act.wait_ge(nm1_ready, 2 * b + k + 1)
                    for t in range(QT):
                        last = nc.scalar.activation(sm1[:, k, t, :], m[:, S * t:S * (t + 1)], ACT.Exp,
                                                    bias=nm1[:, k, t:t + 1], accum_out=sum1[:, k, t:t + 1])
                    last.then_inc(misc_act, 1)
                elif name in ("pT", "pT_"):
                    evict(task, pT1[:, int(name == "pT_"), :, :], m.rearrange("p (k q) -> p k q", k=QT))
                elif name == "pv1":
                    evict(task, q1T[:, :, :].rearrange("p b q -> p (b q)"), m)
                elif name == "xT4":
                    act.wait_ge(xf_ready, b + 1)
                    nc.scalar.copy(xs[:, 0, GT * b:GT * (b + 1)], cls32[:, :, :].rearrange("p a q -> p (a q)"))
                    nc.scalar.activation(xsq[:, :, :], cls32[:, :, :], ACT.Square).then_inc(xsq_done, 1)

            for s in range(SLOTS):
                t = s - B_START
                if 0 <= t < A_SLOTS:
                    act.wait_ge(scores_exp, t + 1)
                    if t >= 4:
                        act.wait_ge(pv_done, t - 3)
                    nc.scalar.activation(probs[:, t % 4, :, :, :],
                                         psum[:, 2:4, :].rearrange("p r (k q) -> p r k q", k=QT),
                                         ACT.Exp).then_inc(exps_done, 1)
                if t >= 4 and t % 4 == 0:
                    c = t // 4 - 1
                    act.wait_ge(pv_done, 4 * (c + 1))
                    if c == 0:
                        act.wait_ge(masks_ready, 1)
                    elif c % 2 == 0:
                        act.wait_ge(misc_full, misc_index(("ctx1", c // 2 - 1)) + 1)
                    nc.scalar.copy(pvT[:, 2 * (c % 2):2 * (c % 2) + 2, :],
                                   psum[:, BANK_PV + c % 2, :].rearrange("p (a q) -> p a q", a=2)).then_inc(pv_evicted, 1)
                for name, b in slot_tasks(s):
                    misc_task(name, b)
                if s == 2:
                    unpack_selectors()
                if s % 3 == 2 and s // 3 < 12:
                    split_weights(s // 3)

            wi = 12
            for n in range(4 * UNITS):
                stage, g, u = n // (2 * UNITS), (n // UNITS) % 2, n % UNITS
                act.wait_ge(gates_done, n + 1)
                if n >= 2:
                    act.wait_ge(hidden_ready, n - 1)
                nc.scalar.activation(sg[:, n % 2, :], psum[:, n % 2, :], ACT.Silu).then_inc(silu_ready, 1)
                if wi < 24 and n % 2 == 1 and (wi < 22 or n > 2 * UNITS + DOWN_LAG):
                    split_weights(wi)
                    wi += 1
                act.wait_ge(hidden_ready, n + 1)
                if n >= 4:
                    act.wait_ge(y_done, n - 3)
                nc.scalar.copy(hs(n)[:, 0, :], h32[:, n % 2, :]).then_inc(hi_ready, 1)
                if u == DOWN_LAG - 1 and n > UNITS:
                    k = n // UNITS - 1
                    act.wait_ge(y_done, UNITS * (k + 1))
                    if k >= 1:
                        act.wait_ge(misc_full, misc_index(("yT", k - 1) if k < 3 else ("final", 0)) + 1)
                    nc.scalar.copy(yT[:, :], psum[:, 5, :]).then_inc(y_evicted, 1)
                for name, b in unit_tasks(stage, g, u):
                    misc_task(name, b)
            act.wait_ge(y_done, 4 * UNITS)
            act.wait_ge(misc_full, misc_index(("final", 0)) + 1)
            nc.scalar.copy(yT[:, :], psum[:, 5, :]).then_inc(y_evicted, 1)

        @block.vector
        def _(dve):
            own = [0]

            def then(ins):
                own[0] += 1
                ins.then_inc(dve_self, 1)
                dve.wait_ge(dve_self, own[0])

            def norm_begin(at, src):
                for t in range(QT):
                    last = nc.vector.bn_stats(stats[:, at, t, :], src[:, t, :])
                then(last)
                for t in range(QT):
                    last = nc.vector.bn_aggr(mv[:, at, t, :], stats[:, at, t, :])
                last.then_inc(norm_stats, 1)

            def norm_begin_group(src):
                for t in range(4):
                    last = nc.vector.bn_stats(stats[:, t // 2, t % 2, :], src(t))
                then(last)
                for t in range(4):
                    last = nc.vector.bn_aggr(mv[:, t // 2, t % 2, :], stats[:, t // 2, t % 2, :])
                last.then_inc(norm_stats, 1)

            def norm_end(n, src):
                dve.wait_ge(rstd_ready, n + 1)
                for t in range(QT):
                    last = nc.vector.tensor_scalar(xn[:, n % 2, t, :], src[:, t, :], mv[:, n % 2, t, 0:1],
                                                   rstd[:, n % 2, t:t + 1], ALU.subtract, ALU.mult)
                last.then_inc(normed, 1)

            nc.vector.memset(vaug[:, :, :, :], 1.0)
            nc.vector.memset(c2[:, 2, :], -1.0)
            nc.vector.memset(rt_sel[:, :, :], NEG)
            nc.vector.memset(rt_rep[:, :, :], NEG)
            nc.vector.memset(d_nd[:, :, :], NEG)
            nc.vector.memset(d_rep[:, :, :], NEG).then_inc(dve_consts, 1)
            dve.wait_ge(in_x, 16)
            norm_begin(0, x_in[:, 0:QT, :])
            dve.wait_ge(in_ident, 16)
            nc.vector.tensor_copy(id16[:, :], id32[:, :])
            norm_end(0, x_in[:, 0:QT, :])
            dve.wait_ge(in_mask, 32)
            then(nc.vector.tensor_scalar(maskb[:, :, :, :], maskq_i[:, :, :, :], 0.0, MASKED, ALU.is_equal, ALU.mult))
            then(nc.vector.tensor_reduce(allmasked[:, :], maskb[:, 0, :, :], AX.X, ALU.max))
            then(nc.vector.tensor_scalar(allmasked[:, :], allmasked[:, :], -1.0, None, ALU.is_gt))
            for t in range(QT):
                last = nc.vector.tensor_scalar(iddiag[:, t, :], id32[:, :], allmasked[:, t:t + 1], None, ALU.mult)
            last.then_inc(masks_ready, 1)
            dve.wait_ge(in_x1, 16)
            norm_begin(1, x_in[:, QT:2 * QT, :])
            dve.wait_ge(misc_full, misc_index(("notfull", 0)) + 1)
            dve.wait_ge(in_rope, 16)
            for t in range(2):
                last = nc.vector.tensor_tensor(ropet[:, t, :], ropet[:, t, :], misc_bank(("notfull", 0))[:, 0:S], ALU.mult)
            last.then_inc(misc_dve, 1)
            dve.wait_ge(misc_dve, 1)
            norm_end(1, x_in[:, QT:2 * QT, :])
            dve.wait_ge(in_qkw, 16)
            dve.wait_ge(dve_consts, 1)

            def late_consts():
                dve.wait_ge(in_small, 16)
                nc.vector.tensor_scalar(c2[:, 0, :], small_w("cent"), 2.0, None, ALU.mult)
                nc.vector.scalar_tensor_tensor(c2[:, 1, :], small_w("cent"), -1.0, small_w("cent"), ALU.mult, ALU.mult)
                nc.vector.memset(ones16, 1.0).then_inc(consts_ready, 1)
                dve.wait_ge(in_rows, 16)
                dve.wait_ge(in_pad, 16)
                then(nc.vector.tensor_scalar(padneg[:, :, :], pad8.rearrange("p (b k) -> p b k", b=B), NEG, None,
                                             ALU.mult))

            def misc_task(name, b):
                task = (name, b)
                if name in MISC_READER:
                    m = misc_bank(task)
                    if MISC_READER[name] != "dve" and name not in ("s1", "s1_"):
                        return
                    dve.wait_ge(misc_full, misc_index(task) + 1)
                if name in ("qproj", "kproj"):
                    t, names = (0, ("bq", "bqr")) if name == "qproj" else (1, ("bk", "bkr"))
                    nc.vector.scalar_tensor_tensor(rot[:, b % 2, t, 0, :], m[:, 0:S], small_w(names[0]),
                                                   ropet[:, 2 * t, :] if t else ropet[:, 0, :], ALU.add, ALU.mult)
                    nc.vector.scalar_tensor_tensor(rot[:, b % 2, t, 1, :], m[:, S:2 * S], small_w(names[1]),
                                                   ropet[:, 2 * t + 1, :] if t else ropet[:, 1, :], ALU.add,
                                                   ALU.mult).then_inc(misc_dve, 1)
                    if name == "kproj":
                        dve.wait_ge(misc_dve, misc_reads(task))
                        if b >= 1:
                            dve.wait_ge(qks_ready, b)
                        nc.vector.tensor_tensor(qk[:, :, :], rot[:, b % 2, :, 0, :], rot[:, b % 2, :, 1, :],
                                                ALU.add).then_inc(qk_ready, 1)
                elif name == "vproj":
                    if b >= 3:
                        dve.wait_ge(pv_done, PAIRS * (b - 2))
                    for k in range(QT):
                        last = nc.vector.tensor_tensor(
                            vheads[:, b % 3, k, :, 0:DK], m[:, D * k:D * (k + 1)].rearrange("p (h d) -> p h d", d=DK),
                            rowb[:, ROW_BV:ROW_BV + D].rearrange("p (h d) -> p h d", d=DK), ALU.add)
                    last.then_inc(misc_dve, 1)
                    if 2 <= b + 1 < B:
                        dve.wait_ge(in_xrest, 16)
                        norm_begin((b + 1) % 2, x_in[:, QT * (b + 1):QT * (b + 2), :])
                elif name == "maxT":
                    nc.vector.tensor_copy(maxrow[:, b % 2, :], m[0:16, 0:S]).then_inc(misc_dve, 1)
                    dve.wait_ge(misc_dve, misc_reads(task))
                    nc.vector.memset(rt_zw[:, 1:2], 0.0).then_inc(maxrow_ready, 1)
                elif name in ("ctx0", "ctx1"):
                    t = 0 if name == "ctx0" else 1
                    v = m.rearrange("p (h c) -> p h c", c=32)
                    then(nc.vector.reciprocal(rden[:, t, :], v[:, :, DK]))
                    nc.vector.tensor_tensor(ctxn[:, b % 2, t, :].rearrange("p (h d) -> p h d", d=DK), v[:, :, 0:DK],
                                            rden[:, t, :].unsqueeze(2).to_broadcast([P, H0, DK]),
                                            ALU.mult).then_inc(misc_dve, 1)
                elif name == "oproj":
                    then(nc.vector.tensor_tensor(x_in[:, 2 * b:2 * b + 2, :], x_in[:, 2 * b:2 * b + 2, :],
                                                 rowb[:, ROW_BO:ROW_BO + D].unsqueeze(1).to_broadcast([P, QT, D]), ALU.add))
                    nc.vector.tensor_tensor(xres[:, b % 2, :, :], x_in[:, 2 * b:2 * b + 2, :],
                                            m[:, 0:QT * D].rearrange("p (t d) -> p t d", t=QT), ALU.add).then_inc(misc_dve, 1)
                    dve.wait_ge(misc_dve, misc_reads(task))
                    norm_begin(ln_index(1, b) % 2, xres[:, b % 2, :, :])
                elif name == "norm":
                    norm_end(ln_index(1, b), xres[:, b % 2, :, :])
                elif name == "xT2":
                    cols = slice(S * b, S * (b + 1))
                    then(nc.vector.tensor_copy(cls32[:, b % 2, :], m[:, 0:S]))
                    then(nc.vector.tensor_copy(xs[:, 0, cols], m[:, 0:S]))
                    nc.vector.tensor_tensor(xs[:, 1, cols], m[:, 0:S], xs[:, 0, cols].bitcast(F32),
                                            ALU.subtract).then_inc(misc_dve, 1)
                elif name == "logits":
                    then(nc.vector.tensor_copy(rt_s[:, :, :], m[:, 0:64 * QT].rearrange("p (t e) -> p t e", t=QT)[:, :, 0:E_ALL]))
                    nc.vector.tensor_reduce(rt_neg[:, :], m[:, 0:64 * QT].rearrange("p (t e) -> p t e", t=QT)[:, :, 0:E_ALL],
                                            AX.X, ALU.max, negate=True).then_inc(misc_dve, 1)
                    dve.wait_ge(misc_dve, misc_reads(task))
                    nc.vector.memset(rt_zw[:, 1:2], 0.0).then_inc(neg_ready, 1)
                elif name == "route":
                    n = ln_index(1, b)
                    dve.wait_ge(act_exp_rt, b + 1)
                    then(nc.vector.reciprocal(rt_sum[:, :], rt_sum[:, :]))
                    then(nc.vector.tensor_tensor(rt_s[:, :, :], rt_e[:, :, :],
                                                 rt_sum[:, :].unsqueeze(2).to_broadcast([P, QT, E_ALL]), ALU.mult))
                    then(nc.vector.tensor_tensor(rt_sel[:, :, 0:E_ALL], rt_s[:, :, :],
                                                 rowb[:, ROW_EB:ROW_EB + E_ALL].unsqueeze(1).to_broadcast([P, QT, E_ALL]),
                                                 ALU.add))
                    for t in range(QT):
                        last = nc.vector.max(rt_top[:, t, :], rt_sel[:, t, :])
                    then(last)
                    then(nc.vector.tensor_copy(rt_rep[:, :, 0:TOP_K], rt_top[:, :, 0:TOP_K]))
                    for t in range(QT):
                        last = nc.vector.match_replace(rt_mr[:, t, :], rt_rep[:, t, :], rt_sel[:, t, :], TAKEN)
                    then(last)
                    then(nc.vector.scalar_tensor_tensor(rt_w[:, :, :], rt_mr[:, :, 0:E_ALL], TAKEN, rt_s[:, :, :],
                                                        ALU.is_equal, ALU.mult))
                    then(nc.vector.tensor_scalar(rt_w[:, :, :], rt_w[:, :, :], ROUTE_SCALE, None, ALU.mult))
                    then(nc.vector.tensor_reduce(rt_zw[:, :], rt_w[:, :, E_ROUTED:E_ALL], AX.X, ALU.add))
                    for t in range(QT):
                        nc.vector.scalar_tensor_tensor(acc[:, 2 * b + t, :], xn[:, n % 2, t, :], rt_zw[:, t:t + 1],
                                                       xres[:, b % 2, t, :], ALU.mult, ALU.add)
                    left = rt_w[:, :, 0:E_ROUTED]
                    for i in range(W_PARTS):
                        part = rt_ws[:, b % 2, :, E_ROUTED * i:E_ROUTED * (i + 1)]
                        then(nc.vector.tensor_copy(rt_b[:, :, :], left))
                        if i < W_PARTS - 1:
                            nc.vector.tensor_copy(part, rt_b[:, :, :])
                            then(nc.vector.tensor_tensor(rt_r[:, :, :], left, rt_b[:, :, :], ALU.subtract))
                            left = rt_r[:, :, :]
                        else:
                            nc.vector.tensor_copy(part, rt_b[:, :, :]).then_inc(routed, 1)
                elif name == "wT":
                    if b == 0:
                        dve.wait_ge(pool_consts, 1)
                    nc.vector.tensor_copy(wT[0:W_PARTS * E_ROUTED, S * b:S * (b + 1)], m[0:W_PARTS * E_ROUTED, 0:S]).then_inc(misc_dve, 1)
                elif name == "ohT":
                    nc.vector.tensor_copy(wT[0:W_PARTS * E_ROUTED, GT * b:GT * (b + 1)], m[0:W_PARTS * E_ROUTED, :]).then_inc(misc_dve, 1)
                elif name == "yT":
                    nc.vector.tensor_tensor(acc[:, 4 * b:4 * b + 4, :], acc[:, 4 * b:4 * b + 4, :],
                                            m.rearrange("p (t d) -> p t d", t=4), ALU.add).then_inc(misc_dve, 1)
                    dve.wait_ge(misc_dve, misc_reads(task))
                    norm_begin_group(lambda t: acc[:, 4 * b + t, :])
                elif name == "norm2":
                    dve.wait_ge(rstd_ready, ln_index(2, b) + 1)
                    for t in range(4):
                        last = nc.vector.tensor_scalar(xn[:, t // 2, t % 2, :], acc[:, 4 * b + t, :],
                                                       mv[:, t // 2, t % 2, 0:1], rstd[:, t // 2, t % 2:t % 2 + 1],
                                                       ALU.subtract, ALU.mult)
                    last.then_inc(normed, 1)
                    dve.wait_ge(normed, 2 * B + b + 1)
                    nc.vector.tensor_tensor(acc[:, 4 * b:4 * b + 4, :], acc[:, 4 * b:4 * b + 4, :],
                                            rowb[:, ROW_BO1:ROW_BO1 + D].unsqueeze(1).to_broadcast([P, 4, D]),
                                            ALU.add).then_inc(dve_self, 1)
                    own[0] += 1
                elif name in ("s1", "s1_"):
                    nc.vector.tensor_reduce(nm1[:, int(name == "s1_"), :], m.rearrange("p (t k) -> p t k", t=QT), AX.X,
                                            ALU.max, negate=True).then_inc(nm1_ready, 1)
                elif name == "oproj1":
                    dve.wait_ge(misc_act, misc_reads(("pv1", b)))
                    dve.wait_ge(dve_self, own[0])
                    then(nc.vector.reciprocal(sum1[:, :, :], sum1[:, :, :]))
                    for t in range(4):
                        last = nc.vector.scalar_tensor_tensor(
                            xres[:, t // 2, t % 2, :], m[:, D * t:D * (t + 1)], sum1[:, t // 2, t % 2:t % 2 + 1],
                            acc[:, 4 * b + t, :], ALU.mult, ALU.add)
                    last.then_inc(misc_dve, 1)
                    dve.wait_ge(misc_dve, misc_reads(task))
                    norm_begin_group(lambda t: xres[:, t // 2, t % 2, :])
                elif name == "norm3":
                    dve.wait_ge(rstd_ready, ln_index(3, b) + 1)
                    for t in range(4):
                        last = nc.vector.tensor_scalar(x4n[:, t // 2, t % 2, :], xres[:, t // 2, t % 2, :],
                                                       mv[:, t // 2, t % 2, 0:1], rms[:, 2, t // 2, t % 2:t % 2 + 1],
                                                       ALU.subtract, ALU.mult)
                    last.then_inc(x4_ready, 1)
                elif name == "xT4":
                    x32 = cls32[:, :, :].rearrange("p a q -> p (a q)")
                    nc.vector.tensor_scalar(x32, m, small_w("scale"), None, ALU.mult).then_inc(misc_dve, 1)
                    dve.wait_ge(misc_dve, misc_reads(task))
                    nc.vector.memset(rt_zw[:, 1:2], 0.0).then_inc(xf_ready, 1)
                    dve.wait_ge(xsq_done, b + 1)
                    nc.vector.tensor_tensor(xs[:, 1, GT * b:GT * (b + 1)], x32, xs[:, 0, GT * b:GT * (b + 1)].bitcast(F32),
                                            ALU.subtract).then_inc(xlo_ready, 1)
                elif name == "dist":
                    nc.vector.memset(d_oh[:, :, :, E_ROUTED:], 0.0)
                    then(nc.vector.tensor_copy(d_nd[:, :, 0:E1], m[:, 0:E1 * 4].rearrange("p (t e) -> p t e", t=4)))
                    for t in range(4):
                        last = nc.vector.max(d_top[:, t, :], d_nd[:, t, :])
                    then(last)
                    then(nc.vector.tensor_copy(d_rep[:, :, 0:1], d_top[:, :, 0:1]))
                    for t in range(4):
                        last = nc.vector.match_replace(d_mr[:, t, :], d_rep[:, t, :], d_nd[:, t, :], TAKEN)
                    then(last)
                    for t in range(4):
                        last = nc.vector.tensor_scalar(
                            d_oh[:, t // 2, t % 2, 0:E_ROUTED].rearrange("p (e r) -> p e r", r=4),
                            d_mr[:, t, 0:E1].unsqueeze(2).to_broadcast([P, E1, 4]), TAKEN, None, ALU.is_equal)
                    last.then_inc(misc_dve, 1)
                elif name == "final":
                    nc.vector.tensor_tensor(acc[:, 4 * b:4 * b + 4, :], acc[:, 4 * b:4 * b + 4, :],
                                            m.rearrange("p (t d) -> p t d", t=4), ALU.add).then_inc(misc_dve, 1)
                    dve.wait_ge(misc_dve, misc_reads(task))
                    nc.vector.memset(rt_zw[:, 1:2], 0.0).then_inc(fin_ready, 1)

            for s in range(SLOTS):
                if s < A_SLOTS:
                    b, j = s // PAIRS, s % PAIRS
                    if s == 0:
                        for task in slot_tasks(0):
                            if task[0] != "vproj":
                                misc_task(*task)
                        dve.wait_ge(in_rows, 16)
                        misc_task("vproj", 0)
                    dve.wait_ge(scores_max, s + 1)
                    bank = a_bank(s)
                    nc.vector.tensor_reduce(negmax[:, b % 2, :, :].rearrange("p t (r j) -> p r t j", r=2)[:, :, :, j],
                                            psum[:, bank:bank + 2, :].rearrange("p r (t k) -> p r t k", t=QT), AX.X,
                                            ALU.max, negate=True).then_inc(maxes_read, 1)
                if s > 0:
                    for name, b in slot_tasks(s):
                        if name == "xT":
                            norm_end(ln_index(0, b), x_in[:, QT * b:QT * (b + 1), :])
                        misc_task(name, b)
                if s == 2:
                    late_consts()

            for n in range(4 * UNITS):
                stage, g, u = n // (2 * UNITS), (n // UNITS) % 2, n % UNITS
                dve.wait_ge(silu_ready, n + 1)
                nc.vector.tensor_tensor(sg[:, n % 2, :], sg[:, n % 2, :], psum[:, 2 + n % 2, :],
                                        ALU.mult).then_inc(up_read, 1)
                dve.wait_ge(up_read, n + 1)
                dve.wait_ge(wb_done, n + 1)
                if n >= 2:
                    dve.wait_ge(lo_ready, n - 1)
                nc.vector.tensor_tensor(h32[:, n % 2, :], sg[:, n % 2, :], psum[:, 4, :],
                                        ALU.mult).then_inc(hidden_ready, 1)
                for name, b in unit_tasks(stage, g, u):
                    misc_task(name, b)
            misc_task("final", GROUPS - 1)

        @block.tensor
        def _(pe):
            uses = misc_uses()

            def claim(task):
                k = uses.index(task)
                if k >= 2:
                    prev = uses[k - 2]
                    pe.wait_ge(misc_dve if MISC_READER[prev[0]] == "dve" else misc_act, misc_reads(prev))
                return misc_bank(task)

            def mm(o, w, r, start=True, stop=True):
                return nc.tensor.matmul(o, w, r, start=start, stop=stop, skip_group_check=True)

            def split3(o, wh, wl, xh, xl, start, stop):
                mm(o, wh, xh, start, False)
                mm(o, wh, xl, False, False)
                return mm(o, wl, xh, False, stop)

            def misc_task(name, b):
                task = (name, b)
                if name not in MISC_READER:
                    return
                m = claim(task)
                last = None
                if name == "notfull":
                    pe.wait_ge(masks_ready, 1)
                    pe.wait_ge(pool_consts, 1)
                    for t in range(QT):
                        last = mm(m[:, P * t:P * (t + 1)], ones[:, :], iddiag[:, t, :])
                elif name == "k1proj":
                    last = mm(m, small_w("wk1"), ctxT[:, GT * b:GT * (b + 1)])
                elif name == "xT":
                    k = ln_index(0, b)
                    pe.wait_ge(normed, k + 1)
                    for t in range(QT):
                        last = nc.tensor.transpose(m[:, P * t:P * (t + 1)], xn[:, k % 2, t, :], id32[:, :])
                elif name == "qproj":
                    pe.wait_ge(misc_act, misc_reads(("xT", b)))
                    pe.wait_ge(in_qkw, 16)
                    mm(m[:, 0:S], small_w("wq"), xnT[:, b % 2, :])
                    last = mm(m[:, S:2 * S], small_w("wqr"), xnT[:, b % 2, :])
                elif name == "kproj":
                    pe.wait_ge(in_ctx0 if b == 0 else in_ctx, 16)
                    mm(m[:, 0:S], small_w("wk"), ctxT[:, S * b:S * (b + 1)])
                    last = mm(m[:, S:2 * S], small_w("wkr"), ctxT[:, S * b:S * (b + 1)])
                elif name == "vproj":
                    pe.wait_ge(in_small, 16)
                    for k in range(QT):
                        last = mm(m[:, D * k:D * (k + 1)], ctxT[:, S * b + P * k:S * b + P * (k + 1)], small_w("wv"))
                elif name == "maxT":
                    pe.wait_ge(maxes_read, PAIRS * (b + 1))
                    for t in range(QT):
                        last = nc.tensor.transpose(m[0:16, P * t:P * (t + 1)], negmax[:, b % 2, t, :], id32[:, :])
                elif name in ("ctx0", "ctx1"):
                    t = 0 if name == "ctx0" else 1
                    pe.wait_ge(pv_evicted, 2 * (b + 1))
                    for q in range(QUADS):
                        last = nc.tensor.transpose(m[:, P * q:P * (q + 1)], pvT[:, q, P * t:P * (t + 1)], id32[:, :])
                elif name == "ctxT":
                    pe.wait_ge(misc_dve, misc_reads(("ctx1", b)))
                    for t in range(QT):
                        last = nc.tensor.transpose(m[:, P * t:P * (t + 1)], ctxn[:, b % 2, t, :], id32[:, :])
                elif name == "oproj":
                    pe.wait_ge(misc_act, misc_reads(("ctxT", b)))
                    for t in range(QT):
                        last = mm(m[:, D * t:D * (t + 1)], ctxnT[:, b % 2, P * t:P * (t + 1)], small_w("wo"))
                elif name == "xT2":
                    k = ln_index(1, b)
                    pe.wait_ge(normed, k + 1)
                    for t in range(QT):
                        last = nc.tensor.transpose(m[:, P * t:P * (t + 1)], xn[:, k % 2, t, :], id32[:, :])
                elif name == "logits":
                    pe.wait_ge(misc_dve, misc_reads(("xT2", b)))
                    for t in range(QT):
                        last = mm(m[:, 64 * t:64 * t + E_ALL], cls32[:, b % 2, P * t:P * (t + 1)], small_w("cls"))
                elif name == "wT":
                    pe.wait_ge(routed, b + 1)
                    for t in range(QT):
                        last = nc.tensor.transpose(m[0:W_PARTS * E_ROUTED, P * t:P * (t + 1)], rt_ws[:, b % 2, t, :], id32[:, :])
                elif name in ("yT", "final"):
                    pe.wait_ge(y_evicted, (b + 1) if name == "yT" else GROUPS + b + 1)
                    for t in range(4):
                        last = nc.tensor.transpose(m[:, P * t:P * (t + 1)], yT[:, P * t:P * (t + 1)], id32[:, :])
                elif name == "xT3":
                    pe.wait_ge(normed, 2 * B + b + 1)
                    for t in range(4):
                        last = nc.tensor.transpose(m[:, P * t:P * (t + 1)], xn[:, t // 2, t % 2, :], id32[:, :])
                elif name == "q1":
                    pe.wait_ge(misc_act, misc_reads(("xT3", b)))
                    last = mm(m, small_w("wq1"), xT3[:, :, :].rearrange("p b q -> p (b q)"))
                elif name in ("s1", "s1_"):
                    k = int(name == "s1_")
                    pe.wait_ge(misc_act, misc_reads(("q1", b)))
                    pe.wait_ge(consts_ready, 1)
                    mm(m, ones16, padneg[0:1, 2 * b + k, :].unsqueeze(1).to_broadcast([1, QT, S]), True, False)
                    for t in range(QT):
                        last = mm(m[:, S * t:S * (t + 1)], q1T[:, k, P * t:P * (t + 1)], k1T[:, k, :], False, t == QT - 1)
                elif name in ("pT", "pT_"):
                    a = int(name == "pT_")
                    pe.wait_ge(misc_act, misc_reads(("s1_" if a else "s1", b)))
                    for k in range(QT):
                        for t in range(QT):
                            last = nc.tensor.transpose(m[:, S * k + P * t:S * k + P * (t + 1)],
                                                       sm1[:, a, t, P * k:P * (k + 1)], id32[:, :])
                elif name == "pv1":
                    pe.wait_ge(misc_act, misc_reads(("pT_", b)))
                    pe.wait_ge(in_late, 48)
                    for a in range(2):
                        for k in range(QT):
                            last = mm(m[:, S * a:S * (a + 1)], ctxk[:, QT * (2 * b + a) + k, :], pT1[:, a, k, :],
                                      k == 0, k == QT - 1)
                elif name == "oproj1":
                    pe.wait_ge(misc_act, misc_reads(("pv1", b)))
                    for t in range(4):
                        last = mm(m[:, D * t:D * (t + 1)], q1T[:, t // 2, P * (t % 2):P * (t % 2 + 1)], small_w("wo1"))
                elif name == "xT4":
                    pe.wait_ge(x4_ready, b + 1)
                    for t in range(4):
                        last = nc.tensor.transpose(m[:, P * t:P * (t + 1)], x4n[:, t // 2, t % 2, :], id32[:, :])
                elif name == "dist":
                    pe.wait_ge(xsq_done, b + 1)
                    pe.wait_ge(consts_ready, 1)
                    for t in range(4):
                        o = m[:, E1 * t:E1 * (t + 1)]
                        tok = slice(P * (t % 2), P * (t % 2 + 1))
                        mm(o, ones[:, :], c2[:, 1, :], t == 0, False)
                        mm(o, xsq[:, t // 2, tok], c2[:, 2, :], False, False)
                        last = mm(o, cls32[:, t // 2, tok], c2[:, 0, :], False, True)
                elif name == "ohT":
                    pe.wait_ge(misc_dve, misc_reads(("dist", b)))
                    for t in range(4):
                        last = nc.tensor.transpose(m[0:W_PARTS * E_ROUTED, P * t:P * (t + 1)], d_oh[:, t // 2, t % 2, :], id32[:, :])
                last.then_inc(misc_full, 1)

            misc_task("notfull", 0)
            for task in slot_tasks(0):
                misc_task(*task)
            for s in range(SLOTS):
                t = s - B_START
                has_a, has_b = s < A_SLOTS, 0 <= t < A_SLOTS
                a_b, a_j, b_b, b_j = s // PAIRS, s % PAIRS, t // PAIRS, t % PAIRS
                if has_a:
                    reads = s if s >= 1 and a_bank(s) == a_bank(s - 1) else s - 1
                    if reads >= 1:
                        pe.wait_ge(maxes_read, reads)
                    bank = a_bank(s)
                    for r in range(2):
                        mm(psum[:, bank + r, :], id16[:, :], maskb[:, 0, :, :].rearrange("p t k -> p (t k)"), True, False)
                    if a_j == 0:
                        pe.wait_ge(stack_in[a_b], 96)
                        if a_b < 3:
                            pe.wait_ge(ones_rows, 2 * (a_b + 1))
                    for q in range(QT):
                        for r in range(2):
                            rows_r = slice(64 * r, 64 * r + 32)
                            last = mm(psum[:, bank + r, S * q:S * (q + 1)], stacks[rows_r, 0, a_b % 3, a_j, P * q:P * (q + 1)],
                                      stacks[rows_r, 1, a_b % 3, a_j, :], False, q == QT - 1)
                    last.then_inc(scores_max, 1)
                if has_b:
                    if t == 0:
                        pe.wait_ge(maxes_read, B_START)
                    if t >= 1:
                        pe.wait_ge(exps_done, t)
                    for r in range(2):
                        mm(psum[:, 2 + r, :], id16[:, :], maskb[:, 1, :, :].rearrange("p k q -> p (k q)"), True, False)
                    if b_j == 0:
                        pe.wait_ge(maxrow_in[b_b], 32)
                    for k in range(QT):
                        for r in range(2):
                            rows_r = slice(64 * r, 64 * r + 33)
                            last = mm(psum[:, 2 + r, S * k:S * (k + 1)], stacks[rows_r, 1, b_b % 3, b_j, P * k:P * (k + 1)],
                                      stacks[rows_r, 0, b_b % 3, b_j, :], False, k == QT - 1)
                    last.then_inc(scores_exp, 1)
                if t >= 1:
                    p = t - 1
                    pb, quad, quarter = p // PAIRS, p // 2, p % 2
                    pe.wait_ge(exps_done, p + 1)
                    if p % PAIRS == 0:
                        pe.wait_ge(misc_dve, misc_reads(("vproj", pb)))
                    if p % 4 == 0 and p >= 8:
                        pe.wait_ge(pv_evicted, p // 4 - 1)
                    for k in range(QT):
                        for r in range(2):
                            g = 2 * quarter + r
                            h = 2 * (p % PAIRS) + r
                            last = mm(psum[32 * g:32 * (g + 1), BANK_PV + (quad // 2) % 2, S * (quad % 2):S * (quad % 2 + 1)],
                                      vaug[:, pb % 3, k, VW * h:VW * h + 32], probs[:, p % 4, r, k, :],
                                      k == 0, k == QT - 1)
                    last.then_inc(pv_done, 1)
                if s > 0:
                    for task in slot_tasks(s):
                        misc_task(*task)

            def down(n):
                stage, g, u = n // (2 * UNITS), (n // UNITS) % 2, n % UNITS
                w = ws0 if stage == 0 else ws1
                pe.wait_ge(hi_ready, n + 1)
                pe.wait_ge(lo_ready, n + 1)
                if n == 2 * UNITS + UNITS // 2:
                    pe.wait_ge(wsplit, 24)
                if u == 0 and n > 0:
                    pe.wait_ge(y_evicted, n // UNITS)
                if n == 0:
                    pe.wait_ge(pv_evicted, 2 * B)
                cols = slice(P * u, P * (u + 1))
                split3(psum[:, 5, :], w[:, 2, 0, cols], w[:, 2, 1, cols], hs(n)[:, 0, :], hs(n)[:, 1, :],
                       u == 0, u == UNITS - 1).then_inc(y_done, 1)

            for n in range(4 * UNITS):
                stage, g, u = n // (2 * UNITS), (n // UNITS) % 2, n % UNITS
                w = ws0 if stage == 0 else ws1
                toks = slice(GT * g, GT * (g + 1))
                if u == 0:
                    if stage == 0:
                        pe.wait_ge(misc_dve, misc_reads(("xT2", 2 * g + 1)))
                        pe.wait_ge(wsplit, 12)
                        pe.wait_ge(act_self, 1)
                        if g == 0:
                            pe.wait_ge(maxes_read, A_SLOTS)
                            pe.wait_ge(exps_done, A_SLOTS)
                    else:
                        pe.wait_ge(xlo_ready, g + 1)
                        pe.wait_ge(wsplit, 22)
                cols = slice(P * u, P * (u + 1))
                if n >= 2:
                    pe.wait_ge(up_read, n - 1)
                split3(psum[:, n % 2, :], w[:, 0, 0, cols], w[:, 0, 1, cols], xs[:, 0, toks], xs[:, 1, toks], True, True)
                split3(psum[:, 2 + n % 2, :], w[:, 1, 0, cols], w[:, 1, 1, cols], xs[:, 0, toks], xs[:, 1, toks],
                       True, True).then_inc(gates_done, 1)
                if u == 0:
                    pe.wait_ge(misc_dve, misc_reads(("wT", 2 * g + 1) if stage == 0 else ("ohT", g)))
                    if n == 0:
                        pe.wait_ge(pv_evicted, 2 * B - 1)
                if n >= 1:
                    pe.wait_ge(hidden_ready, n)
                mm(psum[:, 4, :], seln[:, u, :], wT[:, toks]).then_inc(wb_done, 1)
                if n >= DOWN_LAG:
                    down(n - DOWN_LAG)
                for task in unit_tasks(stage, g, u):
                    misc_task(*task)
            for n in range(4 * UNITS - DOWN_LAG, 4 * UNITS):
                down(n)
            misc_task("final", GROUPS - 1)


def rope_tables():
    inv = (1.0 / 10000.0 ** (np.arange(0, DK, 2, dtype=np.float32) / DK)).astype(np.float32)
    f = np.arange(S, dtype=np.float32)[None, :] * np.concatenate([inv, inv])[:, None]
    cos, sin = np.cos(f), np.sin(f)
    sign = np.array([-1.0] * (DK // 2) + [1.0] * (DK // 2), np.float32)[:, None]
    one = np.stack([cos / math.sqrt(DK), sign * sin / math.sqrt(DK), cos, sign * sin], axis=1)
    return np.tile(np.repeat(one, PAIRS, axis=0), (2, 1, 1)).astype(np.float32)


def selectors():
    m = np.zeros((P, UNITS, P), np.float32)
    for u in range(UNITS):
        for e in range(2):
            for i in range(W_PARTS):
                m[E_ROUTED * i + 2 * u + e, u, 64 * e:64 * (e + 1)] = 1.0
    return m.reshape(P, UNITS * P)


def kernel(x, ctx_1024, mask_1x1xSxS2_ik0, mask_BxS2_bk0, L0_xattn_w_q, L0_xattn_b_q, L0_xattn_w_k, L0_xattn_b_k,
           L0_xattn_w_v, L0_xattn_b_v, L0_xattn_w_o, L0_xattn_b_o, L0_ffn_classifier_weight,
           L0_ffn_e_score_correction_bias, L0_ffn_gate_up_proj, L0_ffn_down_proj, L1_xattn_Wq, L1_xattn_bq,
           L1_xattn_Wk, L1_xattn_bk, L1_xattn_Wo, L1_xattn_bo, L1_ffn_scale, L1_ffn_centroids, L1_ffn_up_w,
           L1_ffn_down_w):
    import concourse.bacc as bacc
    from concourse.bass_utils import run_bass_kernel_spmd as run

    a = np.asarray
    swap = np.concatenate([np.arange(1, DK, 2), np.arange(0, DK, 2)])
    heads = DK * np.arange(H0).reshape(PAIRS, 2).T
    plain = (heads[:, None, :] + np.arange(DK)[None, :, None]).reshape(-1)
    turned = (heads[:, None, :] + swap[None, :, None]).reshape(-1)
    wq, wk, bq, bk = a(L0_xattn_w_q), a(L0_xattn_w_k), a(L0_xattn_b_q), a(L0_xattn_b_k)
    small = np.concatenate([
        bq[plain][:, None], bq[turned][:, None], bk[plain][:, None], bk[turned][:, None], wq[plain].T, wq[turned].T,
        wk[plain].T, wk[turned].T, a(L0_xattn_w_v).T, a(L0_xattn_w_o).T, a(L1_xattn_Wq).T, a(L1_xattn_Wk).T,
        a(L1_xattn_Wo).T, a(L0_ffn_classifier_weight).T, a(L1_ffn_centroids).T, a(L1_xattn_bq)[:, None],
        a(L1_xattn_bk)[:, None], a(L1_ffn_scale)[:, None]], axis=1)
    rows = np.concatenate([a(L0_xattn_b_v), a(L0_xattn_b_o), a(L1_xattn_bo), a(L0_ffn_e_score_correction_bias)])[None]
    gu = a(L0_ffn_gate_up_proj)[:E_ROUTED].reshape(E_ROUTED, 2, 64, D)
    up1 = a(L1_ffn_up_w).reshape(E1, D, 2, CHUNK // E1)
    experts = np.stack([
        gu[:, 0].transpose(2, 0, 1).reshape(D, CHUNK),
        gu[:, 1].transpose(2, 0, 1).reshape(D, CHUNK),
        a(L0_ffn_down_proj).transpose(0, 2, 1).reshape(UNITS, P, D).transpose(1, 0, 2).reshape(P, CHUNK),
        up1[:, :, 1].transpose(1, 0, 2).reshape(D, CHUNK),
        up1[:, :, 0].transpose(1, 0, 2).reshape(D, CHUNK),
        a(L1_ffn_down_w).reshape(UNITS, P, D).transpose(1, 0, 2).reshape(P, CHUNK)], axis=1)
    mask = a(mask_1x1xSxS2_ik0)[0, 0]
    arrays = {
        "x": a(x).reshape(T, D), "ctx_t": a(ctx_1024).reshape(T, D).T, "ctx_tok": a(ctx_1024).reshape(T, D),
        "mask_q": mask.reshape(QT, P, S).transpose(1, 0, 2), "mask_k": mask.T.reshape(QT, P, S).transpose(1, 0, 2),
        "pad": a(mask_BxS2_bk0).reshape(1, T), "small": small, "rows": rows, "experts": experts,
        "ident": np.eye(P, dtype=np.float32), "rope": rope_tables(), "sel": selectors()}
    arrays = {k: np.ascontiguousarray(v) for k, v in arrays.items()}
    nc = bacc.Bacc("TRN2", target_bir_lowering=False, num_devices=1)
    aps = [nc.dram_tensor(k, v.shape, mybir.dt.from_np(v.dtype), kind="ExternalInput").ap() for k, v in arrays.items()]
    out = nc.dram_tensor("out", (T, D), F32, kind="ExternalOutput").ap()
    build(nc, *aps, out)
    result = run(nc, [arrays], core_ids=[0])
    return result.results[0]["out"].reshape(B, S, D)
```

```python
import math
from contextlib import ExitStack

import numpy as np

import concourse.bass as bass
from concourse import mybir

F32 = mybir.dt.float32
F32R = mybir.dt.float32r
BF16 = mybir.dt.bfloat16
I32 = mybir.dt.int32
U8 = mybir.dt.uint8
ALU = mybir.AluOpType
ACT = mybir.ActivationFunctionType
AX = mybir.AxisListType

P = 128
B, S, D = 4, 256, 128
T = B * S
TILES = T // P
QT = S // P
H0, DK = 16, 8
PAIRS = H0 // 2
QUADS = H0 // 4
VW = DK + 1
E_ROUTED, E_ZERO, TOP_K, ROUTE_SCALE = 32, 8, 6, 2.5
E_ALL = E_ROUTED + E_ZERO
E1 = 8
UNITS = 16
CHUNK = UNITS * P
GROUPS, GT = 2, 512
MASKED = -float(2 ** 30)
W_PARTS = 3
NEG = -3.0e38
TAKEN = 3.0e38
LN_EPS, RMS_EPS = 1e-5, 1e-6
LAG = 3
A_SLOTS = B * PAIRS
B_START = PAIRS + LAG
SLOTS = A_SLOTS + B_START + 1
DOWN_LAG = 3
LOW_ON_DVE = 4 * UNITS - 1

SM = {}
_at = 0
for _name, _n in (("bq", 1), ("bqr", 1), ("bk", 1), ("bkr", 1), ("wq", D), ("wqr", D), ("wk", D), ("wkr", D),
                  ("wv", D), ("wo", D), ("wq1", D), ("wk1", D), ("wo1", D), ("cls", E_ALL), ("cent", E1),
                  ("bq1", 1), ("bk1", 1), ("scale", 1)):
    SM[_name] = (_at, _at + _n)
    _at += _n
SMALL = _at
SMALL_QK = SM["wv"][0]
ROW_BV, ROW_BO, ROW_BO1, ROW_EB = 0, D, 2 * D, 3 * D
ROWS = 3 * D + E_ALL


def misc_uses():
    uses = []
    for s in range(SLOTS):
        uses += [t for t in slot_tasks(s) if t[0] in MISC_READER]
    for stage in (0, 1):
        for g in range(GROUPS):
            for u in range(UNITS):
                uses += [t for t in unit_tasks(stage, g, u) if t[0] in MISC_READER]
    uses += [("final", GROUPS - 1)]
    return uses


MISC_READER = {
    "xT": "act", "qproj": "dve", "kproj": "dve", "vproj": "dve", "maxT": "dve", "ctx0": "dve",
    "ctx1": "dve", "ctxT": "act", "oproj": "dve", "xT2": "dve", "logits": "dve", "wT": "dve", "yT": "dve",
    "k1proj": "act", "xT3": "act", "q1": "act", "s1": "act", "s1_": "act", "pT": "act", "pT_": "act", "pv1": "act",
    "oproj1": "dve", "xT4": "dve", "dist": "dve", "ohT": "dve", "final": "dve",
}
PREP = {"norm0": 8, "kproj": 9, "xT": 9, "qproj": 10, "vproj": 12}
TAIL = {"ctx0": 0, "ctx1": 0, "ctxT": 1, "oproj": 2, "norm": 4, "xT2": 5, "logits": 6, "route": 7, "route1": 8,
        "route2": 9, "part0": 9, "part1": 10, "part2": 11, "wT": 13}
SECOND = {"yT": 3, "norm2": 4, "k1proj": 4, "xT3": 5, "q1": 6, "s1": 7, "s1_": 7, "pT": 8, "pT_": 8, "pv1": 9,
          "oproj1": 10, "norm3": 11, "skip": 12, "xT4": 12, "dist": 13, "ohT": 14}


def slot_tasks(s):
    tasks = []
    if s == 0:
        return [("kproj", 0), ("xT", 0), ("qproj", 0), ("kproj", 1), ("xT", 1), ("qproj", 1), ("vproj", 0)]
    if s == PAIRS - 1:
        tasks.append(("vproj", 1))
    for b in range(B):
        for name, at in PREP.items():
            if b > 1 and s == PAIRS * (b - 2) + at:
                tasks.append((name, b))
        if s == PAIRS * (b + 1) - 1:
            tasks.insert(0, ("maxT", b))
        tasks += tail_tasks(s, b)
    return tasks


def tail_tasks(s, b):
    return [(name, b) for name, at in TAIL.items() if s == PAIRS * b + B_START + PAIRS + 1 + at]


def unit_tasks(stage, g, u):
    tasks = []
    if stage == 0 and g == 0:
        for b in range(B):
            tasks += tail_tasks(SLOTS + u, b)
    if (stage, g) in ((0, 1), (1, 0)):
        tasks += [(name, g ^ 1) for name, at in SECOND.items() if u == at]
    if stage == 1 and g == 1 and u == SECOND["yT"]:
        tasks.append(("final", 0))
    return tasks


def misc_index(task):
    return misc_uses().index(task)


def misc_reads(task):
    uses = misc_uses()
    k = uses.index(task)
    return sum(1 for t in uses[:k + 1] if MISC_READER[t[0]] == MISC_READER[task[0]])


def build(nc, x, ctx_t, ctx_tok, mask_q, mask_k, pad, small, rows, experts, ident, rope, sel, out):
    with ExitStack() as ctx:
        def sb(name, shape, dt=F32):
            return ctx.enter_context(nc.sbuf_tensor(name, shape, dt))

        def sem(name):
            return ctx.enter_context(nc.semaphore(name))

        psum = ctx.enter_context(nc.psum_tensor("psum", [P, 8, 512], F32))
        qk_scratch = nc.dram_tensor("qk_scratch", [B, 2, 2, 2, DK * PAIRS, S], F32, kind="Internal").ap()

        x_in = sb("x_in", [P, TILES, D])
        acc = x_in
        xn = sb("xn", [P, 2, QT, D])
        xres = sb("xres", [P, 2, QT, D])
        stats = sb("stats", [P, 2, QT, 6])
        mv = sb("mv", [P, 2, QT, 2])
        rstd = sb("rstd", [P, 2, QT])
        veps = sb("veps", [P, 2, QT])
        rms = sb("rms", [P, 3, 2, QT])
        half = sb("half", [P, 2, QT])
        id32 = sb("id32", [P, P])
        id16 = sb("id16", [P, P], BF16)
        sm = sb("sm", [P, SMALL])
        rowb = sb("rowb", [P, ROWS])
        ropet = sb("ropet", [P, 4, S])
        maskb = sb("maskb", [P, 2, QT, S], BF16)
        allmasked = sb("allmasked", [P, QT])
        iddiag = sb("iddiag", [P, QT, P])
        ones16 = iddiag[0:1, 0, 0:P // 2].bitcast(BF16)
        ones = sb("ones", [P, P])
        padneg = sb("padneg", [P, B, S], BF16)
        seln = sb("seln", [P, UNITS, P], BF16)
        ctxT = sb("ctxT", [P, T])
        ctxk = sb("ctxk", [P, TILES, D])
        xnT = sb("xnT", [P, 2, S])
        early = sb("early", [P, 6144])
        probs = early[:, 0:4096].rearrange("p (n r k q) -> p n r k q", n=4, r=2, k=QT)
        rot = early[:, 4096:6144].rearrange("p (n t i q) -> p n t i q", n=2, t=2, i=2)
        qk = sb("qk", [P, 2, S])
        parts = sb("parts", [P, 2048], F32R)
        qks = parts[:, :].rearrange("p (n t l q) -> p n t l q", n=2, t=2, l=2)
        big = sb("big", [P, 6 * CHUNK], F32R)
        stacks = big[:, :].rearrange("p (t b j q) -> p t b j q", t=2, b=3, j=PAIRS)
        vaug = sb("vaug", [P, 3, QT, VW * H0 + 32 - VW])
        vheads = vaug[:, :, :, 0:VW * H0].rearrange("p b k (h c) -> p b k h c", c=VW)
        negmax = sb("negmax", [P, 2, QT, 16])
        maxrow = sb("maxrow", [16, 2, S], F32R)
        pvT = sb("pvT", [P, QUADS, S])
        maskq_i = pvT[:, :, :].bitcast(I32).rearrange("p (m t) k -> p m t k", m=2)
        rden = sb("rden", [P, 2, H0])
        ctxn = sb("ctxn", [P, 2, QT, D])
        pad8 = ctxn[:, 0, :, :].rearrange("p t d -> p (t d)").bitcast(U8)
        ctxnT = sb("ctxnT", [P, 2, S])
        rt_neg = sb("rt_neg", [P, QT])
        rt_sum = sb("rt_sum", [P, QT])
        rt_e = sb("rt_e", [P, QT, E_ALL])
        rt_s = sb("rt_s", [P, QT, E_ALL])
        rt_sel = sb("rt_sel", [P, QT, E_ALL + 8])
        rt_top = sb("rt_top", [P, QT, 8])
        rt_rep = sb("rt_rep", [P, QT, 8])
        rt_mr = sb("rt_mr", [P, QT, E_ALL + 8])
        rt_w = sb("rt_w", [P, QT, E_ALL])
        rt_ws = sb("rt_ws", [P, 2, QT, W_PARTS * E_ROUTED])
        rt_b = sb("rt_b", [P, QT, E_ROUTED], BF16)
        rt_r = sb("rt_r", [P, QT, E_ROUTED])
        rt_zw = sb("rt_zw", [P, QT])
        cls32 = xnT
        wT = sb("wT", [P, T], BF16)
        raw = sb("raw", [P, 2, CHUNK // 2])
        ws0 = sb("ws0", [P, 3, 2, CHUNK], F32R)
        ws1 = big[:, :].rearrange("p (c h n) -> p c h n", c=3, h=2)
        xs = sb("xs", [P, 2, T], F32R)
        sg = early[:, 0:1024].rearrange("p (n t) -> p n t", n=2)
        h32 = early[:, 1024:2048].rearrange("p (n t) -> p n t", n=2)
        yT = early[:, 2048:2560]
        k1T = sb("k1T", [P, 2, S])
        xT3 = early[:, 2560:3072].rearrange("p (n q) -> p n q", n=2)
        q1T = early[:, 3072:3584].rearrange("p (n q) -> p n q", n=2)
        sm1 = early[:, 3584:4608].rearrange("p (n t k) -> p n t k", n=2, t=QT)
        pT1 = early[:, 4608:5632].rearrange("p (n k q) -> p n k q", n=2, k=QT)
        nm1 = sb("nm1", [P, 2, QT])
        sum1 = sb("sum1", [P, 2, QT])
        x4n = ctxn
        xsq = qk
        c2 = sb("c2", [P, 3, E1])
        d_nd = sb("d_nd", [P, GT // P, 16])
        d_top = sb("d_top", [P, GT // P, 8])
        d_rep = sb("d_rep", [P, GT // P, 8])
        d_mr = rt_mr[:, :, :].rearrange("p t e -> p (t e)")[:, 0:GT // P * 16].rearrange("p (t c) -> p t c", c=16)
        d_oh = rt_ws

        in_x, in_x1, in_xrest, in_ctx0, in_ctx, in_qkw, in_small, in_ident, in_rope, in_ropek, in_mask, in_rows, in_pad, in_late = (
            sem(n) for n in ("in_x", "in_x1", "in_xrest", "in_ctx0", "in_ctx", "in_qkw", "in_small", "in_ident", "in_rope", "in_ropek",
                             "in_mask", "in_rows", "in_pad", "in_late"))
        ones_rows = sem("ones_rows")
        in_raw = [sem(f"in_raw{i}") for i in range(12)]
        scratch_k = [sem(f"scratch_k{b}") for b in range(B)]
        scratch_q = [sem(f"scratch_q{b}") for b in range(B)]
        stack_in = [sem(f"stack_in{b}") for b in range(B)]
        maxrow_in = [sem(f"maxrow_in{b}") for b in range(B)]
        out_done = sem("out_done")
        dve_self, pool_self, act_self = sem("dve_self"), sem("pool_self"), sem("act_self")
        misc_full, misc_dve, misc_act = sem("misc_full"), sem("misc_dve"), sem("misc_act")
        consts_ready, masks_ready, norm_stats, normed = (sem(n) for n in ("consts_ready", "masks_ready", "norm_stats", "normed"))
        maxes_read = sem("maxes_read")
        hidden_ready, up_read, nm1_ready, dve_consts, qk_ready, xlo_ready, routed, x4_ready = (
            sem(n) for n in ("hidden_ready", "up_read", "nm1_ready", "dve_consts", "qk_ready", "xlo_ready",
                             "routed", "x4_ready"))
        last_lo_ready, csum_done = sem("last_lo_ready"), sem("csum_done")
        rw_ready, skip_normed, rms_ready, shift_ready = (
            sem(n) for n in ("rw_ready", "skip_normed", "rms_ready", "shift_ready"))
        rstd_ready, qks_ready, pool_consts, wsplit, lo_ready, acc4_ready = (
            sem(n) for n in ("rstd_ready", "qks_ready", "pool_consts", "wsplit", "lo_ready", "acc4_ready"))
        exps_done, pv_evicted, act_exp_rt, silu_ready, hi_ready, y_evicted, whi_ready, xsq_done, qhi_ready = (
            sem(n) for n in ("exps_done", "pv_evicted", "act_exp_rt", "silu_ready", "hi_ready", "y_evicted",
                             "whi_ready", "xsq_done", "qhi_ready"))
        notfull_done, scores_max, scores_exp, pv_done, gates_done, wb_done, y_done = (
            sem(n) for n in ("notfull_done", "scores_max", "scores_exp", "pv_done", "gates_done", "wb_done", "y_done"))

        def hs(n):
            if n % 4 < 2:
                room = parts[:, 1024 * (n % 4):1024 * (n % 4 + 1)]
            elif n < 2 * UNITS:
                room = ws1[:, 2, n % 4 - 2, CHUNK // 2:CHUNK]
            else:
                room = ws0[:, 0, n % 4 - 2, 0:CHUNK // 2]
            return room.rearrange("p (l t) -> p l t", l=2)

        def small_w(name):
            return sm[:, SM[name][0]:SM[name][1]]

        def misc_bank(task):
            return psum[:, 6 + misc_index(task) % 2, :]

        BANK_PV = 4
        BANK_NOTFULL = 5

        def b_bank(t):
            return 0 if t + B_START >= A_SLOTS and t % 2 == 1 else 2

        def a_bank(s):
            return 2 if s < B_START and s % 2 == 1 else 0

        def ln_index(kind, b):
            return LN_ORDER.index((kind, b))

        block = ctx.enter_context(nc.Block())

        LN_ORDER = [(0, 0), (0, 1)]
        for s in range(SLOTS):
            for name, b in slot_tasks(s):
                if name == "vproj" and 2 <= b + 1 < B:
                    LN_ORDER.append((0, b + 1))
                if name == "oproj":
                    LN_ORDER.append((1, b))
        for u in range(UNITS):
            for name, b in unit_tasks(0, 0, u):
                if name == "oproj":
                    LN_ORDER.append((1, b))
        for g in range(GROUPS):
            LN_ORDER += [(2, g), (3, g)]

        @block.sync
        def _(sp):
            def x_batches(lo, hi, signal):
                sp.dma_start(x_in[:, QT * lo:QT * hi, :],
                             x[S * lo:S * hi, :].rearrange("(t p) d -> p t d", p=P)).then_inc(signal, 16)

            x_batches(0, 1, in_x)
            sp.dma_start(id32[:, :], ident).then_inc(in_ident, 16)
            sp.dma_start(sm[:, 0:SMALL_QK], small[:, 0:SMALL_QK]).then_inc(in_qkw, 16)
            sp.dma_start(ctxT[:, 0:S], ctx_t[:, 0:S]).then_inc(in_ctx0, 16)
            sp.dma_start(ropet[:, 2:4, :], rope[:, 2:4, :]).then_inc(in_ropek, 16)
            sp.dma_start(maskq_i[:, 0, :, :], mask_q).then_inc(in_mask, 16)
            sp.dma_start(maskq_i[:, 1, :, :], mask_k).then_inc(in_mask, 16)
            sp.dma_start(ropet[:, 0:2, :], rope[:, 0:2, :]).then_inc(in_rope, 16)
            x_batches(1, 2, in_x1)
            sp.dma_start(ctxT[:, S:T], ctx_t[:, S:T]).then_inc(in_ctx, 16)
            sp.dma_start(sm[:, SMALL_QK:SMALL], small[:, SMALL_QK:SMALL]).then_inc(in_small, 16)
            sp.dma_start(rowb[:, :], rows.to_broadcast([P, ROWS])).then_inc(in_rows, 16)

            def late_loads():
                x_batches(2, B, in_xrest)
                sp.dma_start(sg[:, :, :], sel[:, 0:1024]).then_inc(in_late, 16)
                sp.dma_start(h32[:, :, :], sel[:, 1024:2048]).then_inc(in_late, 16)
                sp.dma_start(pad8, pad.to_broadcast([P, T])).then_inc(in_pad, 16)
                sp.dma_start(ctxk[:, :, :], ctx_tok.rearrange("(t p) d -> p t d", p=P)).then_inc(in_late, 16)

            def stack_batch(b):
                def write(t, written):
                    for r in range(2):
                        sp.dma_start(qk_scratch[b, r, t].rearrange("l c q -> c l q"),
                                     qks[64 * r:64 * (r + 1), b % 2, t, :, :].bitcast(F32)).then_inc(written, 16)

                def read(t, r, k):
                    src = qk_scratch[b, r, t].rearrange("l (d j) q -> l d (j q)", j=PAIRS)
                    dst = stacks[64 * r:64 * r + 32, t, b % 3, :, :].bitcast(F32).rearrange("c j q -> c (j q)")
                    if t == 1:
                        dst, src = dst[16 * k:16 * (k + 1), :], src[k]
                    shape = [2] + list(src.shape)
                    sp.dma_start(dst, src.unsqueeze(0).to_broadcast(shape)).then_inc(stack_in[b], 16)

                sp.wait_ge(qks_ready, 2 * b + 1)
                write(1, scratch_k[b])
                sp.wait_ge(scratch_k[b], 32)
                if b >= 3:
                    sp.wait_ge(scores_exp, PAIRS * (b - 2))
                read(1, 0, 0)
                sp.wait_ge(qks_ready, 2 * b + 2)
                write(0, scratch_q[b])
                read(1, 0, 1)
                read(1, 1, 0)
                read(1, 1, 1)
                sp.wait_ge(scratch_q[b], 32)
                for r in range(2):
                    read(0, r, 0)

            def maxrow_batch(b):
                sp.wait_ge(misc_dve, misc_reads(("maxT", b)))
                for r in range(2):
                    sp.dma_start(stacks[64 * r + 32:64 * r + 33, 0, b % 3, :, :].bitcast(F32),
                                 maxrow[PAIRS * r:PAIRS * (r + 1), b % 2, :].bitcast(F32)).then_inc(maxrow_in[b], 16)

            for s in range(SLOTS):
                for name, b in slot_tasks(s):
                    if name == "kproj":
                        stack_batch(b)
                        if b == 1:
                            late_loads()
                    if name == "maxT":
                        maxrow_batch(b)
            for g in range(GROUPS):
                sp.wait_ge(misc_dve, misc_reads(("final", g)))
                sp.dma_start(out[GT * g:GT * (g + 1), :].rearrange("(t p) d -> p t d", p=P),
                             acc[:, 4 * g:4 * g + 4, :]).then_inc(out_done, 16)
            sp.wait_ge(out_done, 16 * GROUPS)

        @block.gpsimd
        def _(pool):
            own = [0]

            def then(ins):
                own[0] += 1
                ins.then_inc(pool_self, 1)
                pool.wait_ge(pool_self, own[0])

            nc.gpsimd.memset(half[:, :, :], -0.5)
            nc.gpsimd.memset(ones[:, :], 1.0)
            nc.gpsimd.memset(wT[:, :], 0.0).then_inc(pool_consts, 1)
            pool.wait_ge(pool_consts, 1)

            def ones_beside_keys(buffer):
                for r in range(2):
                    nc.gpsimd.memset(stacks[64 * r + 32:64 * r + 33, 1, buffer, :, :].bitcast(F32), 1.0).then_inc(ones_rows, 1)
                pool.wait_ge(ones_rows, 2 * (buffer + 1))

            ones_beside_keys(0)

            def inv_sqrt(n, at):
                pool.wait_ge(norm_stats, n + 1)
                then(nc.gpsimd.tensor_scalar_add(veps[:, at, :], mv[:, at, :, 1], LN_EPS))
                nc.gpsimd.tensor_tensor(rstd[:, at, :], veps[:, at, :], half[:, 0, :], ALU.pow).then_inc(rstd_ready, 1)

            def inv_sqrt_group(n):
                pool.wait_ge(norm_stats, n + 1)
                then(nc.gpsimd.tensor_scalar_add(veps[:, :, :], mv[:, :, :, 1], LN_EPS))
                nc.gpsimd.tensor_tensor(rstd[:, :, :], veps[:, :, :], half[:, :, :], ALU.pow).then_inc(rstd_ready, 1)

            def rms_factor(b):
                pool.wait_ge(norm_stats, ln_index(3, b) + 1)
                then(nc.gpsimd.tensor_scalar(rms[:, 0, :, :], mv[:, :, :, 1], 1.0 + RMS_EPS, LN_EPS * RMS_EPS, ALU.mult, ALU.add))
                nc.gpsimd.tensor_tensor(rms[:, 1, :, :], rms[:, 0, :, :], half[:, :, :], ALU.pow).then_inc(rms_ready, 1)

            def skip_shift(b):
                pool.wait_ge(rstd_ready, ln_index(3, b) + 1)
                then(nc.gpsimd.tensor_scalar(rms[:, 2, :, :], mv[:, :, :, 0], -1.0, None, ALU.mult))
                nc.gpsimd.tensor_tensor(rms[:, 2, :, :], rms[:, 2, :, :], rstd[:, :, :], ALU.mult).then_inc(shift_ready, 1)

            def split_qk(b, t):
                pool.wait_ge(qhi_ready, 2 * b + 2 - t)
                nc.gpsimd.tensor_tensor(qks[:, b % 2, t, 1, :], qk[:, t, :], qks[:, b % 2, t, 0, :].bitcast(F32),
                                        ALU.subtract).then_inc(qks_ready, 1)

            def split_routing(b, i):
                pool.wait_ge(rw_ready, b + 1)
                left = rt_w[:, :, 0:E_ROUTED] if i == 0 else rt_r[:, :, :]
                part = rt_ws[:, b % 2, :, E_ROUTED * i:E_ROUTED * (i + 1)]
                then(nc.gpsimd.tensor_copy(rt_b[:, :, :], left))
                if i < W_PARTS - 1:
                    then(nc.gpsimd.tensor_copy(part, rt_b[:, :, :]))
                    then(nc.gpsimd.tensor_tensor(rt_r[:, :, :], left, part, ALU.subtract))
                else:
                    nc.gpsimd.tensor_copy(part, rt_b[:, :, :]).then_inc(routed, 1)

            def split_weights(i):
                c, q = i // 4, i % 4
                pool.wait_ge(whi_ready, i + 1)
                ws = (ws0 if c < 3 else ws1)[:, c % 3, :, 512 * q:512 * (q + 1)]
                src = raw[:, (i // 2) % 2, 512 * (q % 2):512 * (q % 2 + 1)]
                nc.gpsimd.tensor_tensor(ws[:, 1, :], src, ws[:, 0, :].bitcast(F32), ALU.subtract).then_inc(wsplit, 1)

            inv_sqrt(0, 0)
            wi = 0
            for s in range(SLOTS):
                if s in (1, 2):
                    pool.wait_ge(qks_ready, 4)
                    ones_beside_keys(s)
                for name, b in slot_tasks(s):
                    if name in ("qproj", "kproj"):
                        split_qk(b, int(name == "kproj"))
                    if (name, b) == ("qproj", 0):
                        inv_sqrt(1, 1)
                    if name == "vproj" and 2 <= b + 1 < B:
                        inv_sqrt(ln_index(0, b + 1), ln_index(0, b + 1) % 2)
                    if name == "oproj":
                        inv_sqrt(ln_index(1, b), ln_index(1, b) % 2)
                    if name in ("part0", "part1", "part2"):
                        split_routing(b, int(name[-1]))
                if s % 3 == 2 and s > 2 and wi < 12:
                    split_weights(wi)
                    wi += 1

            n_unit = 0
            for stage in (0, 1):
                for g in range(GROUPS):
                    for u in range(UNITS):
                        n = n_unit
                        for name, b in unit_tasks(stage, g, u):
                            if name == "oproj":
                                inv_sqrt(ln_index(1, b), ln_index(1, b) % 2)
                            if name in ("part0", "part1", "part2"):
                                split_routing(b, int(name[-1]))
                            if name == "yT":
                                inv_sqrt_group(ln_index(2, b))
                            if name == "oproj1":
                                rms_factor(b)
                            if name == "skip":
                                inv_sqrt_group(ln_index(3, b))
                                skip_shift(b)
                            if name == "ohT":
                                pool.wait_ge(skip_normed, 2 * (b + 1))
                                nc.gpsimd.tensor_tensor(acc[:, 4 * b:4 * b + 4, :],
                                                        xres[:, :, :, :].rearrange("p a t d -> p (a t) d"),
                                                        xn[:, :, :, :].rearrange("p a t d -> p (a t) d"),
                                                        ALU.add).then_inc(acc4_ready, 1)
                        if n >= LOW_ON_DVE:
                            break
                        pool.wait_ge(hi_ready, n + 1)
                        nc.gpsimd.tensor_tensor(hs(n)[:, 1, :], h32[:, n % 2, :], hs(n)[:, 0, :].bitcast(F32),
                                                ALU.subtract).then_inc(lo_ready, 1)
                        if wi < 24 and n % 3 == 1 and (wi < 22 or n > 2 * UNITS + DOWN_LAG):
                            split_weights(wi)
                            wi += 1
                        n_unit += 1

        @block.scalar
        def _(act):
            def unpack_selectors():
                act.wait_ge(in_late, 48)
                nc.scalar.copy(seln[:, 0:8, :], sg[:, :, :].rearrange("p a (b n) -> p (a b) n", n=P))
                nc.scalar.copy(seln[:, 8:16, :], h32[:, :, :].rearrange("p a (b n) -> p (a b) n", n=P)).then_inc(act_self, 1)
                act.wait_ge(act_self, 1)

            def split_weights(i):
                c, q = i // 4, i % 4
                if q % 2 == 0:
                    act.wait_ge(in_raw[i // 2], 16)
                if q % 2 == 0 and 2 <= i < 22:
                    act.wait_ge(wsplit, i)
                    k = i // 2 + 1
                    nc.scalar.dma_start(raw[:, k % 2, :],
                                        experts[:, k // 2, 1024 * (k % 2):1024 * (k % 2 + 1)]).then_inc(in_raw[k], 16)
                if i == 12:
                    act.wait_ge(scores_exp, A_SLOTS)
                if i == 22:
                    act.wait_ge(y_done, 2 * UNITS)
                ws = (ws0 if c < 3 else ws1)[:, c % 3, :, 512 * q:512 * (q + 1)]
                src = raw[:, (i // 2) % 2, 512 * (q % 2):512 * (q % 2 + 1)]
                nc.scalar.copy(ws[:, 0, :], src).then_inc(whi_ready, 1)

            def evict(task, dst, src, bias=None):
                act.wait_ge(misc_full, misc_index(task) + 1)
                if bias is None:
                    nc.scalar.copy(dst, src).then_inc(misc_act, 1)
                else:
                    nc.scalar.activation(dst, src, ACT.Identity, bias=bias).then_inc(misc_act, 1)

            def misc_task(name, b):
                task = (name, b)
                m = misc_bank(task) if name in MISC_READER else None
                if name == "xT":
                    evict(task, xnT[:, b % 2, :], m[:, 0:S])
                elif name in ("qproj", "kproj"):
                    t = int(name == "kproj")
                    act.wait_ge(qk_ready, 2 * b + 2 - t)
                    if b >= 2:
                        act.wait_ge((scratch_k if t else scratch_q)[b - 2], 32)
                    nc.scalar.copy(qks[:, b % 2, t, 0, :], qk[:, t, :]).then_inc(qhi_ready, 1)
                elif name == "ctxT":
                    evict(task, ctxnT[:, b % 2, :], m[:, 0:S])
                elif name == "logits":
                    act.wait_ge(misc_dve, misc_reads(task))
                    for t in range(QT):
                        last = nc.scalar.activation(rt_e[:, t, :], rt_s[:, t, :], ACT.Exp,
                                                    bias=rt_neg[:, t:t + 1], accum_out=rt_sum[:, t:t + 1])
                    last.then_inc(act_exp_rt, 1)
                elif name == "k1proj":
                    evict(task, k1T[:, :, :].rearrange("p b k -> p (b k)"), m, small_w("bk1"))
                elif name == "xT3":
                    evict(task, xT3[:, :, :].rearrange("p b q -> p (b q)"), m)
                elif name == "q1":
                    evict(task, q1T[:, :, :].rearrange("p b q -> p (b q)"), m, small_w("bq1"))
                elif name in ("s1", "s1_"):
                    k = int(name == "s1_")
                    act.wait_ge(nm1_ready, 2 * b + k + 1)
                    for t in range(QT):
                        last = nc.scalar.activation(sm1[:, k, t, :], m[:, S * t:S * (t + 1)], ACT.Exp,
                                                    bias=nm1[:, k, t:t + 1], accum_out=sum1[:, k, t:t + 1])
                    last.then_inc(misc_act, 1)
                elif name in ("pT", "pT_"):
                    evict(task, pT1[:, int(name == "pT_"), :, :], m.rearrange("p (k q) -> p k q", k=QT))
                elif name == "pv1":
                    evict(task, q1T[:, :, :].rearrange("p b q -> p (b q)"), m)
                elif name in ("dist", "ohT"):
                    act.wait_ge(shift_ready, b + 1)
                    a = int(name == "ohT")
                    for t in range(QT):
                        last = nc.scalar.activation(xn[:, a, t, :], xres[:, a, t, :], ACT.Identity, bias=rms[:, 2, a, t:t + 1],
                                                    scale=rstd[:, a, t:t + 1])
                    last.then_inc(skip_normed, 1)
                elif name == "xT4":
                    act.wait_ge(misc_dve, misc_reads(task))
                    nc.scalar.copy(xs[:, 0, GT * b:GT * (b + 1)], cls32[:, :, :].rearrange("p a q -> p (a q)"))
                    nc.scalar.activation(xsq[:, :, :], cls32[:, :, :], ACT.Square).then_inc(xsq_done, 1)

            for s in range(SLOTS):
                t = s - B_START
                if 0 <= t < A_SLOTS:
                    act.wait_ge(scores_exp, t + 1)
                    if t >= 4:
                        act.wait_ge(pv_done, t - 3)
                    nc.scalar.activation(probs[:, t % 4, :, :, :],
                                         psum[:, b_bank(t):b_bank(t) + 2, :].rearrange("p r (k q) -> p r k q", k=QT),
                                         ACT.Exp).then_inc(exps_done, 1)
                if t >= 4 and t % 4 == 0:
                    c = t // 4 - 1
                    act.wait_ge(pv_done, 4 * (c + 1))
                    if c == 0:
                        act.wait_ge(masks_ready, 1)
                    elif c % 2 == 0:
                        act.wait_ge(misc_full, misc_index(("ctx1", c // 2 - 1)) + 1)
                    nc.scalar.copy(pvT[:, 2 * (c % 2):2 * (c % 2) + 2, :],
                                   psum[:, BANK_PV + c % 2, :].rearrange("p (a q) -> p a q", a=2)).then_inc(pv_evicted, 1)
                for name, b in sorted(slot_tasks(s), key=lambda task: (s == 0 and task[1], task[0] != "xT")):
                    misc_task(name, b)
                if s == 2:
                    for k in range(2):
                        nc.scalar.dma_start(raw[:, k, :], experts[:, 0, 1024 * k:1024 * (k + 1)]).then_inc(in_raw[k], 16)
                if s == PAIRS:
                    unpack_selectors()
                if s % 3 == 2 and 1 <= s // 3 <= 12:
                    split_weights(s // 3 - 1)

            def hidden_high(n):
                act.wait_ge(hidden_ready, n + 1)
                if n >= 4:
                    act.wait_ge(y_done, n - 3)
                nc.scalar.copy(hs(n)[:, 0, :], h32[:, n % 2, :]).then_inc(hi_ready, 1)

            wi = 12
            for n in range(4 * UNITS):
                stage, g, u = n // (2 * UNITS), (n // UNITS) % 2, n % UNITS
                act.wait_ge(gates_done, n + 1)
                if n >= 2:
                    act.wait_ge(hidden_ready, n - 1)
                nc.scalar.activation(sg[:, n % 2, :], psum[:, n % 2, :], ACT.Silu).then_inc(silu_ready, 1)
                if wi < 24 and n % 3 == 1 and (wi < 22 or n > 2 * UNITS + DOWN_LAG):
                    split_weights(wi)
                    wi += 1
                if n >= 1:
                    hidden_high(n - 1)
                if u == DOWN_LAG - 1 and n > UNITS:
                    k = n // UNITS - 1
                    act.wait_ge(y_done, UNITS * (k + 1))
                    if k >= 1:
                        act.wait_ge(misc_full, misc_index(("yT", k - 1) if k < 3 else ("final", 0)) + 1)
                    nc.scalar.copy(yT[:, :], psum[:, 5, :]).then_inc(y_evicted, 1)
                for name, b in unit_tasks(stage, g, u):
                    misc_task(name, b)
            hidden_high(4 * UNITS - 1)
            act.wait_ge(y_done, 4 * UNITS)
            act.wait_ge(misc_full, misc_index(("final", 0)) + 1)
            nc.scalar.copy(yT[:, :], psum[:, 5, :]).then_inc(y_evicted, 1)

        @block.vector
        def _(dve):
            own = [0]

            def then(ins):
                own[0] += 1
                ins.then_inc(dve_self, 1)
                dve.wait_ge(dve_self, own[0])

            def norm_begin(at, src):
                for t in range(QT):
                    last = nc.vector.bn_stats(stats[:, at, t, :], src[:, t, :])
                then(last)
                for t in range(QT):
                    last = nc.vector.bn_aggr(mv[:, at, t, :], stats[:, at, t, :])
                last.then_inc(norm_stats, 1)

            def norm_begin_group(src):
                for t in range(4):
                    last = nc.vector.bn_stats(stats[:, t // 2, t % 2, :], src(t))
                then(last)
                for t in range(4):
                    last = nc.vector.bn_aggr(mv[:, t // 2, t % 2, :], stats[:, t // 2, t % 2, :])
                last.then_inc(norm_stats, 1)

            def norm_end(n, src):
                dve.wait_ge(rstd_ready, n + 1)
                for t in range(QT):
                    last = nc.vector.tensor_scalar(xn[:, n % 2, t, :], src[:, t, :], mv[:, n % 2, t, 0:1],
                                                   rstd[:, n % 2, t:t + 1], ALU.subtract, ALU.mult)
                last.then_inc(normed, 1)

            nc.vector.memset(vaug[:, :, :, :], 1.0)
            nc.vector.memset(c2[:, 2, :], -1.0)
            nc.vector.memset(rt_sel[:, :, :], NEG)
            nc.vector.memset(rt_rep[:, :, :], NEG)
            nc.vector.memset(d_nd[:, :, :], NEG)
            nc.vector.memset(d_rep[:, :, :], NEG).then_inc(dve_consts, 1)
            dve.wait_ge(in_x, 16)
            norm_begin(0, x_in[:, 0:QT, :])
            dve.wait_ge(in_ident, 16)
            nc.vector.tensor_copy(id16[:, :], id32[:, :])
            norm_end(0, x_in[:, 0:QT, :])
            dve.wait_ge(dve_consts, 1)

            def masks():
                dve.wait_ge(in_mask, 32)
                then(nc.vector.tensor_scalar(maskb[:, :, :, :], maskq_i[:, :, :, :], 0.0, MASKED, ALU.is_equal, ALU.mult))
                then(nc.vector.tensor_reduce(allmasked[:, :], maskb[:, 0, :, :], AX.X, ALU.max))
                then(nc.vector.tensor_scalar(allmasked[:, :], allmasked[:, :], -1.0, None, ALU.is_gt))
                for t in range(QT):
                    last = nc.vector.tensor_scalar(iddiag[:, t, :], id32[:, :], allmasked[:, t:t + 1], None, ALU.mult)
                last.then_inc(masks_ready, 1)

            def zero_masked():
                for t in range(2):
                    last = nc.vector.tensor_tensor(ropet[:, t, :], ropet[:, t, :], psum[:, BANK_NOTFULL, 0:S], ALU.mult)
                then(last)

            def late_consts():
                dve.wait_ge(in_small, 16)
                nc.vector.tensor_scalar(c2[:, 0, :], small_w("cent"), 2.0, None, ALU.mult)
                nc.vector.scalar_tensor_tensor(c2[:, 1, :], small_w("cent"), -1.0, small_w("cent"), ALU.mult, ALU.mult)
                nc.vector.memset(ones16, 1.0).then_inc(consts_ready, 1)
                dve.wait_ge(in_rows, 16)
                dve.wait_ge(in_pad, 16)
                then(nc.vector.tensor_scalar(padneg[:, :, :], pad8.rearrange("p (b k) -> p b k", b=B), NEG, None,
                                             ALU.mult))

            def misc_task(name, b):
                task = (name, b)
                if name in MISC_READER:
                    m = misc_bank(task)
                    if MISC_READER[name] != "dve" and name not in ("s1", "s1_"):
                        return
                    dve.wait_ge(misc_full, misc_index(task) + 1)
                if name in ("qproj", "kproj"):
                    t, names = (0, ("bq", "bqr")) if name == "qproj" else (1, ("bk", "bkr"))
                    nc.vector.scalar_tensor_tensor(rot[:, b % 2, t, 0, :], m[:, 0:S], small_w(names[0]),
                                                   ropet[:, 2 * t, :], ALU.add, ALU.mult)
                    nc.vector.scalar_tensor_tensor(rot[:, b % 2, t, 1, :], m[:, S:2 * S], small_w(names[1]),
                                                   ropet[:, 2 * t + 1, :], ALU.add,
                                                   ALU.mult).then_inc(misc_dve, 1)
                    dve.wait_ge(misc_dve, misc_reads(task))
                    if b >= 1:
                        dve.wait_ge(qks_ready, 2 * b - t)
                    last = nc.vector.tensor_tensor(qk[:, t, :], rot[:, b % 2, t, 0, :], rot[:, b % 2, t, 1, :], ALU.add)
                    if task == ("qproj", 0):
                        then(last)
                        dve.wait_ge(notfull_done, 1)
                        last = nc.vector.tensor_tensor(qk[:, t, :], qk[:, t, :], psum[:, BANK_NOTFULL, 0:S], ALU.mult)
                    last.then_inc(qk_ready, 1)
                elif name == "vproj":
                    if b >= 3:
                        dve.wait_ge(pv_done, PAIRS * (b - 2))
                    for k in range(QT):
                        last = nc.vector.tensor_tensor(
                            vheads[:, b % 3, k, :, 0:DK], m[:, D * k:D * (k + 1)].rearrange("p (h d) -> p h d", d=DK),
                            rowb[:, ROW_BV:ROW_BV + D].rearrange("p (h d) -> p h d", d=DK), ALU.add)
                    last.then_inc(misc_dve, 1)
                    if 2 <= b + 1 < B:
                        dve.wait_ge(in_xrest, 16)
                        norm_begin((b + 1) % 2, x_in[:, QT * (b + 1):QT * (b + 2), :])
                elif name == "maxT":
                    nc.vector.tensor_copy(maxrow[:, b % 2, :], m[0:16, 0:S]).then_inc(misc_dve, 1)
                    dve.wait_ge(misc_dve, misc_reads(task))
                elif name in ("ctx0", "ctx1"):
                    t = 0 if name == "ctx0" else 1
                    v = m.rearrange("p (h c) -> p h c", c=32)
                    then(nc.vector.reciprocal(rden[:, t, :], v[:, :, DK]))
                    nc.vector.tensor_tensor(ctxn[:, b % 2, t, :].rearrange("p (h d) -> p h d", d=DK), v[:, :, 0:DK],
                                            rden[:, t, :].unsqueeze(2).to_broadcast([P, H0, DK]),
                                            ALU.mult).then_inc(misc_dve, 1)
                elif name == "oproj":
                    then(nc.vector.tensor_tensor(x_in[:, 2 * b:2 * b + 2, :], x_in[:, 2 * b:2 * b + 2, :],
                                                 rowb[:, ROW_BO:ROW_BO + D].unsqueeze(1).to_broadcast([P, QT, D]), ALU.add))
                    nc.vector.tensor_tensor(xres[:, b % 2, :, :], x_in[:, 2 * b:2 * b + 2, :],
                                            m[:, 0:QT * D].rearrange("p (t d) -> p t d", t=QT), ALU.add).then_inc(misc_dve, 1)
                    dve.wait_ge(misc_dve, misc_reads(task))
                    norm_begin(ln_index(1, b) % 2, xres[:, b % 2, :, :])
                elif name == "norm":
                    norm_end(ln_index(1, b), xres[:, b % 2, :, :])
                elif name == "xT2":
                    cols = slice(S * b, S * (b + 1))
                    then(nc.vector.tensor_copy(cls32[:, b % 2, :], m[:, 0:S]))
                    then(nc.vector.tensor_copy(xs[:, 0, cols], m[:, 0:S]))
                    nc.vector.tensor_tensor(xs[:, 1, cols], m[:, 0:S], xs[:, 0, cols].bitcast(F32),
                                            ALU.subtract).then_inc(misc_dve, 1)
                elif name == "logits":
                    then(nc.vector.tensor_copy(rt_s[:, :, :], m[:, 0:64 * QT].rearrange("p (t e) -> p t e", t=QT)[:, :, 0:E_ALL]))
                    nc.vector.tensor_reduce(rt_neg[:, :], m[:, 0:64 * QT].rearrange("p (t e) -> p t e", t=QT)[:, :, 0:E_ALL],
                                            AX.X, ALU.max, negate=True).then_inc(misc_dve, 1)
                    dve.wait_ge(misc_dve, misc_reads(task))
                elif name == "route":
                    dve.wait_ge(act_exp_rt, b + 1)
                    then(nc.vector.reciprocal(rt_sum[:, :], rt_sum[:, :]))
                    then(nc.vector.tensor_tensor(rt_s[:, :, :], rt_e[:, :, :],
                                                 rt_sum[:, :].unsqueeze(2).to_broadcast([P, QT, E_ALL]), ALU.mult))
                    then(nc.vector.tensor_tensor(rt_sel[:, :, 0:E_ALL], rt_s[:, :, :],
                                                 rowb[:, ROW_EB:ROW_EB + E_ALL].unsqueeze(1).to_broadcast([P, QT, E_ALL]),
                                                 ALU.add))
                    for t in range(QT):
                        last = nc.vector.max(rt_top[:, t, :], rt_sel[:, t, :])
                    then(last)
                elif name == "route1":
                    then(nc.vector.tensor_copy(rt_rep[:, :, 0:TOP_K], rt_top[:, :, 0:TOP_K]))
                    for t in range(QT):
                        last = nc.vector.match_replace(rt_mr[:, t, :], rt_rep[:, t, :], rt_sel[:, t, :], TAKEN)
                    then(last)
                elif name == "route2":
                    n = ln_index(1, b)
                    if b >= 1:
                        dve.wait_ge(routed, b)
                    then(nc.vector.scalar_tensor_tensor(rt_w[:, :, :], rt_mr[:, :, 0:E_ALL], TAKEN, rt_s[:, :, :],
                                                        ALU.is_equal, ALU.mult))
                    nc.vector.tensor_scalar(rt_w[:, :, :], rt_w[:, :, :], ROUTE_SCALE, None, ALU.mult).then_inc(rw_ready, 1)
                    dve.wait_ge(rw_ready, b + 1)
                    then(nc.vector.tensor_reduce(rt_zw[:, :], rt_w[:, :, E_ROUTED:E_ALL], AX.X, ALU.add))
                    for t in range(QT):
                        nc.vector.scalar_tensor_tensor(acc[:, 2 * b + t, :], xn[:, n % 2, t, :], rt_zw[:, t:t + 1],
                                                       xres[:, b % 2, t, :], ALU.mult, ALU.add)
                elif name == "wT":
                    if b == 0:
                        dve.wait_ge(pool_consts, 1)
                    nc.vector.tensor_copy(wT[0:W_PARTS * E_ROUTED, S * b:S * (b + 1)], m[0:W_PARTS * E_ROUTED, 0:S]).then_inc(misc_dve, 1)
                elif name == "ohT":
                    nc.vector.tensor_copy(wT[0:W_PARTS * E_ROUTED, GT * b:GT * (b + 1)], m[0:W_PARTS * E_ROUTED, :]).then_inc(misc_dve, 1)
                elif name == "yT":
                    nc.vector.tensor_tensor(acc[:, 4 * b:4 * b + 4, :], acc[:, 4 * b:4 * b + 4, :],
                                            m.rearrange("p (t d) -> p t d", t=4), ALU.add).then_inc(misc_dve, 1)
                    dve.wait_ge(misc_dve, misc_reads(task))
                    norm_begin_group(lambda t: acc[:, 4 * b + t, :])
                elif name == "norm2":
                    dve.wait_ge(rstd_ready, ln_index(2, b) + 1)
                    for t in range(4):
                        last = nc.vector.tensor_scalar(xn[:, t // 2, t % 2, :], acc[:, 4 * b + t, :],
                                                       mv[:, t // 2, t % 2, 0:1], rstd[:, t // 2, t % 2:t % 2 + 1],
                                                       ALU.subtract, ALU.mult)
                    last.then_inc(normed, 1)
                    dve.wait_ge(normed, 2 * B + b + 1)
                    nc.vector.tensor_tensor(acc[:, 4 * b:4 * b + 4, :], acc[:, 4 * b:4 * b + 4, :],
                                            rowb[:, ROW_BO1:ROW_BO1 + D].unsqueeze(1).to_broadcast([P, 4, D]),
                                            ALU.add).then_inc(dve_self, 1)
                    own[0] += 1
                elif name in ("s1", "s1_"):
                    nc.vector.tensor_reduce(nm1[:, int(name == "s1_"), :], m.rearrange("p (t k) -> p t k", t=QT), AX.X,
                                            ALU.max, negate=True).then_inc(nm1_ready, 1)
                elif name == "oproj1":
                    dve.wait_ge(misc_act, misc_reads(("pv1", b)))
                    dve.wait_ge(dve_self, own[0])
                    then(nc.vector.reciprocal(sum1[:, :, :], sum1[:, :, :]))
                    for t in range(4):
                        last = nc.vector.scalar_tensor_tensor(
                            xres[:, t // 2, t % 2, :], m[:, D * t:D * (t + 1)], sum1[:, t // 2, t % 2:t % 2 + 1],
                            acc[:, 4 * b + t, :], ALU.mult, ALU.add)
                    last.then_inc(misc_dve, 1)
                    dve.wait_ge(misc_dve, misc_reads(task))
                    norm_begin_group(lambda t: xres[:, t // 2, t % 2, :])
                elif name == "norm3":
                    dve.wait_ge(rms_ready, b + 1)
                    for t in range(4):
                        last = nc.vector.tensor_scalar(x4n[:, t // 2, t % 2, :], xres[:, t // 2, t % 2, :],
                                                       mv[:, t // 2, t % 2, 0:1], rms[:, 1, t // 2, t % 2:t % 2 + 1],
                                                       ALU.subtract, ALU.mult)
                    last.then_inc(x4_ready, 1)
                elif name == "xT4":
                    x32 = cls32[:, :, :].rearrange("p a q -> p (a q)")
                    nc.vector.tensor_scalar(x32, m, small_w("scale"), None, ALU.mult).then_inc(misc_dve, 1)
                    dve.wait_ge(misc_dve, misc_reads(task))
                    dve.wait_ge(xsq_done, b + 1)
                    nc.vector.tensor_tensor(xs[:, 1, GT * b:GT * (b + 1)], x32, xs[:, 0, GT * b:GT * (b + 1)].bitcast(F32),
                                            ALU.subtract).then_inc(xlo_ready, 1)
                elif name == "dist":
                    nc.vector.memset(d_oh[:, :, :, E_ROUTED:], 0.0)
                    then(nc.vector.tensor_tensor(d_nd[:, :, 0:E1], m[:, 0:E1 * 4].rearrange("p (t e) -> p t e", t=4),
                                                 c2[:, 1, :].unsqueeze(1).to_broadcast([P, 4, E1]), ALU.add))
                    for t in range(4):
                        last = nc.vector.max(d_top[:, t, :], d_nd[:, t, :])
                    then(last)
                    then(nc.vector.tensor_copy(d_rep[:, :, 0:1], d_top[:, :, 0:1]))
                    for t in range(4):
                        last = nc.vector.match_replace(d_mr[:, t, :], d_rep[:, t, :], d_nd[:, t, :], TAKEN)
                    then(last)
                    for t in range(4):
                        last = nc.vector.tensor_scalar(
                            d_oh[:, t // 2, t % 2, 0:E_ROUTED].rearrange("p (e r) -> p e r", r=4),
                            d_mr[:, t, 0:E1].unsqueeze(2).to_broadcast([P, E1, 4]), TAKEN, None, ALU.is_equal)
                    last.then_inc(misc_dve, 1)
                elif name == "final":
                    nc.vector.tensor_tensor(acc[:, 4 * b:4 * b + 4, :], acc[:, 4 * b:4 * b + 4, :],
                                            m.rearrange("p (t d) -> p t d", t=4), ALU.add).then_inc(misc_dve, 1)
                    dve.wait_ge(misc_dve, misc_reads(task))

            for s in range(SLOTS):
                if s < A_SLOTS:
                    b, j = s // PAIRS, s % PAIRS
                    if s == 0:
                        for task in slot_tasks(0):
                            if task == ("kproj", 0):
                                dve.wait_ge(in_qkw, 16)
                                dve.wait_ge(in_ropek, 16)
                            if task == ("qproj", 0):
                                masks()
                                dve.wait_ge(in_rope, 16)
                            if task == ("kproj", 1):
                                zero_masked()
                                dve.wait_ge(in_x1, 16)
                                norm_begin(1, x_in[:, QT:2 * QT, :])
                            if task == ("xT", 1):
                                norm_end(1, x_in[:, QT:2 * QT, :])
                            if task == ("vproj", 0):
                                dve.wait_ge(in_rows, 16)
                            misc_task(*task)
                    dve.wait_ge(scores_max, s + 1)
                    bank = a_bank(s)
                    nc.vector.tensor_reduce(negmax[:, b % 2, :, :].rearrange("p t (r j) -> p r t j", r=2)[:, :, :, j],
                                            psum[:, bank:bank + 2, :].rearrange("p r (t k) -> p r t k", t=QT), AX.X,
                                            ALU.max, negate=True).then_inc(maxes_read, 1)
                if s > 0:
                    for name, b in slot_tasks(s):
                        if name == "norm0":
                            norm_end(ln_index(0, b), x_in[:, QT * b:QT * (b + 1), :])
                        misc_task(name, b)
                if s == PAIRS:
                    late_consts()
                if s == PAIRS + 2:
                    dve.wait_ge(csum_done, 1)
                    then(nc.vector.tensor_copy(c2[:, 1, :], psum[:, BANK_NOTFULL, 0:E1]))

            for n in range(4 * UNITS):
                stage, g, u = n // (2 * UNITS), (n // UNITS) % 2, n % UNITS
                dve.wait_ge(silu_ready, n + 1)
                nc.vector.tensor_tensor(sg[:, n % 2, :], sg[:, n % 2, :], psum[:, 2 + n % 2, :],
                                        ALU.mult).then_inc(up_read, 1)
                dve.wait_ge(up_read, n + 1)
                dve.wait_ge(wb_done, n + 1 if stage == 0 else 2 * UNITS + (n - 2 * UNITS) // 2 + 1)
                if n >= 2:
                    dve.wait_ge(lo_ready, n - 1)
                nc.vector.tensor_tensor(h32[:, n % 2, :], sg[:, n % 2, :], psum[:, 4, :],
                                        ALU.mult).then_inc(hidden_ready, 1)
                for name, b in unit_tasks(stage, g, u):
                    misc_task(name, b)
                if n >= LOW_ON_DVE:
                    dve.wait_ge(hi_ready, n + 1)
                    nc.vector.tensor_tensor(hs(n)[:, 1, :], h32[:, n % 2, :], hs(n)[:, 0, :].bitcast(F32),
                                            ALU.subtract).then_inc(last_lo_ready, 1)
            misc_task("final", GROUPS - 1)

        @block.tensor
        def _(pe):
            uses = misc_uses()

            def claim(task):
                k = uses.index(task)
                if k >= 2:
                    prev = uses[k - 2]
                    pe.wait_ge(misc_dve if MISC_READER[prev[0]] == "dve" else misc_act, misc_reads(prev))
                return misc_bank(task)

            def mm(o, w, r, start=True, stop=True):
                return nc.tensor.matmul(o, w, r, start=start, stop=stop, skip_group_check=True)

            def split3(o, wh, wl, xh, xl, start, stop):
                mm(o, wh, xh, start, False)
                mm(o, wh, xl, False, False)
                return mm(o, wl, xh, False, stop)

            def misc_task(name, b):
                task = (name, b)
                if name not in MISC_READER:
                    return
                m = claim(task)
                if name == "k1proj":
                    last = mm(m, small_w("wk1"), ctxT[:, GT * b:GT * (b + 1)])
                elif name == "xT":
                    k = ln_index(0, b)
                    if b == 0:
                        pe.wait_ge(in_ident, 16)
                    pe.wait_ge(normed, k + 1)
                    for t in range(QT):
                        last = nc.tensor.transpose(m[:, P * t:P * (t + 1)], xn[:, k % 2, t, :], id32[:, :])
                elif name == "qproj":
                    pe.wait_ge(misc_act, misc_reads(("xT", b)))
                    mm(m[:, 0:S], small_w("wq"), xnT[:, b % 2, :])
                    last = mm(m[:, S:2 * S], small_w("wqr"), xnT[:, b % 2, :])
                elif name == "kproj":
                    pe.wait_ge(in_ctx0 if b == 0 else in_ctx, 16)
                    pe.wait_ge(in_qkw, 16)
                    mm(m[:, 0:S], small_w("wk"), ctxT[:, S * b:S * (b + 1)])
                    last = mm(m[:, S:2 * S], small_w("wkr"), ctxT[:, S * b:S * (b + 1)])
                elif name == "vproj":
                    pe.wait_ge(in_small, 16)
                    for k in range(QT):
                        last = mm(m[:, D * k:D * (k + 1)], ctxT[:, S * b + P * k:S * b + P * (k + 1)], small_w("wv"))
                elif name == "maxT":
                    pe.wait_ge(maxes_read, PAIRS * (b + 1))
                    for t in range(QT):
                        last = nc.tensor.transpose(m[0:16, P * t:P * (t + 1)], negmax[:, b % 2, t, :], id32[:, :])
                elif name in ("ctx0", "ctx1"):
                    t = 0 if name == "ctx0" else 1
                    pe.wait_ge(pv_evicted, 2 * (b + 1))
                    for q in range(QUADS):
                        last = nc.tensor.transpose(m[:, P * q:P * (q + 1)], pvT[:, q, P * t:P * (t + 1)], id32[:, :])
                elif name == "ctxT":
                    pe.wait_ge(misc_dve, misc_reads(("ctx1", b)))
                    for t in range(QT):
                        last = nc.tensor.transpose(m[:, P * t:P * (t + 1)], ctxn[:, b % 2, t, :], id32[:, :])
                elif name == "oproj":
                    pe.wait_ge(misc_act, misc_reads(("ctxT", b)))
                    for t in range(QT):
                        last = mm(m[:, D * t:D * (t + 1)], ctxnT[:, b % 2, P * t:P * (t + 1)], small_w("wo"))
                elif name == "xT2":
                    k = ln_index(1, b)
                    pe.wait_ge(normed, k + 1)
                    for t in range(QT):
                        last = nc.tensor.transpose(m[:, P * t:P * (t + 1)], xn[:, k % 2, t, :], id32[:, :])
                elif name == "logits":
                    pe.wait_ge(misc_dve, misc_reads(("xT2", b)))
                    for t in range(QT):
                        last = mm(m[:, 64 * t:64 * t + E_ALL], cls32[:, b % 2, P * t:P * (t + 1)], small_w("cls"))
                elif name == "wT":
                    pe.wait_ge(routed, b + 1)
                    for t in range(QT):
                        last = nc.tensor.transpose(m[0:W_PARTS * E_ROUTED, P * t:P * (t + 1)], rt_ws[:, b % 2, t, :], id32[:, :])
                elif name in ("yT", "final"):
                    pe.wait_ge(y_evicted, (b + 1) if name == "yT" else GROUPS + b + 1)
                    for t in range(4):
                        last = nc.tensor.transpose(m[:, P * t:P * (t + 1)], yT[:, P * t:P * (t + 1)], id32[:, :])
                elif name == "xT3":
                    pe.wait_ge(normed, 2 * B + b + 1)
                    for t in range(4):
                        last = nc.tensor.transpose(m[:, P * t:P * (t + 1)], xn[:, t // 2, t % 2, :], id32[:, :])
                elif name == "q1":
                    pe.wait_ge(misc_act, misc_reads(("xT3", b)))
                    last = mm(m, small_w("wq1"), xT3[:, :, :].rearrange("p b q -> p (b q)"))
                elif name in ("s1", "s1_"):
                    k = int(name == "s1_")
                    pe.wait_ge(misc_act, misc_reads(("q1", b)))
                    pe.wait_ge(consts_ready, 1)
                    mm(m, ones16, padneg[0:1, 2 * b + k, :].unsqueeze(1).to_broadcast([1, QT, S]), True, False)
                    for t in range(QT):
                        last = mm(m[:, S * t:S * (t + 1)], q1T[:, k, P * t:P * (t + 1)], k1T[:, k, :], False, t == QT - 1)
                elif name in ("pT", "pT_"):
                    a = int(name == "pT_")
                    pe.wait_ge(misc_act, misc_reads(("s1_" if a else "s1", b)))
                    for k in range(QT):
                        for t in range(QT):
                            last = nc.tensor.transpose(m[:, S * k + P * t:S * k + P * (t + 1)],
                                                       sm1[:, a, t, P * k:P * (k + 1)], id32[:, :])
                elif name == "pv1":
                    pe.wait_ge(misc_act, misc_reads(("pT_", b)))
                    pe.wait_ge(in_late, 48)
                    for a in range(2):
                        for k in range(QT):
                            last = mm(m[:, S * a:S * (a + 1)], ctxk[:, QT * (2 * b + a) + k, :], pT1[:, a, k, :],
                                      k == 0, k == QT - 1)
                elif name == "oproj1":
                    pe.wait_ge(misc_act, misc_reads(("pv1", b)))
                    for t in range(4):
                        last = mm(m[:, D * t:D * (t + 1)], q1T[:, t // 2, P * (t % 2):P * (t % 2 + 1)], small_w("wo1"))
                elif name == "xT4":
                    pe.wait_ge(x4_ready, b + 1)
                    for t in range(4):
                        last = nc.tensor.transpose(m[:, P * t:P * (t + 1)], x4n[:, t // 2, t % 2, :], id32[:, :])
                elif name == "dist":
                    pe.wait_ge(xsq_done, b + 1)
                    pe.wait_ge(consts_ready, 1)
                    for t in range(4):
                        o = m[:, E1 * t:E1 * (t + 1)]
                        tok = slice(P * (t % 2), P * (t % 2 + 1))
                        mm(o, xsq[:, t // 2, tok], c2[:, 2, :], t == 0, False)
                        last = mm(o, cls32[:, t // 2, tok], c2[:, 0, :], False, True)
                elif name == "ohT":
                    pe.wait_ge(misc_dve, misc_reads(("dist", b)))
                    for t in range(4):
                        last = nc.tensor.transpose(m[0:W_PARTS * E_ROUTED, P * t:P * (t + 1)], d_oh[:, t // 2, t % 2, :], id32[:, :])
                last.then_inc(misc_full, 1)

            for task in slot_tasks(0):
                misc_task(*task)
                if task == ("qproj", 0):
                    pe.wait_ge(masks_ready, 1)
                    pe.wait_ge(pool_consts, 1)
                    for t in range(QT):
                        last = mm(psum[:, BANK_NOTFULL, P * t:P * (t + 1)], ones[:, :], iddiag[:, t, :])
                    last.then_inc(notfull_done, 1)
            for s in range(SLOTS):
                t = s - B_START
                has_a, has_b = s < A_SLOTS, 0 <= t < A_SLOTS
                a_b, a_j, b_b, b_j = s // PAIRS, s % PAIRS, t // PAIRS, t % PAIRS
                if has_a:
                    reads = s if s >= 1 and a_bank(s) == a_bank(s - 1) else s - 1
                    if reads >= 1:
                        pe.wait_ge(maxes_read, reads)
                    bank = a_bank(s)
                    for r in range(2):
                        mm(psum[:, bank + r, :], id16[:, :], maskb[:, 0, :, :].rearrange("p t k -> p (t k)"), True, False)
                    if a_j == 0:
                        pe.wait_ge(stack_in[a_b], 96)
                        if a_b < 3:
                            pe.wait_ge(ones_rows, 2 * (a_b + 1))
                    for q in range(QT):
                        for r in range(2):
                            rows_r = slice(64 * r, 64 * r + 32)
                            last = mm(psum[:, bank + r, S * q:S * (q + 1)], stacks[rows_r, 0, a_b % 3, a_j, P * q:P * (q + 1)],
                                      stacks[rows_r, 1, a_b % 3, a_j, :], False, q == QT - 1)
                    last.then_inc(scores_max, 1)
                if has_b:
                    if t == 0:
                        pe.wait_ge(maxes_read, B_START)
                    if s == A_SLOTS:
                        pe.wait_ge(maxes_read, A_SLOTS)
                    bank = b_bank(t)
                    reads = t if t >= 1 and b_bank(t - 1) == bank else t - 1
                    if reads >= 1:
                        pe.wait_ge(exps_done, reads)
                    for r in range(2):
                        mm(psum[:, bank + r, :], id16[:, :], maskb[:, 1, :, :].rearrange("p k q -> p (k q)"), True, False)
                    if b_j == 0:
                        pe.wait_ge(maxrow_in[b_b], 32)
                    for k in range(QT):
                        for r in range(2):
                            rows_r = slice(64 * r, 64 * r + 33)
                            last = mm(psum[:, bank + r, S * k:S * (k + 1)], stacks[rows_r, 1, b_b % 3, b_j, P * k:P * (k + 1)],
                                      stacks[rows_r, 0, b_b % 3, b_j, :], False, k == QT - 1)
                    last.then_inc(scores_exp, 1)
                if t >= 1:
                    p = t - 1
                    pb, quad, quarter = p // PAIRS, p // 2, p % 2
                    pe.wait_ge(exps_done, p + 1)
                    if p % PAIRS == 0:
                        pe.wait_ge(misc_dve, misc_reads(("vproj", pb)))
                    if p % 4 == 0 and p >= 8:
                        pe.wait_ge(pv_evicted, p // 4 - 1)
                    for k in range(QT):
                        for r in range(2):
                            g = 2 * quarter + r
                            h = 2 * (p % PAIRS) + r
                            last = mm(psum[32 * g:32 * (g + 1), BANK_PV + (quad // 2) % 2, S * (quad % 2):S * (quad % 2 + 1)],
                                      vaug[:, pb % 3, k, VW * h:VW * h + 32], probs[:, p % 4, r, k, :],
                                      k == 0, k == QT - 1)
                    last.then_inc(pv_done, 1)
                if s > 0:
                    for task in slot_tasks(s):
                        misc_task(*task)
                if s == PAIRS + 2:
                    pe.wait_ge(consts_ready, 1)
                    mm(psum[:, BANK_NOTFULL, 0:E1], ones[:, :], c2[:, 1, :]).then_inc(csum_done, 1)

            def down(n):
                stage, g, u = n // (2 * UNITS), (n // UNITS) % 2, n % UNITS
                w = ws0 if stage == 0 else ws1
                pe.wait_ge(hi_ready, n + 1)
                if n < LOW_ON_DVE:
                    pe.wait_ge(lo_ready, n + 1)
                else:
                    pe.wait_ge(last_lo_ready, n - LOW_ON_DVE + 1)
                if n == 2 * UNITS + UNITS // 2:
                    pe.wait_ge(wsplit, 24)
                if u == 0 and n > 0:
                    pe.wait_ge(y_evicted, n // UNITS)
                if n == 0:
                    pe.wait_ge(pv_evicted, 2 * B)
                cols = slice(P * u, P * (u + 1))
                split3(psum[:, 5, :], w[:, 2, 0, cols], w[:, 2, 1, cols], hs(n)[:, 0, :], hs(n)[:, 1, :],
                       u == 0, u == UNITS - 1).then_inc(y_done, 1)

            for n in range(4 * UNITS):
                stage, g, u = n // (2 * UNITS), (n // UNITS) % 2, n % UNITS
                w = ws0 if stage == 0 else ws1
                toks = slice(GT * g, GT * (g + 1))
                if u == 0:
                    if stage == 0:
                        pe.wait_ge(misc_dve, misc_reads(("xT2", 2 * g + 1)))
                        pe.wait_ge(wsplit, 12)
                        pe.wait_ge(act_self, 1)
                        if g == 0:
                            pe.wait_ge(maxes_read, A_SLOTS)
                            pe.wait_ge(exps_done, A_SLOTS)
                    else:
                        pe.wait_ge(xlo_ready, g + 1)
                        pe.wait_ge(wsplit, 22)
                cols = slice(P * u, P * (u + 1))
                if n >= 2:
                    pe.wait_ge(up_read, n - 1)
                split3(psum[:, n % 2, :], w[:, 0, 0, cols], w[:, 0, 1, cols], xs[:, 0, toks], xs[:, 1, toks], True, True)
                split3(psum[:, 2 + n % 2, :], w[:, 1, 0, cols], w[:, 1, 1, cols], xs[:, 0, toks], xs[:, 1, toks],
                       True, True).then_inc(gates_done, 1)
                if n >= DOWN_LAG:
                    down(n - DOWN_LAG)
                if u == 0:
                    pe.wait_ge(misc_dve, misc_reads(("wT", 2 * g + 1) if stage == 0 else ("ohT", g)))
                    if n == 0:
                        pe.wait_ge(pv_evicted, 2 * B - 1)
                if stage == 0 or u % 2 == 0:
                    if n >= 1:
                        pe.wait_ge(hidden_ready, n)
                    mm(psum[:, 4, :], seln[:, u, :], wT[:, toks]).then_inc(wb_done, 1)
                for task in unit_tasks(stage, g, u):
                    misc_task(*task)
            for n in range(4 * UNITS - DOWN_LAG, 4 * UNITS):
                down(n)
            misc_task("final", GROUPS - 1)


def rope_tables():
    inv = (1.0 / 10000.0 ** (np.arange(0, DK, 2, dtype=np.float32) / DK)).astype(np.float32)
    f = np.arange(S, dtype=np.float32)[None, :] * np.concatenate([inv, inv])[:, None]
    cos, sin = np.cos(f), np.sin(f)
    sign = np.array([-1.0] * (DK // 2) + [1.0] * (DK // 2), np.float32)[:, None]
    one = np.stack([cos / math.sqrt(DK), sign * sin / math.sqrt(DK), cos, sign * sin], axis=1)
    return np.tile(np.repeat(one, PAIRS, axis=0), (2, 1, 1)).astype(np.float32)


def selectors():
    m = np.zeros((P, UNITS, P), np.float32)
    for u in range(UNITS):
        for e in range(2):
            for i in range(W_PARTS):
                m[E_ROUTED * i + 2 * u + e, u, 64 * e:64 * (e + 1)] = 1.0
    return m.reshape(P, UNITS * P)


def kernel(x, ctx_1024, mask_1x1xSxS2_ik0, mask_BxS2_bk0, L0_xattn_w_q, L0_xattn_b_q, L0_xattn_w_k, L0_xattn_b_k,
           L0_xattn_w_v, L0_xattn_b_v, L0_xattn_w_o, L0_xattn_b_o, L0_ffn_classifier_weight,
           L0_ffn_e_score_correction_bias, L0_ffn_gate_up_proj, L0_ffn_down_proj, L1_xattn_Wq, L1_xattn_bq,
           L1_xattn_Wk, L1_xattn_bk, L1_xattn_Wo, L1_xattn_bo, L1_ffn_scale, L1_ffn_centroids, L1_ffn_up_w,
           L1_ffn_down_w):
    import concourse.bacc as bacc
    from concourse.bass_utils import run_bass_kernel_spmd as run

    a = np.asarray
    swap = np.concatenate([np.arange(1, DK, 2), np.arange(0, DK, 2)])
    heads = DK * np.arange(H0).reshape(PAIRS, 2).T
    plain = (heads[:, None, :] + np.arange(DK)[None, :, None]).reshape(-1)
    turned = (heads[:, None, :] + swap[None, :, None]).reshape(-1)
    wq, wk, bq, bk = a(L0_xattn_w_q), a(L0_xattn_w_k), a(L0_xattn_b_q), a(L0_xattn_b_k)
    small = np.concatenate([
        bq[plain][:, None], bq[turned][:, None], bk[plain][:, None], bk[turned][:, None], wq[plain].T, wq[turned].T,
        wk[plain].T, wk[turned].T, a(L0_xattn_w_v).T, a(L0_xattn_w_o).T, a(L1_xattn_Wq).T, a(L1_xattn_Wk).T,
        a(L1_xattn_Wo).T, a(L0_ffn_classifier_weight).T, a(L1_ffn_centroids).T, a(L1_xattn_bq)[:, None],
        a(L1_xattn_bk)[:, None], a(L1_ffn_scale)[:, None]], axis=1)
    rows = np.concatenate([a(L0_xattn_b_v), a(L0_xattn_b_o), a(L1_xattn_bo), a(L0_ffn_e_score_correction_bias)])[None]
    gu = a(L0_ffn_gate_up_proj)[:E_ROUTED].reshape(E_ROUTED, 2, 64, D)
    up1 = a(L1_ffn_up_w).reshape(E1, D, 2, CHUNK // E1)
    experts = np.stack([
        gu[:, 0].transpose(2, 0, 1).reshape(D, CHUNK),
        gu[:, 1].transpose(2, 0, 1).reshape(D, CHUNK),
        a(L0_ffn_down_proj).transpose(0, 2, 1).reshape(UNITS, P, D).transpose(1, 0, 2).reshape(P, CHUNK),
        up1[:, :, 1].transpose(1, 0, 2).reshape(D, CHUNK),
        up1[:, :, 0].transpose(1, 0, 2).reshape(D, CHUNK),
        a(L1_ffn_down_w).reshape(UNITS, P, D).transpose(1, 0, 2).reshape(P, CHUNK)], axis=1)
    mask = a(mask_1x1xSxS2_ik0)[0, 0]
    arrays = {
        "x": a(x).reshape(T, D), "ctx_t": a(ctx_1024).reshape(T, D).T, "ctx_tok": a(ctx_1024).reshape(T, D),
        "mask_q": mask.reshape(QT, P, S).transpose(1, 0, 2), "mask_k": mask.T.reshape(QT, P, S).transpose(1, 0, 2),
        "pad": a(mask_BxS2_bk0).reshape(1, T), "small": small, "rows": rows, "experts": experts,
        "ident": np.eye(P, dtype=np.float32), "rope": rope_tables(), "sel": selectors()}
    arrays = {k: np.ascontiguousarray(v) for k, v in arrays.items()}
    nc = bacc.Bacc("TRN2", target_bir_lowering=False, num_devices=1)
    aps = [nc.dram_tensor(k, v.shape, mybir.dt.from_np(v.dtype), kind="ExternalInput").ap() for k, v in arrays.items()]
    out = nc.dram_tensor("out", (T, D), F32, kind="ExternalOutput").ap()
    build(nc, *aps, out)
    result = run(nc, [arrays], core_ids=[0])
    return result.results[0]["out"].reshape(B, S, D)
```
